# Optimizing a Trainium2 kernel written in Bass

```python
import numpy as np
import jax
import jax.numpy as jnp

def _softmax(x, axis=-1):
    return jax.nn.softmax(x, axis=axis)

def _gelu(x):
    return jax.nn.gelu(x, approximate=True)

def _silu(x):
    return jax.nn.silu(x)

def _sigmoid(x):
    return jax.nn.sigmoid(x)

def _layernorm(x, axis=-1, eps=1e-05):
    m = jnp.mean(x, axis=axis, keepdims=True)
    v = jnp.var(x, axis=axis, keepdims=True)
    return (x - m) / jnp.sqrt(v + eps)

def _scatter_add(tgt, idx, src, axis=0):
    return tgt.at[idx].add(src)

def _segment_sum(src, seg, n):
    return jax.ops.segment_sum(src, seg, n)
kernel_name = 'mk_flamingo_gated_d4_seqx_r8_e56bec'

def setup_inputs(seed: int=0):
    np.random.seed(seed)
    _w = jnp.asarray

    def _rec_inputs():
        import jax
        import jax.numpy as jnp
        _rk = jax.random.key(seed)
        x = 7.22e-05 + 1 * jax.random.normal(jax.random.fold_in(_rk, 1), (2, 512, 128), jnp.float32)
        _lenS = 512 - jax.random.randint(jax.random.fold_in(_rk, 7), (2,), 0, max(1, 512 // 4) + 1, jnp.int32)
        _lenS2 = 77 - jax.random.randint(jax.random.fold_in(_rk, 8), (2,), 0, max(1, 77 // 4) + 1, jnp.int32)
        _ctx_1024P = jax.random.normal(jax.random.fold_in(_rk, 11), (2, 16, 128), jnp.float32)
        _ctx_1024c = jax.random.dirichlet(jax.random.fold_in(_rk, 511), 0.3 * jnp.ones((16,), jnp.float32), (2, 77))
        _ctx_1024t = jnp.einsum('bsk,bkd->bsd', _ctx_1024c, _ctx_1024P)
        _ctx_1024t = _ctx_1024t * jax.lax.rsqrt(jnp.mean(jnp.square(_ctx_1024t)) + 1e-12) * 0.953939
        ctx_1024 = 4.13588e-05 + 0.999923 * (_ctx_1024t + 0.3 * jax.random.normal(jax.random.fold_in(_rk, 611), (2, 77, 128), jnp.float32))
        _validS = jnp.arange(512)[None, :] < _lenS[:, None]
        _validS2 = jnp.arange(77)[None, :] < _lenS2[:, None]
        _causal = jnp.tril(jnp.ones((512, 512), dtype=bool))
        mask_Bx1xSxS2_if1 = jnp.where(jnp.ones((2, 1, 512, 77), dtype=bool), 1, 0).astype(jnp.int32)
        _g = jax.random.normal(jax.random.fold_in(_rk, 9001), (2, 4), jnp.float32)
        _g = jnp.sign(_g) * jnp.maximum(jnp.abs(_g), 1.0) + (_g == 0) * 1.0
        g_xattn = _g[0]
        g_ffn = _g[1]
        return (x, ctx_1024, mask_Bx1xSxS2_if1, g_xattn, g_ffn)
    x, ctx_1024, mask_Bx1xSxS2_if1, g_xattn, g_ffn = _rec_inputs()

    def _L0_xattn_setup():
        import jax, jax.numpy as jnp
        import numpy as np
        B, S, D = (4, 256, 128)
        H = 16
        DK = D // H

        def _split_heads(x):
            b, s, _ = x.shape
            return x.reshape(b, s, H, DK).transpose(0, 2, 1, 3)
        key = jax.random.key(seed)
        ks = jax.random.split(key, 8)
        scale = 1.0 / np.sqrt(D)
        return {'q': jax.random.normal(ks[0], (B, S, D), dtype=jnp.float32), 'k': jax.random.normal(ks[1], (B, S, D), dtype=jnp.float32), 'v': jax.random.normal(ks[2], (B, S, D), dtype=jnp.float32), 'mask': jnp.ones((B, 1, S, S), dtype=jnp.int32), 'Wq': jax.random.normal(ks[3], (D, D), dtype=jnp.float32) * scale, 'bq': jnp.zeros((D,), dtype=jnp.float32), 'Wo': jax.random.normal(ks[4], (D, D), dtype=jnp.float32) * scale, 'bo': jnp.zeros((D,), dtype=jnp.float32)}
    _L0_xattn_all = _L0_xattn_setup()
    _L0_xattn_in = {k: v for k, v in _L0_xattn_all.items() if k in ('Wq', 'bq', 'Wo', 'bo')}
    del _L0_xattn_all

    def _L0_ffn_setup():
        import jax, jax.numpy as jnp
        import numpy as np
        B, S, D = (4, 256, 128)
        N_EXPERTS, EXPERT_SIZE = (16, 32)
        WIDTH = N_EXPERTS * EXPERT_SIZE
        key = jax.random.key(seed)
        k_x, k_w1, k_w2, k_g = jax.random.split(key, 4)
        x = jax.random.normal(k_x, (B, S, D), dtype=jnp.float32)
        w1 = jax.random.normal(k_w1, (D, WIDTH), dtype=jnp.float32) / np.sqrt(D).astype(np.float32)
        b1 = jnp.zeros((WIDTH,), dtype=jnp.float32)
        w2 = jax.random.normal(k_w2, (WIDTH, D), dtype=jnp.float32) / np.sqrt(WIDTH).astype(np.float32)
        b2 = jnp.zeros((D,), dtype=jnp.float32)
        return {'x': x, 'w1': w1, 'b1': b1, 'w2': w2, 'b2': b2}
    _L0_ffn_all = _L0_ffn_setup()
    _L0_ffn_in = {k: v for k, v in _L0_ffn_all.items() if k in ('w1', 'b1', 'w2', 'b2')}
    del _L0_ffn_all

    def _L1_xattn_setup():
        import jax, jax.numpy as jnp
        import numpy as np
        EMB = 128
        NH = 16
        HD = EMB // NH
        key = jax.random.key(seed)
        ks = jax.random.split(key, 11)
        B, S = (4, 256)
        s_in = 1.0 / np.sqrt(EMB)
        return {'q': jax.random.normal(ks[0], (B, S, EMB), jnp.float32), 'k': jax.random.normal(ks[1], (B, S, EMB), jnp.float32), 'v': jax.random.normal(ks[2], (B, S, EMB), jnp.float32), 'Wq': jax.random.normal(ks[3], (EMB, NH * HD), jnp.float32) * s_in, 'bq': jnp.zeros((NH * HD,), jnp.float32), 'Wk': jax.random.normal(ks[4], (EMB, HD), jnp.float32) * s_in, 'bk': jnp.zeros((HD,), jnp.float32), 'Wv': jax.random.normal(ks[5], (EMB, HD), jnp.float32) * s_in, 'bv': jnp.zeros((HD,), jnp.float32), 'Wo': jax.random.normal(ks[6], (NH * HD, EMB), jnp.float32) * s_in, 'bo': jnp.zeros((EMB,), jnp.float32)}
    _L1_xattn_all = _L1_xattn_setup()
    _L1_xattn_in = {k: v for k, v in _L1_xattn_all.items() if k in ('Wq', 'bq', 'Wk', 'bk', 'Wv', 'bv', 'Wo', 'bo')}
    del _L1_xattn_all

    def _L1_ffn_setup():
        import jax, jax.numpy as jnp
        import numpy as np
        HIDDEN = 128
        MOE_FF = 64
        SHARED_FF = 352
        NUM_EXPERTS = 16
        TOP_K = 2
        NORM_TOPK = True
        key = jax.random.key(seed)
        ks = jax.random.split(key, 8)
        s = 0.02
        return {'layer_input': jax.random.normal(ks[0], (1, 256, HIDDEN), dtype=jnp.float32), 'gate_w': jax.random.normal(ks[1], (NUM_EXPERTS, HIDDEN), dtype=jnp.float32) * s, 'w_gate_up': jax.random.normal(ks[2], (NUM_EXPERTS, HIDDEN, 2 * MOE_FF), dtype=jnp.float32) * s, 'w_down': jax.random.normal(ks[3], (NUM_EXPERTS, MOE_FF, HIDDEN), dtype=jnp.float32) * s, 'shared_w_gate': jax.random.normal(ks[4], (SHARED_FF, HIDDEN), dtype=jnp.float32) * s, 'shared_w_up': jax.random.normal(ks[5], (SHARED_FF, HIDDEN), dtype=jnp.float32) * s, 'shared_w_down': jax.random.normal(ks[6], (HIDDEN, SHARED_FF), dtype=jnp.float32) * s, 'shared_gate_w': jax.random.normal(ks[7], (1, HIDDEN), dtype=jnp.float32) * s}
    _L1_ffn_all = _L1_ffn_setup()
    _L1_ffn_in = {k: v for k, v in _L1_ffn_all.items() if k in ('gate_w', 'w_gate_up', 'w_down', 'shared_w_gate', 'shared_w_up', 'shared_w_down', 'shared_gate_w')}
    del _L1_ffn_all

    def _L2_xattn_setup():
        import jax, jax.numpy as jnp
        import numpy as np
        N_HEAD = 16
        D_MODEL = 128
        D_K = D_MODEL // N_HEAD
        key = jax.random.key(seed)
        ks = jax.random.split(key, 11)
        B, S = (4, 256)
        s = 1.0 / np.sqrt(D_MODEL)
        return {'q': jax.random.normal(ks[0], (B, S, D_MODEL), jnp.float32), 'k': jax.random.normal(ks[1], (B, S, D_MODEL), jnp.float32), 'v': jax.random.normal(ks[2], (B, S, D_MODEL), jnp.float32), 'wq': jax.random.normal(ks[3], (D_MODEL, D_MODEL), jnp.float32) * s, 'bq': jax.random.normal(ks[4], (D_MODEL,), jnp.float32) * s, 'wk': jax.random.normal(ks[5], (D_MODEL, D_MODEL), jnp.float32) * s, 'bk': jax.random.normal(ks[6], (D_MODEL,), jnp.float32) * s, 'wv': jax.random.normal(ks[7], (D_MODEL, D_MODEL), jnp.float32) * s, 'bv': jax.random.normal(ks[8], (D_MODEL,), jnp.float32) * s, 'wo': jax.random.normal(ks[9], (D_MODEL, D_MODEL), jnp.float32) * s, 'bo': jax.random.normal(ks[10], (D_MODEL,), jnp.float32) * s}
    _L2_xattn_all = _L2_xattn_setup()
    _L2_xattn_in = {k: v for k, v in _L2_xattn_all.items() if k in ('wq', 'bq', 'wk', 'bk', 'wv', 'bv', 'wo', 'bo')}
    del _L2_xattn_all

    def _L2_ffn_setup():
        import jax, jax.numpy as jnp
        import numpy as np
        B, K, D = (128, 32, 128)
        E = 32
        H = int(D * 0.25)

        def _rsqrt_uniform(key, shape, d):
            bound = d ** (-0.5)
            return jax.random.uniform(key, shape, jnp.float32, -bound, bound)
        key = jax.random.key(seed)
        ks = jax.random.split(key, 7)
        return {'x': jax.random.normal(ks[0], (B, K, D), jnp.float32), 'router_w': _rsqrt_uniform(ks[1], (E, D), D), 'router_b': _rsqrt_uniform(ks[2], (E,), D), 'weights1': _rsqrt_uniform(ks[3], (E, D, H), H), 'bias1': _rsqrt_uniform(ks[4], (E, H), H), 'weights2': _rsqrt_uniform(ks[5], (E, H, D), D), 'bias2': _rsqrt_uniform(ks[6], (E, D), D)}
    _L2_ffn_all = _L2_ffn_setup()
    _L2_ffn_in = {k: v for k, v in _L2_ffn_all.items() if k in ('router_w', 'router_b', 'weights1', 'bias1', 'weights2', 'bias2')}
    del _L2_ffn_all

    def _L3_xattn_setup():
        import jax, jax.numpy as jnp
        import numpy as np
        EPS = 1e-06
        NUM_ITERS = 3

        def rmsnorm(x, w, eps=EPS):
            return x * jax.lax.rsqrt(jnp.mean(x * x, axis=-1, keepdims=True) + eps) * w

        def gru_cell(x, h, wi, wh, bi, bh):
            d = h.shape[-1]
            gi = jnp.einsum('...d,ed->...e', x, wi) + bi
            gh = jnp.einsum('...d,ed->...e', h, wh) + bh
            ir, iz, inn = (gi[..., :d], gi[..., d:2 * d], gi[..., 2 * d:])
            hr, hz, hn = (gh[..., :d], gh[..., d:2 * d], gh[..., 2 * d:])
            r = jax.nn.sigmoid(ir + hr)
            z = jax.nn.sigmoid(iz + hz)
            n = jnp.tanh(inn + r * hn)
            return (1.0 - z) * n + z * h
        key = jax.random.key(seed)
        ks = jax.random.split(key, 12)
        B, K, M, d = (8, 64, 512, 128)
        s = 0.02
        return {'slots': jax.random.normal(ks[0], (B, K, d), jnp.float32), 'P': jax.random.normal(ks[1], (B, M, d), jnp.float32), 'Wq': jax.random.normal(ks[2], (d, d), jnp.float32) * s, 'Wk': jax.random.normal(ks[3], (d, d), jnp.float32) * s, 'Wv': jax.random.normal(ks[4], (d, d), jnp.float32) * s, 'gru_wi': jax.random.normal(ks[5], (3 * d, d), jnp.float32) * s, 'gru_wh': jax.random.normal(ks[6], (3 * d, d), jnp.float32) * s, 'gru_bi': jax.random.normal(ks[7], (3 * d,), jnp.float32) * s, 'gru_bh': jax.random.normal(ks[8], (3 * d,), jnp.float32) * s, 'slot_norm_w': jnp.ones((d,), jnp.float32), 'input_norm_w': jnp.ones((d,), jnp.float32)}
    _L3_xattn_all = _L3_xattn_setup()
    _L3_xattn_in = {k: v for k, v in _L3_xattn_all.items() if k in ('Wq', 'Wk', 'Wv', 'gru_wi', 'gru_wh', 'gru_bi', 'gru_bh', 'slot_norm_w', 'input_norm_w')}
    del _L3_xattn_all

    def _L3_ffn_setup():
        import jax, jax.numpy as jnp
        import numpy as np
        INT8_MAX = 127.0

        def _absmax_scale(x, axes):
            amax = jnp.max(jnp.abs(x), axis=axes, keepdims=True)
            return jnp.maximum(amax, 1e-12) / INT8_MAX
        key = jax.random.key(seed)
        k1, k2 = jax.random.split(key)
        lhs = jax.random.normal(k1, (4, 1024, 128), dtype=jnp.float32)
        rhs = jax.random.normal(k2, (128, 128), dtype=jnp.float32)
        return {'lhs': lhs, 'rhs': rhs}
    _L3_ffn_all = _L3_ffn_setup()
    _L3_ffn_in = {k: v for k, v in _L3_ffn_all.items() if k in ('rhs',)}
    del _L3_ffn_all
    return {'x': x, 'ctx_1024': ctx_1024, 'mask_Bx1xSxS2_if1': mask_Bx1xSxS2_if1, 'g_xattn': g_xattn, 'g_ffn': g_ffn, 'L0_xattn_Wq': _L0_xattn_in['Wq'], 'L0_xattn_bq': _L0_xattn_in['bq'], 'L0_xattn_Wo': _L0_xattn_in['Wo'], 'L0_xattn_bo': _L0_xattn_in['bo'], 'L0_ffn_w1': _L0_ffn_in['w1'], 'L0_ffn_b1': _L0_ffn_in['b1'], 'L0_ffn_w2': _L0_ffn_in['w2'], 'L0_ffn_b2': _L0_ffn_in['b2'], 'L1_xattn_Wq': _L1_xattn_in['Wq'], 'L1_xattn_bq': _L1_xattn_in['bq'], 'L1_xattn_Wk': _L1_xattn_in['Wk'], 'L1_xattn_bk': _L1_xattn_in['bk'], 'L1_xattn_Wv': _L1_xattn_in['Wv'], 'L1_xattn_bv': _L1_xattn_in['bv'], 'L1_xattn_Wo': _L1_xattn_in['Wo'], 'L1_xattn_bo': _L1_xattn_in['bo'], 'L1_ffn_gate_w': _L1_ffn_in['gate_w'], 'L1_ffn_w_gate_up': _L1_ffn_in['w_gate_up'], 'L1_ffn_w_down': _L1_ffn_in['w_down'], 'L1_ffn_shared_w_gate': _L1_ffn_in['shared_w_gate'], 'L1_ffn_shared_w_up': _L1_ffn_in['shared_w_up'], 'L1_ffn_shared_w_down': _L1_ffn_in['shared_w_down'], 'L1_ffn_shared_gate_w': _L1_ffn_in['shared_gate_w'], 'L2_xattn_wq': _L2_xattn_in['wq'], 'L2_xattn_bq': _L2_xattn_in['bq'], 'L2_xattn_wk': _L2_xattn_in['wk'], 'L2_xattn_bk': _L2_xattn_in['bk'], 'L2_xattn_wv': _L2_xattn_in['wv'], 'L2_xattn_bv': _L2_xattn_in['bv'], 'L2_xattn_wo': _L2_xattn_in['wo'], 'L2_xattn_bo': _L2_xattn_in['bo'], 'L2_ffn_router_w': _L2_ffn_in['router_w'], 'L2_ffn_router_b': _L2_ffn_in['router_b'], 'L2_ffn_weights1': _L2_ffn_in['weights1'], 'L2_ffn_bias1': _L2_ffn_in['bias1'], 'L2_ffn_weights2': _L2_ffn_in['weights2'], 'L2_ffn_bias2': _L2_ffn_in['bias2'], 'L3_xattn_Wq': _L3_xattn_in['Wq'], 'L3_xattn_Wk': _L3_xattn_in['Wk'], 'L3_xattn_Wv': _L3_xattn_in['Wv'], 'L3_xattn_gru_wi': _L3_xattn_in['gru_wi'], 'L3_xattn_gru_wh': _L3_xattn_in['gru_wh'], 'L3_xattn_gru_bi': _L3_xattn_in['gru_bi'], 'L3_xattn_gru_bh': _L3_xattn_in['gru_bh'], 'L3_xattn_slot_norm_w': _L3_xattn_in['slot_norm_w'], 'L3_xattn_input_norm_w': _L3_xattn_in['input_norm_w'], 'L3_ffn_rhs': _L3_ffn_in['rhs']}

def reference(x, ctx_1024, mask_Bx1xSxS2_if1, g_xattn, g_ffn, L0_xattn_Wq, L0_xattn_bq, L0_xattn_Wo, L0_xattn_bo, L0_ffn_w1, L0_ffn_b1, L0_ffn_w2, L0_ffn_b2, L1_xattn_Wq, L1_xattn_bq, L1_xattn_Wk, L1_xattn_bk, L1_xattn_Wv, L1_xattn_bv, L1_xattn_Wo, L1_xattn_bo, L1_ffn_gate_w, L1_ffn_w_gate_up, L1_ffn_w_down, L1_ffn_shared_w_gate, L1_ffn_shared_w_up, L1_ffn_shared_w_down, L1_ffn_shared_gate_w, L2_xattn_wq, L2_xattn_bq, L2_xattn_wk, L2_xattn_bk, L2_xattn_wv, L2_xattn_bv, L2_xattn_wo, L2_xattn_bo, L2_ffn_router_w, L2_ffn_router_b, L2_ffn_weights1, L2_ffn_bias1, L2_ffn_weights2, L2_ffn_bias2, L3_xattn_Wq, L3_xattn_Wk, L3_xattn_Wv, L3_xattn_gru_wi, L3_xattn_gru_wh, L3_xattn_gru_bi, L3_xattn_gru_bh, L3_xattn_slot_norm_w, L3_xattn_input_norm_w, L3_ffn_rhs):
    import jax
    import jax.numpy as jnp

    def _L0_xattn_ref(q, k, v, mask, Wq, bq, Wo, bo):
        import jax, jax.numpy as jnp
        import numpy as np
        B, S, D = (4, 256, 128)
        H = 16
        DK = D // H

        def _split_heads(x):
            b, s, _ = x.shape
            return x.reshape(b, s, H, DK).transpose(0, 2, 1, 3)
        qh = _split_heads(q @ Wq.T + bq)
        kh = _split_heads(k @ Wq.T + bq)
        vh = _split_heads(v @ Wq.T + bq)
        scores = jnp.einsum('bhqd,bhkd->bhqk', qh, kh) / jnp.sqrt(jnp.float32(DK))
        scores = jnp.where(mask == 0, jnp.float32(-1000000000.0), scores)
        p_attn = jax.nn.softmax(scores, axis=-1)
        x = jnp.einsum('bhqk,bhkd->bhqd', p_attn, vh)
        x = x.transpose(0, 2, 1, 3).reshape(q.shape[0], -1, H * DK)
        return x @ Wo.T + bo

    def _L0_ffn_ref(x, w1, b1, w2, b2):
        import jax, jax.numpy as jnp
        import numpy as np
        B, S, D = (4, 256, 128)
        N_EXPERTS, EXPERT_SIZE = (16, 32)
        WIDTH = N_EXPERTS * EXPERT_SIZE
        h = jax.nn.relu(jnp.einsum('bsd,dw->bsw', x, w1) + b1)
        return jnp.einsum('bsw,wd->bsd', h, w2) + b2

    def _L1_xattn_ref(q, k, v, Wq, bq, Wk, bk, Wv, bv, Wo, bo):
        import jax, jax.numpy as jnp
        import numpy as np
        EMB = 128
        NH = 16
        HD = EMB // NH
        B, S, _ = q.shape
        scale = HD ** (-0.5)
        Q = (q @ Wq + bq).reshape(B, S, NH, HD).transpose(0, 2, 1, 3)
        K = k @ Wk + bk
        V = v @ Wv + bv
        scores = jnp.einsum('bhqd,bkd->bhqk', Q, K) * scale
        attn = jax.nn.softmax(scores, axis=-1)
        out = jnp.einsum('bhqk,bkd->bhqd', attn, V)
        out = out.transpose(0, 2, 1, 3).reshape(B, S, NH * HD)
        return out @ Wo + bo

    def _L1_ffn_ref(layer_input, gate_w, w_gate_up, w_down, shared_w_gate, shared_w_up, shared_w_down, shared_gate_w):
        import jax, jax.numpy as jnp
        import numpy as np
        HIDDEN = 128
        MOE_FF = 64
        SHARED_FF = 352
        NUM_EXPERTS = 16
        TOP_K = 2
        NORM_TOPK = True
        B, S, D = layer_input.shape
        x = layer_input.reshape(-1, D)
        N = x.shape[0]
        shared = jax.nn.silu(x @ shared_w_gate.T) * (x @ shared_w_up.T) @ shared_w_down.T
        shared = shared * jax.nn.sigmoid(x @ shared_gate_w.T)
        logits = x @ gate_w.T
        probs = jax.nn.softmax(logits.astype(jnp.float32), axis=-1)
        rw, sel = jax.lax.top_k(probs, TOP_K)
        if NORM_TOPK:
            rw = rw / rw.sum(axis=-1, keepdims=True)
        rw = rw.astype(x.dtype)
        combine = jnp.zeros((N, NUM_EXPERTS), x.dtype).at[jnp.arange(N)[:, None], sel].set(rw)
        gu = jnp.einsum('nd,edf->nef', x, w_gate_up)
        g, h = jnp.split(gu, 2, axis=-1)
        h = jax.nn.silu(g) * h
        expert_out = jnp.einsum('nef,efd,ne->nd', h, w_down, combine)
        out = expert_out + shared
        return out.reshape(B, S, D)

    def _L2_xattn_ref(q, k, v, wq, bq, wk, bk, wv, bv, wo, bo):
        import jax, jax.numpy as jnp
        import numpy as np
        N_HEAD = 16
        D_MODEL = 128
        D_K = D_MODEL // N_HEAD
        B, S, _ = q.shape

        def proj(x, w, b):
            y = x @ w.T + b
            return y.reshape(B, -1, N_HEAD, D_K).transpose(0, 2, 1, 3)
        qh = proj(q, wq, bq)
        kh = proj(k, wk, bk)
        vh = proj(v, wv, bv)
        scale = jnp.sqrt(jnp.float32(D_K))
        scores = jnp.einsum('bhsd,bhtd->bhst', qh, kh) / scale
        attn = jax.nn.softmax(scores, axis=-1)
        out = jnp.einsum('bhst,bhtd->bhsd', attn, vh)
        out = out.transpose(0, 2, 1, 3).reshape(B, S, D_MODEL)
        return out @ wo.T + bo

    def _L2_ffn_ref(x, router_w, router_b, weights1, bias1, weights2, bias2):
        import jax, jax.numpy as jnp
        import numpy as np
        B, K, D = (128, 32, 128)
        E = 32
        H = int(D * 0.25)

        def _rsqrt_uniform(key, shape, d):
            bound = d ** (-0.5)
            return jax.random.uniform(key, shape, jnp.float32, -bound, bound)
        b, k, d = x.shape
        x_flat = x.reshape(-1, d)
        n = x_flat.shape[0]
        logits = x_flat @ router_w.T + router_b
        routed_idx = jnp.argmax(logits, axis=-1)

        def expert_mlp(w1, b1, w2, b2):
            h = jax.nn.relu(x_flat @ w1 + b1)
            return jax.nn.relu(h @ w2 + b2)
        y_all = jax.vmap(expert_mlp)(weights1, bias1, weights2, bias2)
        out_flat = y_all[routed_idx, jnp.arange(n)]
        return out_flat.reshape(b, k, d)

    def _L3_xattn_ref(slots, P, Wq, Wk, Wv, gru_wi, gru_wh, gru_bi, gru_bh, slot_norm_w, input_norm_w):
        import jax, jax.numpy as jnp
        import numpy as np
        EPS = 1e-06
        NUM_ITERS = 3

        def rmsnorm(x, w, eps=EPS):
            return x * jax.lax.rsqrt(jnp.mean(x * x, axis=-1, keepdims=True) + eps) * w

        def gru_cell(x, h, wi, wh, bi, bh):
            d = h.shape[-1]
            gi = jnp.einsum('...d,ed->...e', x, wi) + bi
            gh = jnp.einsum('...d,ed->...e', h, wh) + bh
            ir, iz, inn = (gi[..., :d], gi[..., d:2 * d], gi[..., 2 * d:])
            hr, hz, hn = (gh[..., :d], gh[..., d:2 * d], gh[..., 2 * d:])
            r = jax.nn.sigmoid(ir + hr)
            z = jax.nn.sigmoid(iz + hz)
            n = jnp.tanh(inn + r * hn)
            return (1.0 - z) * n + z * h
        d = slots.shape[-1]
        scale = d ** (-0.5)
        Pn = rmsnorm(P, input_norm_w)
        k_proj = jnp.einsum('bmd,ed->bme', Pn, Wk)
        v_proj = jnp.einsum('bmd,ed->bme', Pn, Wv)
        for _ in range(NUM_ITERS):
            sn = rmsnorm(slots, slot_norm_w)
            q = jnp.einsum('bkd,ed->bke', sn, Wq)
            scores = jnp.einsum('bkd,bmd->bkm', q, k_proj) * scale
            attn = jax.nn.softmax(scores, axis=-2)
            attn = attn / (jnp.sum(attn, axis=-1, keepdims=True) + EPS)
            updates = jnp.einsum('bkm,bmd->bkd', attn, v_proj)
            slots = gru_cell(updates, slots, gru_wi, gru_wh, gru_bi, gru_bh)
        return slots

    def _L3_ffn_ref(lhs, rhs):
        import jax, jax.numpy as jnp
        import numpy as np
        INT8_MAX = 127.0

        def _absmax_scale(x, axes):
            amax = jnp.max(jnp.abs(x), axis=axes, keepdims=True)
            return jnp.maximum(amax, 1e-12) / INT8_MAX
        lhs_scale = _absmax_scale(lhs, (2,))
        rhs_scale = _absmax_scale(rhs, (0,))
        q_lhs = jnp.clip(jnp.round(lhs / lhs_scale), -INT8_MAX, INT8_MAX).astype(jnp.int8)
        q_rhs = jnp.clip(jnp.round(rhs / rhs_scale), -INT8_MAX, INT8_MAX).astype(jnp.int8)
        acc = jax.lax.dot_general(q_lhs, q_rhs, (((2,), (0,)), ((), ())), preferred_element_type=jnp.int32)
        return acc.astype(jnp.float32) * lhs_scale * rhs_scale
    x = x + jnp.tanh(g_xattn[0]) * _L0_xattn_ref(_layernorm(x, axis=-1), ctx_1024, ctx_1024, mask_Bx1xSxS2_if1, L0_xattn_Wq, L0_xattn_bq, L0_xattn_Wo, L0_xattn_bo)
    x = x + jnp.tanh(g_ffn[0]) * _L0_ffn_ref(_layernorm(x, axis=-1), L0_ffn_w1, L0_ffn_b1, L0_ffn_w2, L0_ffn_b2)
    x = x + jnp.tanh(g_xattn[1]) * _L1_xattn_ref(_layernorm(x, axis=-1), ctx_1024, ctx_1024, L1_xattn_Wq, L1_xattn_bq, L1_xattn_Wk, L1_xattn_bk, L1_xattn_Wv, L1_xattn_bv, L1_xattn_Wo, L1_xattn_bo)
    x = x + jnp.tanh(g_ffn[1]) * _L1_ffn_ref(_layernorm(x, axis=-1), L1_ffn_gate_w, L1_ffn_w_gate_up, L1_ffn_w_down, L1_ffn_shared_w_gate, L1_ffn_shared_w_up, L1_ffn_shared_w_down, L1_ffn_shared_gate_w)
    x = x + jnp.tanh(g_xattn[2]) * _L2_xattn_ref(_layernorm(x, axis=-1), ctx_1024, ctx_1024, L2_xattn_wq, L2_xattn_bq, L2_xattn_wk, L2_xattn_bk, L2_xattn_wv, L2_xattn_bv, L2_xattn_wo, L2_xattn_bo)
    x = x + jnp.tanh(g_ffn[2]) * _L2_ffn_ref(_layernorm(x, axis=-1), L2_ffn_router_w, L2_ffn_router_b, L2_ffn_weights1, L2_ffn_bias1, L2_ffn_weights2, L2_ffn_bias2)
    x = x + jnp.tanh(g_xattn[3]) * _L3_xattn_ref(_layernorm(x, axis=-1), ctx_1024, L3_xattn_Wq, L3_xattn_Wk, L3_xattn_Wv, L3_xattn_gru_wi, L3_xattn_gru_wh, L3_xattn_gru_bi, L3_xattn_gru_bh, L3_xattn_slot_norm_w, L3_xattn_input_norm_w)
    x = x + jnp.tanh(g_ffn[3]) * _L3_ffn_ref(_layernorm(x, axis=-1), L3_ffn_rhs)
    return x

_drawn_inputs = setup_inputs


def setup_inputs(seed=0):
    import zlib

    import numpy as np

    out = dict(_drawn_inputs(seed))
    spreads = {'L0_xattn_bq': (0.0, 0.1),
     'L0_xattn_bo': (0.0, 0.1),
     'L0_ffn_b1': (0.0, 0.1),
     'L0_ffn_b2': (0.0, 0.1),
     'L1_xattn_bq': (0.0, 0.291),
     'L1_xattn_bk': (0.0, 2.0),
     'L1_xattn_bv': (0.0, 0.1),
     'L1_xattn_bo': (0.0, 0.1),
     'L3_xattn_slot_norm_w': (1.0, 0.6),
     'L3_xattn_input_norm_w': (1.0, 0.6)}
    factors = {'L1_ffn_gate_w': 8.0,
     'L1_ffn_w_gate_up': 8.0,
     'L1_ffn_w_down': 8.0,
     'L1_ffn_shared_w_gate': 6.985,
     'L1_ffn_shared_w_up': 6.938,
     'L1_ffn_shared_w_down': 7.669,
     'L1_ffn_shared_gate_w': 8.0,
     'L2_xattn_bq': 4.076,
     'L2_xattn_bk': 64.0,
     'L2_ffn_bias1': 17.812,
     'L2_ffn_bias2': 3.15,
     'L3_xattn_Wq': 8.0,
     'L3_xattn_Wk': 8.0,
     'L3_xattn_Wv': 3.896,
     'L3_xattn_gru_wi': 3.965,
     'L3_xattn_gru_bi': 14.499,
     'L3_xattn_gru_bh': 20.277,
     'L2_ffn_router_b': 3.471}
    for name, (base, spread) in spreads.items():
        noise = np.random.default_rng([zlib.crc32(name.encode()), seed]).standard_normal(out[name].shape)
        drawn = base * np.exp(spread * noise) if base else spread * noise
        out[name] = jnp.asarray(drawn.astype(out[name].dtype))
    for name, factor in factors.items():
        out[name] = (out[name] * factor).astype(out[name].dtype)
    return out
```

```python
from contextlib import ExitStack

import numpy as np

import concourse.bass as bass
from concourse import mybir

ALU = mybir.AluOpType
ACT = mybir.ActivationFunctionType
AX = mybir.AxisListType
F32 = mybir.dt.float32
F32R = mybir.dt.float32r
BF16 = mybir.dt.bfloat16
I32 = mybir.dt.int32

P = 128
B = 2
S = 512
D = 128
T = S // P
CTX = 77
H = 16
DH = D // H
HK = H * CTX
NC = -(-HK // P)
WIN = 3
HEAD_GROUPS = [(0, 6), (6, 12), (12, 16)]
FIRST_HEAD = [min(P * c // CTX, H - WIN) for c in range(NC)]
ROWS = [min(P, HK - P * c) for c in range(NC)]
VC = DH + 1
BANKS = 8
E1, F1, SH = 16, 64, 352
E2, F2 = 32, 32
C1 = E1 * F1 // P
SHC = [(i, min(P, SH - i)) for i in range(0, SH, P)]
C2 = E2 * F2 // P
W0 = 512
C0 = W0 // P
ITERS = 3
MASKED = -(2.0 ** 100)
ROUND = 1.5 * 2.0 ** 23
LN_EPS, RMS_EPS = 1e-5, 1e-6

COLS = [("bq0", 1), ("bq1", 1), ("bk1", 1), ("bq2", 1), ("bk2", 1), ("b1", C0), ("bias1", C2),
        ("bi", 3), ("bh", 3), ("w_slot", 1), ("w_in", 1)]
ROWSPACK = [("g", 8), ("bv0", D), ("bv1", D), ("bv2", D), ("bo0", D), ("b2", D), ("bo1", D), ("bo2", D),
            ("router_b", E2)]
CONSTS = [("ident", P), ("head_mask", H), ("chunk_mask", NC * WIN), ("rev16", E1), ("rev32", E2)]
CONSTS_ONCE = [("neg_ind", HK), ("key_of", NC * P), ("sel1", C1 * P), ("sel2", C2 * P)]
PACKS = {
    "attn0": [("wq", D), ("wo", D)],
    "ffn0": [("w1", W0), ("w2", C0 * D)],
    "attn1": [("wk", D), ("wv", D), ("wq", D), ("wo", D)],
    "ffn1": [("gates", E1 + 1), ("w_g", C1 * P), ("w_u", C1 * P), ("w_down", C1 * D), ("s_g", SH), ("s_u", SH),
             ("s_down", len(SHC) * D)],
    "attn2": [("wk", D), ("wv", D), ("wq", D), ("wo", D)],
    "ffn2": [("router", E2), ("w1", C2 * P), ("w2", C2 * D), ("bias2", D)],
    "attn3": [("wk", D), ("wv", D), ("wq", D), ("wi", 3 * D), ("wh", 3 * D), ("rhs_t", D)],
}


def columns(pack):
    at, out = 0, {}
    for name, n in pack:
        out[name] = (at, at + n)
        at += n
    return out, at


def psum_plan():
    plan = []

    def unit(reader, *name):
        plan.append((name, reader))

    for layer in range(3):
        unit("act", "k", layer)
        unit("dve", "v", layer)
        for b in range(B):
            unit("dve", "vrows", layer, b)
    for b in range(B):
        unit("act", "mask_t", b)
    unit("act", "pn_t")
    unit("act", "kproj")
    unit("dve", "kq")
    unit("act", "vproj")
    for b in range(B):
        unit("act", "vw", b)
    unit("dve", "rq_t")
    unit("act", "rscale")

    def turned(stage):
        for b in range(B):
            unit("act", "xn_t", stage, b)

    def attention(stage, layer):
        turned(stage)
        for b in range(B):
            unit("act", "q", layer, b)
        for b in range(B):
            for t in range(T):
                for g in range(len(HEAD_GROUPS)):
                    unit("dve", "max", layer, b, t, g)
        for b in range(B):
            unit("act", "max_t", layer, b)
            for c in range(NC):
                unit("act", "p", layer, b, c)
        for b in range(B):
            for u in range(T // 2):
                unit("dve", "pv", layer, b, u)
        for b in range(B):
            unit("act", "o_t", layer, b)
        for b in range(B):
            unit("dve", "out", stage, b)

    attention(0, 0)
    turned(1)
    for b in range(B):
        for m in range(C0):
            unit("act" if m % 2 else "dve", "h0", b, m)
    for b in range(B):
        unit("dve", "out", 1, b)
    attention(2, 1)
    turned(3)
    for b in range(B):
        unit("dve", "gates1", b)
    for b in range(B):
        for i in range(len(SHC)):
            unit("act", "s_g", b, i)
            unit("dve", "s_u", b, i)
        unit("act", "comb_t", b)
        for c in range(C1):
            unit("act", "e_g", b, c)
            unit("dve", "e_u", b, c)
            unit("dve", "e_w", b, c)
    for b in range(B):
        unit("dve", "s_out", b)
        unit("dve", "out", 3, b)
    attention(4, 2)
    turned(5)
    for b in range(B):
        unit("dve", "router", b)
    for b in range(B):
        unit("act", "hot_t", b)
    for b in range(B):
        for c in range(C2):
            unit("act" if c % 2 else "dve", "h2", b, c)
    for b in range(B):
        unit("act", "out", 5, b)
    turned(6)
    for it in range(ITERS):
        for b in range(B):
            unit("dve", "ss", it, b)
        for b in range(B):
            unit("dve", "s", it, b)
        for b in range(B):
            unit("act", "rstd_b", it, b)
        for b in range(B):
            unit("dve", "asum", it, b)
        for b in range(B):
            unit("dve", "ra_b", it, b)
        for b in range(B):
            unit("act", "r", it, b)
            unit("act", "hn", it, b)
            unit("act", "z", it, b)
            unit("dve", "n", it, b)
    for b in range(B):
        unit("dve", "out", 6, b)
    turned_last = [("q_t", b) for b in range(B)]
    for name in turned_last:
        unit("dve", *name)
    for b in range(B):
        unit("dve", "out", 7, b)
    return plan


class Banks:

    def __init__(self, psum, filled, drained):
        self.psum, self.filled, self.drained = psum, filled, drained
        self.plan = psum_plan()
        self.index = {name: i for i, (name, _) in enumerate(self.plan)}
        assert len(self.index) == len(self.plan)
        seen = {"act": 0, "dve": 0}
        self.rank = []
        for _, reader in self.plan:
            seen[reader] += 1
            self.rank.append(seen[reader])

    def bank(self, *name):
        return self.psum[:, self.index[name] % BANKS, :]

    def full(self, *name):
        return self.filled, self.index[name] + 1

    def emptied(self, *name):
        i = self.index[name]
        return self.drained[self.plan[i][1]], self.rank[i]

    def reused(self, *name):
        return self.index[name] >= BANKS

    def free(self, *name):
        before = self.index[name] - BANKS
        return self.drained[self.plan[before][1]], self.rank[before]


def program(nc, a, out, stages=8):
    with ExitStack() as ctx:
        def sb(name, shape, dt=F32):
            return ctx.enter_context(nc.sbuf_tensor(name, shape, dt))

        def sem(name):
            return ctx.enter_context(nc.semaphore(name))

        x = sb("x", [P, B, T, D])
        cols_at, cols_n = columns(COLS)
        rows_at, rows_n = columns(ROWSPACK)
        const_at, const_n = columns(CONSTS)
        once_at, once_n = columns(CONSTS_ONCE)
        cols = sb("cols", [P, cols_n])
        rows = sb("rows", [P, rows_n])
        consts = sb("consts", [P, const_n])
        ctx_t = sb("ctx_t", [P, B * CTX])
        ctx_rows = sb("ctx_rows", [CTX, B, D])
        mask_i = sb("mask_i", [P, B, T, CTX], I32)
        packs = {k: sb("w_" + k, [P, columns(v)[1]]) for k, v in PACKS.items() if k != "ffn2"}
        packs["ffn2"] = packs["ffn1"][:, 0:columns(PACKS["ffn2"])[1]]

        def w(pack, name):
            lo, hi = columns(PACKS[pack])[0][name]
            return packs[pack][:, lo:hi]

        def col(name, i=0):
            lo = cols_at[name][0] + i
            return cols[:, lo:lo + 1]

        def row(name):
            lo, hi = rows_at[name]
            return rows[:, lo:hi]

        def const(name):
            lo, hi = const_at[name]
            return consts[:, lo:hi]

        def once(name):
            lo, hi = once_at[name]
            return wide[:, 0, :, :].rearrange("p c s -> p (c s)")[:, lo:hi]

        ident = const("ident")

        ident16 = sb("ident16", [P, P], BF16)
        ones = sb("ones", [P, 2])
        neg_ind = sb("neg_ind", [P, HK], F32R)
        key_of = sb("key_of", [CTX, NC * P], BF16)
        sel1 = sb("sel1", [P, C1 * P], F32R)
        sel2 = sb("sel2", [P, C2 * P], BF16)
        mask_b16 = sb("mask_b16", [P, B, T, CTX], BF16)
        mask_t = sb("mask_t", [CTX, B, S], BF16)
        gain = sb("gain", [P, 8])
        gbias = sb("gbias", [P, 4, D])
        k_t = sb("k_t", [P, 3, B * CTX])
        k_hi = sb("k_hi", [P, 3, B * CTX], F32R)
        k_lo = sb("k_lo", [P, 3, B * CTX], F32R)
        kbd_hi = sb("kbd_hi", [P, 2, B, HK], F32R)
        kbd_lo = sb("kbd_lo", [P, 2, B, HK], F32R)
        v_rows = sb("v_rows", [CTX, 3, B, D])
        v_win = sb("v_win", [P, 3, B, NC * WIN, VC])
        pn = sb("pn", [CTX, B, D])
        p_ss = sb("p_ss", [CTX, B])
        p_small = sb("p_small", [CTX, 4, B])
        pn_t = sb("pn_t", [P, B * CTX])
        kproj = sb("kproj", [P, B * CTX])
        vproj = sb("vproj", [P, B * CTX])
        kq = sb("kq", [P, B * CTX])
        vw = sb("vw", [CTX, B, 3 * D])
        half_bias = sb("half_bias", [P, 3])
        rscale = sb("rscale", [P, 4])
        rq = sb("rq", [P, D])
        rhs_q = sb("rhs_q", [P, D], BF16)
        rscale_b = sb("rscale_b", [P, D])

        stats = sb("stats", [P, B, T, 6])
        mv = sb("mv", [P, B, T, 2])
        nw = sb("nw", [P, B, 4, T])
        xn = sb("xn", [P, B, T, D])
        xn_t = sb("xn_t", [P, B, S])
        q_t = sb("q_t", [P, B, S])
        q_hi = sb("q_hi", [P, B, S], F32R)
        q_lo = sb("q_lo", [P, B, S], F32R)
        mx = sb("mx", [P, B, T, H])
        mx_parts = sb("mx_parts", [P, B, T, 2 * H], F32R)
        max_t = sb("max_t", [P, B, S], F32R)
        wide = sb("wide", [P, B, C1 + len(SHC), S])
        rsum = sb("rsum", [P, B, T, H])
        o = sb("o", [P, B, T, D])
        lg = sb("lg", [P, B, T, E2])
        route = sb("route", [P, B, 5, T, E2])
        route_s = sb("route_s", [P, B, 8, T])
        comb = sb("comb", [P, B, T, 2 * E1], F32R)
        nothot_t = sb("nothot_t", [P, B, S], BF16)
        o_t, slots_t, act_s = q_t, q_t, q_t
        y = o
        act_u = o[:, :, :, :].rearrange("p b t d -> p b (t d)")
        lhs_q = nothot_t
        hot_t = xn[0:E2, :, :, :].rearrange("p b t d -> p b (t d)")
        mask_b = o[:, :, :, 0:CTX]
        wide3 = wide[:, :, 0:11, :]
        sq, rb, sc, ex, at, an, tr, hnb, tz, tt, dd = [wide3[:, :, i, :] for i in range(11)]
        nn = xn_t
        nmax = sb("nmax", [CTX, B, 4])

        psum = ctx.enter_context(nc.psum_tensor("psum", [P, BANKS, 512], F32))

        loaded = {k: sem("loaded_" + k) for k in
                  ["x", "cols", "rows", "consts", "consts_once", "ctx_t", "ctx_rows", "mask"] + list(PACKS)}
        filled = sem("bank_filled")
        drained = {"act": sem("bank_drained_by_act"), "dve": sem("bank_drained_by_dve")}
        consts_made = sem("consts_made")
        dve_step = sem("dve_step")
        pool_step = sem("pool_step")
        act_step = sem("act_step")
        gain_ready = sem("gain_ready")
        gbias_ready = sem("gbias_ready")
        k_parts = sem("k_parts")
        kbd_ready = sem("kbd_ready")
        mask_b_ready = sem("mask_b_ready")
        p_ss_ready = sem("p_ss_ready")
        pn_ready = sem("pn_ready")
        rq_ready = sem("rq_ready")

        def per_half(name):
            return [sem(f"{name}_{b}") for b in range(B)]

        xn_ready = per_half("xn_ready")
        bias_added = per_half("bias_added")
        q_parts = per_half("q_parts")
        max_ready = per_half("max_ready")
        gap_ready = per_half("gap_ready")
        second_ready = per_half("second_ready")
        comb_ready = per_half("comb_ready")
        hot_ready = per_half("hot_ready")
        nothot_ready = per_half("nothot_ready")
        relu_ready = per_half("relu_ready")
        sq_ready = per_half("sq_ready")
        rstd_ready = per_half("rstd_ready")
        nmax_ready = per_half("nmax_ready")
        ex_ready = per_half("ex_ready")
        at_ready = per_half("at_ready")
        ra_ready = per_half("ra_ready")
        n_ready = per_half("n_ready")
        slots_ready = per_half("slots_ready")
        x_final = per_half("x_final")
        stored = sem("stored")

        banks = Banks(psum, filled, drained)
        BIASED = {0: 0, 1: 1, 2: 2, 4: 3}
        GAIN_OF = [0, 4, 1, 5, 2, 6, 3, 7]

        block = ctx.enter_context(nc.Block())

        @block.sync
        def _(sp):
            sp.dma_start(x[:, :, :, :], a["x"].rearrange("b (t p) d -> p b t d", p=P)).then_inc(loaded["x"], 16)
            sp.dma_start(cols[:, :], a["cols"]).then_inc(loaded["cols"], 16)
            sp.dma_start(ctx_t[:, :], a["ctx_t"]).then_inc(loaded["ctx_t"], 16)
            sp.dma_start(rows[:, :], a["rows"].broadcast_to([P, rows_n])).then_inc(loaded["rows"], 16)
            sp.dma_start(packs["attn0"][:, :], a["attn0"]).then_inc(loaded["attn0"], 16)
            sp.dma_start(consts[:, :], a["consts"]).then_inc(loaded["consts"], 16)
            sp.dma_start(wide[:, 0, :, :].rearrange("p c s -> p (c s)")[:, 0:once_n], a["consts_once"])\
              .then_inc(loaded["consts_once"], 16)
            sp.dma_start(mask_i[:, :, :, :], a["mask"].rearrange("b o (t p) k -> p b (o t) k", p=P))\
              .then_inc(loaded["mask"], 16)
            sp.dma_start(packs["attn1"][:, :], a["attn1"]).then_inc(loaded["attn1"], 16)
            sp.dma_start(packs["attn2"][:, :], a["attn2"]).then_inc(loaded["attn2"], 16)
            sp.dma_start(ctx_rows[:, :, :], a["ctx_rows"].rearrange("b k d -> k b d")).then_inc(loaded["ctx_rows"], 16)
            sp.dma_start(packs["attn3"][:, :], a["attn3"]).then_inc(loaded["attn3"], 16)
            sp.dma_start(packs["ffn0"][:, :], a["ffn0"]).then_inc(loaded["ffn0"], 16)
            sp.dma_start(packs["ffn1"][:, :], a["ffn1"]).then_inc(loaded["ffn1"], 16)
            sp.wait_ge(*banks.full("out", 3, B - 1))
            sp.dma_start(packs["ffn2"][:, :], a["ffn2"]).then_inc(loaded["ffn2"], 16)
            for b in range(B):
                sp.wait_ge(x_final[b], 1)
                sp.dma_start(out[b].rearrange("(t p) d -> p t d", p=P), x[:, b, :, :]).then_inc(stored, 16)
            sp.wait_ge(stored, 16 * B)

        @block.gpsimd
        def _(pool):
            nc.gpsimd.memset(ones[:, 0:1], 1.0)
            nc.gpsimd.memset(ones[:, 1:2], 1.0 / D)
            nc.gpsimd.memset(max_t[:, :, :].bitcast(F32), 0.0)
            nc.gpsimd.memset(nothot_t[:, :, :], 0.0)
            pool.wait_ge(loaded["consts"], 16)
            pool.wait_ge(loaded["consts_once"], 16)
            nc.gpsimd.tensor_copy(ident16[:, :], ident)
            nc.gpsimd.tensor_copy(neg_ind[:, :], once("neg_ind"))
            nc.gpsimd.tensor_copy(key_of[:, :], once("key_of")[0:CTX, :])
            nc.gpsimd.tensor_copy(sel1[:, :], once("sel1"))
            nc.gpsimd.tensor_copy(sel2[:, :], once("sel2")).then_inc(consts_made, 1)

            def spread_keys(layer):
                pool.wait_ge(k_parts, layer + 1)
                if layer == 2:
                    pool.wait_ge(*banks.full("p", 0, B - 1, NC - 1))
                for b in range(B):
                    for part, dst in ((k_hi, kbd_hi), (k_lo, kbd_lo)):
                        keys = part[:, layer, b * CTX:(b + 1) * CTX].bitcast(F32)
                        nc.gpsimd.tensor_tensor(
                            dst[:, layer % 2, b, :].rearrange("p (h k) -> p h k", h=H),
                            keys.unsqueeze(1).broadcast_to([P, H, CTX]),
                            const("head_mask").unsqueeze(2).broadcast_to([P, H, CTX]), ALU.mult).then_inc(kbd_ready, 1)

            spread_keys(0)
            spread_keys(1)
            for stage in range(stages):
                if stage in BIASED:
                    for b in range(B):
                        pool.wait_ge(xn_ready[b], stage + 1)
                        pool.wait_ge(gbias_ready, 1)
                        nc.gpsimd.tensor_tensor(
                            x[:, b, :, :], x[:, b, :, :],
                            gbias[:, BIASED[stage]:BIASED[stage] + 1, :].broadcast_to([P, T, D]),
                            ALU.add).then_inc(bias_added[b], 1)
                if stage == 0:
                    spread_keys(2)

        @block.tensor
        def _(pe):
            def start_unit(*name):
                if banks.reused(*name):
                    pe.wait_ge(*banks.free(*name))
                return banks.bank(*name)

            def mm(out_, lhs, rhs, start=True, stop=True, **kw):
                return nc.tensor.matmul(out_, lhs, rhs, start=start, stop=stop, **kw)

            pe.wait_ge(loaded["ctx_t"], 16)
            for layer in range(3):
                pack = f"attn{layer}"
                pe.wait_ge(loaded[pack], 16)
                wk = w(pack, "wq" if layer == 0 else "wk")
                wv = w(pack, "wq" if layer == 0 else "wv")
                bk = start_unit("k", layer)
                mm(bk[:, 0:B * CTX], wk, ctx_t[:, :]).then_inc(filled, 1)
                bk = start_unit("v", layer)
                for b in range(B):
                    last = mm(bk[0:CTX, b * D:(b + 1) * D], ctx_t[:, b * CTX:(b + 1) * CTX], wv)
                last.then_inc(filled, 1)
                if layer == 0:
                    pe.wait_ge(loaded["consts"], 16)
                    pe.wait_ge(loaded["consts_once"], 16)
                for b in range(B):
                    bk = start_unit("vrows", layer, b)
                    pe.wait_ge(*banks.emptied("v", layer))
                    for c in range(NC):
                        h0 = FIRST_HEAD[c]
                        last = mm(bk[:, c * WIN * DH:(c + 1) * WIN * DH],
                                  once("key_of")[0:CTX, c * P:(c + 1) * P],
                                  v_rows[:, layer, b, h0 * DH:(h0 + WIN) * DH])
                    last.then_inc(filled, 1)
            for b in range(B):
                bk = start_unit("mask_t", b)
                pe.wait_ge(mask_b_ready, b + 1)
                for t in range(T):
                    last = nc.tensor.transpose(bk[0:CTX, t * P:(t + 1) * P], mask_b[:, b, t, :], ident)
                last.then_inc(filled, 1)
            pe.wait_ge(loaded["attn3"], 16)
            bk = start_unit("pn_t")
            pe.wait_ge(pn_ready, 1)
            for b in range(B):
                last = nc.tensor.transpose(bk[:, b * CTX:(b + 1) * CTX], pn[:, b, :], ident[0:CTX, 0:CTX])
            last.then_inc(filled, 1)
            bk = start_unit("kproj")
            pe.wait_ge(*banks.emptied("pn_t"))
            mm(bk[:, 0:B * CTX], w("attn3", "wk"), pn_t[:, :]).then_inc(filled, 1)
            bk = start_unit("kq")
            pe.wait_ge(*banks.emptied("kproj"))
            mm(bk[:, 0:B * CTX], w("attn3", "wq"), kproj[:, :]).then_inc(filled, 1)
            bk = start_unit("vproj")
            mm(bk[:, 0:B * CTX], w("attn3", "wv"), pn_t[:, :]).then_inc(filled, 1)
            for b in range(B):
                bk = start_unit("vw", b)
                pe.wait_ge(*banks.emptied("vproj"))
                mm(bk[0:CTX, 0:3 * D], vproj[:, b * CTX:(b + 1) * CTX], w("attn3", "wi")).then_inc(filled, 1)
            bk = start_unit("rq_t")
            pe.wait_ge(rq_ready, 1)
            nc.tensor.transpose(bk[:, 0:D], rq[:, :], ident).then_inc(filled, 1)
            bk = start_unit("rscale")
            mm(bk[:, 0:D], rscale[:, 1:2].broadcast_to([P, P]), ident).then_inc(filled, 1)

            def turn(stage):
                for b in range(B):
                    bk = start_unit("xn_t", stage, b)
                    pe.wait_ge(xn_ready[b], stage + 1)
                    for t in range(T):
                        last = nc.tensor.transpose(bk[:, t * P:(t + 1) * P], xn[:, b, t, :], ident)
                    last.then_inc(filled, 1)

            def attention(stage, layer):
                turn(stage)
                pack = f"attn{layer}"
                for b in range(B):
                    bk = start_unit("q", layer, b)
                    pe.wait_ge(*banks.emptied("xn_t", stage, b))
                    mm(bk, w(pack, "wq"), xn_t[:, b, :]).then_inc(filled, 1)
                pe.wait_ge(kbd_ready, 2 * B * (layer + 1))
                pe.wait_ge(consts_made, 1)
                for b in range(B):
                    pe.wait_ge(q_parts[b], layer + 1)
                    for t in range(T):
                        for g, (h0, h1) in enumerate(HEAD_GROUPS):
                            bk = start_unit("max", layer, b, t, g)
                            last = mm(bk[:, 0:(h1 - h0) * CTX], q_hi[:, b, t * P:(t + 1) * P],
                                      kbd_hi[:, layer % 2, b, h0 * CTX:h1 * CTX], stop=layer > 0)
                            if layer == 0:
                                last = mm(bk[:, 0:(h1 - h0) * CTX].rearrange("p (h k) -> p h k", k=CTX),
                                          ident16[:, :],
                                          mask_b16[:, b, t, :].unsqueeze(1).broadcast_to([P, h1 - h0, CTX]),
                                          start=False)
                            last.then_inc(filled, 1)
                for b in range(B):
                    bk = start_unit("max_t", layer, b)
                    pe.wait_ge(max_ready[b], layer + 1)
                    for t in range(T):
                        last = nc.tensor.transpose(bk[0:2 * H, t * P:(t + 1) * P],
                                                   mx_parts[:, b, t, :].bitcast(F32), ident)
                    last.then_inc(filled, 1)
                    for c in range(NC):
                        bk = start_unit("p", layer, b, c)
                        r = ROWS[c]
                        hi = kbd_hi[:, layer % 2, b, c * P:c * P + r]
                        lo = kbd_lo[:, layer % 2, b, c * P:c * P + r]
                        mm(bk[0:r, :], lo, q_hi[:, b, :], stop=False)
                        mm(bk[0:r, :], hi, q_lo[:, b, :], start=False, stop=False)
                        mm(bk[0:r, :], hi, q_hi[:, b, :], start=False, stop=False)
                        if layer == 0:
                            pe.wait_ge(*banks.emptied("mask_t", b))
                            mm(bk[0:r, :], key_of[:, c * P:c * P + r], mask_t[:, b, :], start=False, stop=False)
                        if c == 0:
                            pe.wait_ge(*banks.emptied("max_t", layer, b))
                        mm(bk[0:r, :], neg_ind[:, c * P:c * P + r], max_t[:, b, :], start=False).then_inc(filled, 1)
                for b in range(B):
                    pe.wait_ge(*banks.emptied("p", layer, b, NC - 1))
                    pe.wait_ge(*banks.emptied("vrows", layer, b))
                    for u in range(T // 2):
                        bk = start_unit("pv", layer, b, u)
                        for i in range(2):
                            t = 2 * u + i
                            for c in range(NC):
                                at_ = i * H * VC + FIRST_HEAD[c] * VC
                                last = mm(bk[:, at_:at_ + WIN * VC], wide[0:ROWS[c], b, c, t * P:(t + 1) * P],
                                          v_win[0:ROWS[c], layer, b, c * WIN:(c + 1) * WIN, :]
                                          .rearrange("p j e -> p (j e)"),
                                          start=c == 0, stop=c == NC - 1, skip_group_check=True)
                        last.then_inc(filled, 1)
                for b in range(B):
                    bk = start_unit("o_t", layer, b)
                    pe.wait_ge(*banks.emptied("pv", layer, b, T // 2 - 1))
                    for t in range(T):
                        last = nc.tensor.transpose(bk[:, t * P:(t + 1) * P], o[:, b, t, :], ident)
                    last.then_inc(filled, 1)
                for b in range(B):
                    bk = start_unit("out", stage, b)
                    pe.wait_ge(*banks.emptied("o_t", layer, b))
                    for t in range(T):
                        last = mm(bk[:, t * P:(t + 1) * P], o_t[:, b, t * P:(t + 1) * P], w(pack, "wo"))
                    last.then_inc(filled, 1)

            def ffn0():
                turn(1)
                pe.wait_ge(loaded["ffn0"], 16)
                for b in range(B):
                    pe.wait_ge(*banks.emptied("xn_t", 1, b))
                    for m in range(C0):
                        bk = start_unit("h0", b, m)
                        mm(bk, w("ffn0", "w1")[:, m * P:(m + 1) * P], xn_t[:, b, :]).then_inc(filled, 1)
                for b in range(B):
                    bk = start_unit("out", 1, b)
                    pe.wait_ge(*banks.emptied("h0", b, C0 - 1))
                    pe.wait_ge(*banks.emptied("h0", b, C0 - 2))
                    for t in range(T):
                        for m in range(C0):
                            last = mm(bk[:, t * P:(t + 1) * P], wide[:, b, m, t * P:(t + 1) * P],
                                      w("ffn0", "w2")[:, m * D:(m + 1) * D], start=m == 0, stop=m == C0 - 1)
                    last.then_inc(filled, 1)

            def ffn1():
                turn(3)
                pe.wait_ge(loaded["ffn1"], 16)
                for b in range(B):
                    bk = start_unit("gates1", b)
                    pe.wait_ge(*banks.emptied("xn_t", 3, b))
                    for t in range(T):
                        last = mm(bk[:, t * (E1 + 1):(t + 1) * (E1 + 1)], xn_t[:, b, t * P:(t + 1) * P],
                                  w("ffn1", "gates"))
                    last.then_inc(filled, 1)
                for b in range(B):
                    for i, (lo, n) in enumerate(SHC):
                        bk = start_unit("s_g", b, i)
                        mm(bk[0:n, :], w("ffn1", "s_g")[:, lo:lo + n], xn_t[:, b, :]).then_inc(filled, 1)
                        bk = start_unit("s_u", b, i)
                        mm(bk[0:n, :], w("ffn1", "s_u")[:, lo:lo + n], xn_t[:, b, :]).then_inc(filled, 1)
                    bk = start_unit("comb_t", b)
                    pe.wait_ge(comb_ready[b], 1)
                    for t in range(T):
                        last = nc.tensor.transpose(bk[0:2 * E1, t * P:(t + 1) * P], comb[:, b, t, :].bitcast(F32),
                                                   ident)
                    last.then_inc(filled, 1)
                    for c in range(C1):
                        bk = start_unit("e_g", b, c)
                        mm(bk, w("ffn1", "w_g")[:, c * P:(c + 1) * P], xn_t[:, b, :]).then_inc(filled, 1)
                        bk = start_unit("e_u", b, c)
                        mm(bk, w("ffn1", "w_u")[:, c * P:(c + 1) * P], xn_t[:, b, :]).then_inc(filled, 1)
                        bk = start_unit("e_w", b, c)
                        if c == 0:
                            pe.wait_ge(*banks.emptied("comb_t", b))
                        mm(bk, sel1[:, c * P:(c + 1) * P], max_t[:, b, :]).then_inc(filled, 1)
                for b in range(B):
                    bk = start_unit("s_out", b)
                    pe.wait_ge(*banks.emptied("s_u", b, len(SHC) - 1))
                    for t in range(T):
                        for i, (lo, n) in enumerate(SHC):
                            last = mm(bk[:, t * P:(t + 1) * P], wide[0:n, b, C1 + i, t * P:(t + 1) * P],
                                      w("ffn1", "s_down")[0:n, i * D:(i + 1) * D], start=i == 0,
                                      stop=i == len(SHC) - 1)
                    last.then_inc(filled, 1)
                    bk = start_unit("out", 3, b)
                    pe.wait_ge(*banks.emptied("e_w", b, C1 - 1))
                    for t in range(T):
                        for c in range(C1):
                            last = mm(bk[:, t * P:(t + 1) * P], wide[:, b, c, t * P:(t + 1) * P],
                                      w("ffn1", "w_down")[:, c * D:(c + 1) * D], start=c == 0, stop=c == C1 - 1)
                    last.then_inc(filled, 1)

            def ffn2():
                turn(5)
                pe.wait_ge(loaded["ffn2"], 16)
                for b in range(B):
                    bk = start_unit("router", b)
                    pe.wait_ge(*banks.emptied("xn_t", 5, b))
                    for t in range(T):
                        last = mm(bk[:, t * E2:(t + 1) * E2], xn_t[:, b, t * P:(t + 1) * P], w("ffn2", "router"))
                    last.then_inc(filled, 1)
                for b in range(B):
                    bk = start_unit("hot_t", b)
                    pe.wait_ge(hot_ready[b], 1)
                    for t in range(T):
                        last = nc.tensor.transpose(bk[0:E2, t * P:(t + 1) * P], route[:, b, 3, t, :], ident)
                    last.then_inc(filled, 1)
                for b in range(B):
                    for c in range(C2):
                        bk = start_unit("h2", b, c)
                        mm(bk, w("ffn2", "w1")[:, c * P:(c + 1) * P], xn_t[:, b, :], stop=False)
                        if c == 0:
                            pe.wait_ge(nothot_ready[b], 1)
                        mm(bk, sel2[:, c * P:(c + 1) * P], nothot_t[:, b, :], start=False).then_inc(filled, 1)
                for b in range(B):
                    bk = start_unit("out", 5, b)
                    pe.wait_ge(*banks.emptied("h2", b, C2 - 1))
                    pe.wait_ge(*banks.emptied("h2", b, C2 - 2))
                    for t in range(T):
                        for c in range(C2):
                            mm(bk[:, t * P:(t + 1) * P], wide[:, b, c, t * P:(t + 1) * P],
                               w("ffn2", "w2")[:, c * D:(c + 1) * D], start=c == 0, stop=False)
                        last = mm(bk[:, t * P:(t + 1) * P], hot_t[:, b, t * P:(t + 1) * P],
                                  w("ffn2", "bias2")[0:E2, :], start=False)
                    last.then_inc(filled, 1)

            def slot_attention():
                turn(6)
                for it in range(ITERS):
                    for b in range(B):
                        bk = start_unit("ss", it, b)
                        pe.wait_ge(sq_ready[b], it + 1)
                        for t in range(T):
                            last = mm(bk[:, t:t + 1], sq[:, b, t * P:(t + 1) * P], ones[:, 1:2])
                        last.then_inc(filled, 1)
                    for b in range(B):
                        bk = start_unit("s", it, b)
                        if it == 0:
                            pe.wait_ge(*banks.emptied("kq"))
                        mm(bk[0:CTX, :], kq[:, b * CTX:(b + 1) * CTX], slots_t[:, b, :]).then_inc(filled, 1)
                    for b in range(B):
                        bk = start_unit("rstd_b", it, b)
                        pe.wait_ge(rstd_ready[b], it + 1)
                        for t in range(T):
                            last = mm(bk[0:CTX, t * P:(t + 1) * P], nw[:, b, 2, t:t + 1].broadcast_to([P, CTX]), ident)
                        last.then_inc(filled, 1)
                    for b in range(B):
                        bk = start_unit("asum", it, b)
                        pe.wait_ge(at_ready[b], it + 1)
                        for t in range(T):
                            last = mm(bk[:, t:t + 1], at[0:CTX, b, t * P:(t + 1) * P], ones[0:CTX, 0:1])
                        last.then_inc(filled, 1)
                    for b in range(B):
                        bk = start_unit("ra_b", it, b)
                        pe.wait_ge(ra_ready[b], it + 1)
                        for t in range(T):
                            last = mm(bk[0:CTX, t * P:(t + 1) * P],
                                      route_s[:, b, 1, t:t + 1].broadcast_to([P, CTX]), ident)
                        last.then_inc(filled, 1)
                    for b in range(B):
                        def gate(name, i, parts):
                            bk = start_unit(name, it, b)
                            if "h" in parts:
                                last = mm(bk, w("attn3", "wh")[:, i * D:(i + 1) * D], slots_t[:, b, :],
                                          stop="v" not in parts)
                            if "v" in parts:
                                if name == "r":
                                    pe.wait_ge(*banks.emptied("vw", B - 1))
                                    pe.wait_ge(*banks.emptied("ra_b", it, b))
                                last = mm(bk, vw[:, b, i * D:(i + 1) * D], an[0:CTX, b, :], start="h" not in parts)
                            last.then_inc(filled, 1)
                        gate("r", 0, "hv")
                        gate("hn", 2, "h")
                        gate("z", 1, "hv")
                        gate("n", 2, "v")
                for b in range(B):
                    bk = start_unit("out", 6, b)
                    pe.wait_ge(slots_ready[b], ITERS)
                    for t in range(T):
                        last = nc.tensor.transpose(bk[:, t * P:(t + 1) * P], slots_t[:, b, t * P:(t + 1) * P], ident)
                    last.then_inc(filled, 1)

            def quantised():
                for b in range(B):
                    bk = start_unit("q_t", b)
                    pe.wait_ge(xn_ready[b], 8)
                    for t in range(T):
                        last = nc.tensor.transpose(bk[:, t * P:(t + 1) * P], y[:, b, t, :], ident)
                    last.then_inc(filled, 1)
                pe.wait_ge(*banks.emptied("rq_t"))
                for b in range(B):
                    bk = start_unit("out", 7, b)
                    pe.wait_ge(*banks.emptied("q_t", b))
                    for t in range(T):
                        last = mm(bk[:, t * P:(t + 1) * P], lhs_q[:, b, t * P:(t + 1) * P], rhs_q[:, :])
                    last.then_inc(filled, 1)

            blocks = [lambda: attention(0, 0), ffn0, lambda: attention(2, 1), ffn1, lambda: attention(4, 2), ffn2,
                      slot_attention, quantised]
            for run in blocks[:stages]:
                run()

        @block.scalar
        def _(act):
            steps = [0]

            def link(ins):
                steps[0] += 1
                ins.then_inc(act_step, 1)
                act.wait_ge(act_step, steps[0])

            act.wait_ge(loaded["rows"], 16)
            nc.scalar.activation(gain[:, :], row("g"), ACT.Tanh).then_inc(gain_ready, 1)
            act.wait_ge(loaded["cols"], 16)
            for i in range(2):
                nc.scalar.activation(half_bias[:, i:i + 1], col("bi", i), ACT.Identity, bias=col("bh", i))
            link(nc.scalar.activation(half_bias[:, 2:3], col("bh", 2), ACT.Identity, scale=0.5))
            link(nc.scalar.activation(half_bias[:, 0:2], half_bias[:, 0:2], ACT.Identity, scale=0.5))
            for layer in range(3):
                act.wait_ge(*banks.full("k", layer))
                bk = banks.bank("k", layer)
                nc.scalar.activation(k_t[:, layer, :], bk[:, 0:B * CTX], ACT.Identity,
                                     bias=col(["bq0", "bk1", "bk2"][layer]))\
                  .then_inc(drained["act"], 1)
            act.wait_ge(loaded["ctx_rows"], 16)
            for b in range(B):
                last = nc.scalar.activation(pn[:, b, :], ctx_rows[:, b, :], ACT.Square, accum_out=p_ss[:, b:b + 1])
            last.then_inc(p_ss_ready, 1)
            for b in range(B):
                act.wait_ge(*banks.full("mask_t", b))
                nc.scalar.activation(mask_t[:, b, :], banks.bank("mask_t", b)[0:CTX, :], ACT.Copy)\
                  .then_inc(drained["act"], 1)
            act.wait_ge(*banks.full("pn_t"))
            nc.scalar.activation(pn_t[:, :], banks.bank("pn_t")[:, 0:B * CTX], ACT.Copy, scale=col("w_in"))\
              .then_inc(drained["act"], 1)
            act.wait_ge(*banks.full("kproj"))
            nc.scalar.activation(kproj[:, :], banks.bank("kproj")[:, 0:B * CTX], ACT.Copy).then_inc(drained["act"], 1)
            act.wait_ge(*banks.full("vproj"))
            nc.scalar.activation(vproj[:, :], banks.bank("vproj")[:, 0:B * CTX], ACT.Copy).then_inc(drained["act"], 1)
            for b in range(B):
                act.wait_ge(*banks.full("vw", b))
                nc.scalar.activation(vw[:, b, :], banks.bank("vw", b)[0:CTX, 0:3 * D], ACT.Copy)\
                  .then_inc(drained["act"], 1)
            act.wait_ge(*banks.full("rscale"))
            nc.scalar.activation(rscale_b[:, :], banks.bank("rscale")[:, 0:D], ACT.Copy).then_inc(drained["act"], 1)

            def turned(stage):
                for b in range(B):
                    act.wait_ge(*banks.full("xn_t", stage, b))
                    nc.scalar.activation((slots_t if stage == 6 else xn_t)[:, b, :], banks.bank("xn_t", stage, b),
                                         ACT.Copy).then_inc(drained["act"], 1)

            def attention(stage, layer):
                turned(stage)
                for b in range(B):
                    act.wait_ge(*banks.full("q", layer, b))
                    nc.scalar.activation(q_t[:, b, :], banks.bank("q", layer, b), ACT.Identity,
                                         bias=col(f"bq{layer}")).then_inc(drained["act"], 1)
                for b in range(B):
                    act.wait_ge(*banks.full("max_t", layer, b))
                    nc.scalar.activation(max_t[0:2 * H, b, :], banks.bank("max_t", layer, b)[0:2 * H, :], ACT.Copy)\
                      .then_inc(drained["act"], 1)
                    for c in range(NC):
                        r = ROWS[c]
                        act.wait_ge(*banks.full("p", layer, b, c))
                        nc.scalar.activation(wide[0:r, b, c, :], banks.bank("p", layer, b, c)[0:r, :], ACT.Exp,
                                             scale=DH ** -0.5).then_inc(drained["act"], 1)
                for b in range(B):
                    act.wait_ge(*banks.full("o_t", layer, b))
                    nc.scalar.activation(o_t[:, b, :], banks.bank("o_t", layer, b), ACT.Copy)\
                      .then_inc(drained["act"], 1)

            def ffn0():
                turned(1)
                for b in range(B):
                    for m in range(1, C0, 2):
                        act.wait_ge(*banks.full("h0", b, m))
                        nc.scalar.activation(wide[:, b, m, :], banks.bank("h0", b, m), ACT.Relu, bias=col("b1", m))\
                          .then_inc(drained["act"], 1)

            def ffn1():
                turned(3)
                for b in range(B):
                    act.wait_ge(gap_ready[b], 1)
                    nc.scalar.activation(route_s[:, b, 4, :], route_s[:, b, 3, :], ACT.Exp)
                    nc.scalar.activation(route_s[:, b, 7, :], lg[:, b, :, E1], ACT.Tanh, scale=0.5)\
                      .then_inc(second_ready[b], 1)
                n = 0
                before = []
                for b in range(B):
                    for i, (_, r) in enumerate(SHC):
                        act.wait_ge(*banks.full("s_g", b, i))
                        if n >= 2:
                            act.wait_ge(*banks.emptied(*before[n - 2]))
                        nc.scalar.activation(act_s[0:r, n % 2, :], banks.bank("s_g", b, i)[0:r, :], ACT.Silu)\
                          .then_inc(drained["act"], 1)
                        before.append(("s_u", b, i))
                        n += 1
                    act.wait_ge(*banks.full("comb_t", b))
                    nc.scalar.activation(max_t[0:2 * E1, b, :], banks.bank("comb_t", b)[0:2 * E1, :], ACT.Copy)\
                      .then_inc(drained["act"], 1)
                    for c in range(C1):
                        act.wait_ge(*banks.full("e_g", b, c))
                        if n >= 2:
                            act.wait_ge(*banks.emptied(*before[n - 2]))
                        nc.scalar.activation(act_s[:, n % 2, :], banks.bank("e_g", b, c), ACT.Silu)\
                          .then_inc(drained["act"], 1)
                        before.append(("e_u", b, c))
                        n += 1

            def ffn2():
                turned(5)
                for b in range(B):
                    act.wait_ge(*banks.full("hot_t", b))
                    nc.scalar.activation(hot_t[:, b, :], banks.bank("hot_t", b)[0:E2, :], ACT.Copy)\
                      .then_inc(drained["act"], 1)
                for b in range(B):
                    for c in range(1, C2, 2):
                        act.wait_ge(*banks.full("h2", b, c))
                        nc.scalar.activation(wide[:, b, c, :], banks.bank("h2", b, c), ACT.Relu,
                                             bias=col("bias1", c)).then_inc(drained["act"], 1)
                for b in range(B):
                    act.wait_ge(*banks.full("out", 5, b))
                    nc.scalar.activation(y[:, b, :, :].rearrange("p t d -> p (t d)"), banks.bank("out", 5, b), ACT.Relu)\
                      .then_inc(drained["act"], 1)

            def slot_attention():
                turned(6)
                for it in range(ITERS):
                    for b in range(B):
                        if it == 0:
                            act.wait_ge(*banks.emptied("xn_t", 6, b))
                        else:
                            act.wait_ge(slots_ready[b], it)
                        nc.scalar.activation(sq[:, b, :], slots_t[:, b, :], ACT.Square).then_inc(sq_ready[b], 1)
                    for b in range(B):
                        act.wait_ge(*banks.full("rstd_b", it, b))
                        nc.scalar.activation(rb[0:CTX, b, :], banks.bank("rstd_b", it, b)[0:CTX, :], ACT.Copy)\
                          .then_inc(drained["act"], 1)
                    for b in range(B):
                        act.wait_ge(nmax_ready[b], it + 1)
                        nc.scalar.activation(ex[0:CTX, b, :], sc[0:CTX, b, :], ACT.Exp, bias=nmax[:, b, 0:1],
                                             accum_out=nmax[:, b, 1:2]).then_inc(ex_ready[b], 1)
                    for b in range(B):
                        for name, dst, bias, fn in (("r", tr, 0, ACT.Tanh), ("hn", hnb, 2, ACT.Identity),
                                                    ("z", tz, 1, ACT.Tanh)):
                            act.wait_ge(*banks.full(name, it, b))
                            nc.scalar.activation(dst[:, b, :], banks.bank(name, it, b), fn,
                                                 bias=half_bias[:, bias:bias + 1], scale=0.5)\
                              .then_inc(drained["act"], 1)
                    for b in range(B):
                        act.wait_ge(*banks.emptied("n", it, b))
                        nc.scalar.activation(nn[:, b, :], tt[:, b, :], ACT.Tanh, bias=col("bi", 2))\
                          .then_inc(n_ready[b], 1)

            blocks = [lambda: attention(0, 0), ffn0, lambda: attention(2, 1), ffn1, lambda: attention(4, 2), ffn2,
                      slot_attention]
            for run in blocks[:stages]:
                run()

        @block.vector
        def _(dve):
            steps = [0]

            def link(ins):
                steps[0] += 1
                ins.then_inc(dve_step, 1)
                dve.wait_ge(dve_step, steps[0])

            V = nc.vector

            def rsqrt(work, src, scale, eps, first=link):
                v, hv, r, t = (work[:, i, :] for i in range(4))
                first(V.tensor_scalar(v, src, scale, eps, ALU.mult, ALU.add))
                V.tensor_scalar(r.bitcast(I32), v.bitcast(I32), -0.5, 1597463007.0, ALU.mult, ALU.add)
                link(V.tensor_scalar(hv, v, -0.5, None, ALU.mult))
                for i in range(3):
                    link(V.tensor_tensor(t, r, r, ALU.mult))
                    link(V.tensor_tensor(t, t, hv, ALU.mult))
                    last = V.scalar_tensor_tensor(r, t, 1.5, r, ALU.add, ALU.mult)
                    if i < 2:
                        link(last)
                return last

            def normalise(stage, b):
                for t in range(T):
                    last = V.bn_stats(stats[:, b, t, :], x[:, b, t, :])
                link(last)
                for t in range(T):
                    last = V.bn_aggr(mv[:, b, t, :], stats[:, b, t, :])
                link(last)
                link(rsqrt(nw[:, b, :, :], mv[:, b, :, 1], 1.0, LN_EPS))
                for t in range(T):
                    last = V.tensor_scalar(xn[:, b, t, :], x[:, b, t, :], mv[:, b, t, 0:1], nw[:, b, 2, t:t + 1],
                                           ALU.subtract, ALU.mult)
                if stage < 7:
                    last.then_inc(xn_ready[b], 1)
                    return
                link(last)
                amax, scale, inverse = (route_s[:, b, i, :] for i in (2, 3, 4))
                link(V.tensor_reduce(amax, xn[:, b, :, :], AX.X, ALU.max, apply_absolute_value=True))
                link(V.tensor_scalar(scale, amax, 1e-12, 1.0 / 127.0, ALU.max, ALU.mult))
                link(V.reciprocal(inverse, scale))
                for t in range(T):
                    last = V.tensor_scalar(y[:, b, t, :], xn[:, b, t, :], inverse[:, t:t + 1], ROUND, ALU.mult, ALU.add)
                link(last)
                V.tensor_scalar(y[:, b, :, :], y[:, b, :, :], ROUND, 127.0, ALU.subtract, ALU.min)\
                 .then_inc(xn_ready[b], 1)

            def flat(tile):
                return tile.rearrange("p t d -> p (t d)")

            def add_out(stage, b):
                dve.wait_ge(*banks.full("out", stage, b))
                if stage in BIASED:
                    dve.wait_ge(bias_added[b], BIASED[stage] + 1)
                g = GAIN_OF[stage]
                V.scalar_tensor_tensor(flat(x[:, b, :, :]), banks.bank("out", stage, b), gain[:, g:g + 1],
                                       flat(x[:, b, :, :]), ALU.mult, ALU.add).then_inc(drained["dve"], 1)
                dve.wait_ge(*banks.emptied("out", stage, b))

            dve.wait_ge(loaded["x"], 16)
            for b in range(B):
                normalise(0, b)
            dve.wait_ge(loaded["rows"], 16)
            dve.wait_ge(gain_ready, 1)
            for i, (name, stage) in enumerate((("bo0", 0), ("b2", 1), ("bo1", 2), ("bo2", 4))):
                g = GAIN_OF[stage]
                last = V.tensor_scalar(gbias[:, i, :], row(name), gain[:, g:g + 1], None, ALU.mult)
            last.then_inc(gbias_ready, 1)
            dve.wait_ge(loaded["mask"], 16)
            for b in range(B):
                V.tensor_scalar(mask_b16[:, b, :, :], mask_i[:, b, :, :], 0.0, MASKED, ALU.is_equal, ALU.mult)
                V.tensor_scalar(mask_b[:, b, :, :], mask_i[:, b, :, :], 0.0, MASKED, ALU.is_equal, ALU.mult)\
                 .then_inc(mask_b_ready, 1)
            dve.wait_ge(loaded["consts"], 16)
            for layer in range(3):
                dve.wait_ge(*banks.emptied("k", layer))
                link(V.tensor_copy(k_hi[:, layer, :], k_t[:, layer, :]))
                V.tensor_tensor(k_lo[:, layer, :], k_t[:, layer, :], k_hi[:, layer, :].bitcast(F32), ALU.subtract)\
                 .then_inc(k_parts, 1)
                dve.wait_ge(*banks.full("v", layer))
                V.tensor_tensor(v_rows[:, layer, :, :],
                                banks.bank("v", layer)[0:CTX, 0:B * D].rearrange("p (b d) -> p b d", b=B),
                                row(f"bv{layer}")[0:CTX, :].unsqueeze(1).broadcast_to([CTX, B, D]), ALU.add)\
                 .then_inc(drained["dve"], 1)
                for b in range(B):
                    V.tensor_copy(v_win[:, layer, b, :, DH], const("chunk_mask"))
                    dve.wait_ge(*banks.full("vrows", layer, b))
                    V.tensor_tensor(v_win[:, layer, b, :, 0:DH],
                                    banks.bank("vrows", layer, b)[:, 0:NC * WIN * DH].rearrange("p (j d) -> p j d", d=DH),
                                    const("chunk_mask").unsqueeze(2).broadcast_to([P, NC * WIN, DH]), ALU.mult)\
                     .then_inc(drained["dve"], 1)
            dve.wait_ge(p_ss_ready, 1)
            link(rsqrt(p_small, p_ss[:, :], 1.0 / D, RMS_EPS))
            for b in range(B):
                last = V.tensor_scalar(pn[:, b, :], ctx_rows[:, b, :], p_small[:, 2, b:b + 1], None, ALU.mult)
            last.then_inc(pn_ready, 1)
            dve.wait_ge(loaded["attn3"], 16)
            link(V.tensor_reduce(rscale[:, 0:1], w("attn3", "rhs_t"), AX.X, ALU.max, apply_absolute_value=True))
            link(V.tensor_scalar(rscale[:, 1:2], rscale[:, 0:1], 1e-12, 1.0 / 127.0, ALU.max, ALU.mult))
            link(V.reciprocal(rscale[:, 2:3], rscale[:, 1:2]))
            link(V.tensor_scalar(rq[:, :], w("attn3", "rhs_t"), rscale[:, 2:3], ROUND, ALU.mult, ALU.add))
            V.tensor_scalar(rq[:, :], rq[:, :], ROUND, 127.0, ALU.subtract, ALU.min).then_inc(rq_ready, 1)
            dve.wait_ge(*banks.full("kq"))
            V.tensor_scalar(kq[:, :], banks.bank("kq")[:, 0:B * CTX], col("w_slot"), D ** -0.5, ALU.mult, ALU.mult)\
             .then_inc(drained["dve"], 1)
            dve.wait_ge(*banks.full("rq_t"))
            V.tensor_scalar(rhs_q[:, :], banks.bank("rq_t")[:, 0:D], -127.0, None, ALU.max).then_inc(drained["dve"], 1)

            def attention(stage, layer):
                for b in range(B):
                    dve.wait_ge(*banks.emptied("q", layer, b))
                    link(V.tensor_copy(q_hi[:, b, :], q_t[:, b, :]))
                    V.tensor_tensor(q_lo[:, b, :], q_t[:, b, :], q_hi[:, b, :].bitcast(F32), ALU.subtract)\
                     .then_inc(q_parts[b], 1)
                for b in range(B):
                    for t in range(T):
                        for g, (h0, h1) in enumerate(HEAD_GROUPS):
                            dve.wait_ge(*banks.full("max", layer, b, t, g))
                            V.tensor_reduce(mx[:, b, t, h0:h1],
                                            banks.bank("max", layer, b, t, g)[:, 0:(h1 - h0) * CTX]
                                            .rearrange("p (h k) -> p h k", k=CTX), AX.X, ALU.max)\
                             .then_inc(drained["dve"], 1)
                    dve.wait_ge(*banks.emptied("max", layer, b, T - 1, len(HEAD_GROUPS) - 1))
                    link(V.tensor_copy(mx_parts[:, b, :, 0:H], mx[:, b, :, :]))
                    V.tensor_tensor(mx_parts[:, b, :, H:2 * H], mx[:, b, :, :],
                                    mx_parts[:, b, :, 0:H].bitcast(F32), ALU.subtract).then_inc(max_ready[b], 1)
                for b in range(B):
                    for u in range(T // 2):
                        dve.wait_ge(*banks.full("pv", layer, b, u))
                        both = banks.bank("pv", layer, b, u)[:, 0:2 * H * VC].rearrange("p (h e) -> p h e", e=VC)
                        sums = rsum[:, b, 2 * u:2 * u + 2, :].rearrange("p t h -> p (t h)")
                        link(V.reciprocal(sums, both[:, :, DH]))
                        V.tensor_tensor(o[:, b, 2 * u:2 * u + 2, :].rearrange("p t (h d) -> p (t h) d", d=DH),
                                        both[:, :, 0:DH], sums.unsqueeze(2).broadcast_to([P, 2 * H, DH]), ALU.mult)\
                         .then_inc(drained["dve"], 1)
                for b in range(B):
                    add_out(stage, b)
                    normalise(stage + 1, b)

            def ffn0():
                for b in range(B):
                    for m in range(0, C0, 2):
                        dve.wait_ge(*banks.full("h0", b, m))
                        V.tensor_scalar(wide[:, b, m, :], banks.bank("h0", b, m), col("b1", m), 0.0, ALU.add, ALU.max)\
                         .then_inc(drained["dve"], 1)
                for b in range(B):
                    add_out(1, b)
                    normalise(2, b)

            def largest(b, logits, n, top, ids, rev):
                link(V.tensor_reduce(top, logits, AX.X, ALU.max))
                eq, order = route[:, b, 0, :, 0:n], route[:, b, 1, :, 0:n]
                first = route_s[:, b, 1, :]
                link(V.tensor_tensor(eq, logits, top.unsqueeze(2).broadcast_to([P, T, n]), ALU.is_equal))
                link(V.tensor_tensor(order, eq, rev, ALU.mult))
                link(V.tensor_reduce(first, order, AX.X, ALU.max))
                return V.tensor_tensor(ids, rev, first.unsqueeze(2).broadcast_to([P, T, n]), ALU.is_equal)

            def ffn1():
                rev = const("rev16").unsqueeze(1).broadcast_to([P, T, E1])
                for b in range(B):
                    dve.wait_ge(*banks.full("gates1", b))
                    V.tensor_copy(lg[:, b, :, 0:E1 + 1],
                                  banks.bank("gates1", b)[:, 0:T * (E1 + 1)].rearrange("p (t e) -> p t e", t=T))\
                     .then_inc(drained["dve"], 1)
                    dve.wait_ge(*banks.emptied("gates1", b))
                    logits = lg[:, b, :, 0:E1]
                    top, second, gap, e2, w1_, w2_, shared = (route_s[:, b, i, :] for i in (0, 2, 3, 4, 5, 6, 7))
                    one, two, rest = (route[:, b, i, :, 0:E1] for i in (2, 3, 4))
                    link(largest(b, logits, E1, top, one, rev))
                    link(V.scalar_tensor_tensor(rest, one, -3e38, logits, ALU.mult, ALU.add))
                    link(largest(b, rest, E1, second, two, rev))
                    V.tensor_tensor(gap, second, top, ALU.subtract).then_inc(gap_ready[b], 1)
                    dve.wait_ge(second_ready[b], 1)
                    link(V.tensor_scalar(w2_, e2, 1.0, None, ALU.add))
                    link(V.reciprocal(w1_, w2_))
                    link(V.tensor_tensor(w2_, e2, w1_, ALU.mult))
                    link(V.tensor_scalar(shared, shared, 0.5, 0.5, ALU.mult, ALU.add))
                    link(V.tensor_scalar(shared, shared, gain[:, GAIN_OF[3]:GAIN_OF[3] + 1], None, ALU.mult))
                    V.tensor_tensor(one, one, w1_.unsqueeze(2).broadcast_to([P, T, E1]), ALU.mult)
                    link(V.tensor_tensor(two, two, w2_.unsqueeze(2).broadcast_to([P, T, E1]), ALU.mult))
                    link(V.tensor_tensor(rest, one, two, ALU.add))
                    link(V.tensor_copy(comb[:, b, :, 0:E1], rest))
                    V.tensor_tensor(comb[:, b, :, E1:2 * E1], rest, comb[:, b, :, 0:E1].bitcast(F32), ALU.subtract)\
                     .then_inc(comb_ready[b], 1)
                n = 0
                for b in range(B):
                    for i, (_, r) in enumerate(SHC):
                        dve.wait_ge(*banks.emptied("s_g", b, i))
                        dve.wait_ge(*banks.full("s_u", b, i))
                        V.tensor_tensor(wide[0:r, b, C1 + i, :], act_s[0:r, n % 2, :], banks.bank("s_u", b, i)[0:r, :],
                                        ALU.mult).then_inc(drained["dve"], 1)
                        n += 1
                    for c in range(C1):
                        dve.wait_ge(*banks.emptied("e_g", b, c))
                        dve.wait_ge(*banks.full("e_u", b, c))
                        V.tensor_tensor(act_u[:, n % 2, :], act_s[:, n % 2, :], banks.bank("e_u", b, c), ALU.mult)\
                         .then_inc(drained["dve"], 1)
                        dve.wait_ge(*banks.emptied("e_u", b, c))
                        dve.wait_ge(*banks.full("e_w", b, c))
                        V.tensor_tensor(wide[:, b, c, :], act_u[:, n % 2, :], banks.bank("e_w", b, c), ALU.mult)\
                         .then_inc(drained["dve"], 1)
                        n += 1
                for b in range(B):
                    dve.wait_ge(*banks.full("s_out", b))
                    for t in range(T):
                        last = V.scalar_tensor_tensor(x[:, b, t, :], banks.bank("s_out", b)[:, t * P:(t + 1) * P],
                                                      route_s[:, b, 7, t:t + 1], x[:, b, t, :], ALU.mult, ALU.add)
                    last.then_inc(drained["dve"], 1)
                    dve.wait_ge(*banks.emptied("s_out", b))
                    add_out(3, b)
                    normalise(4, b)

            def ffn2():
                rev = const("rev32").unsqueeze(1).broadcast_to([P, T, E2])
                for b in range(B):
                    dve.wait_ge(*banks.full("router", b))
                    V.tensor_tensor(lg[:, b, :, :], banks.bank("router", b)[:, 0:T * E2].rearrange("p (t e) -> p t e", t=T),
                                    row("router_b").unsqueeze(1).broadcast_to([P, T, E2]), ALU.add)\
                     .then_inc(drained["dve"], 1)
                    dve.wait_ge(*banks.emptied("router", b))
                    largest(b, lg[:, b, :, :], E2, route_s[:, b, 0, :], route[:, b, 3, :, :], rev)\
                        .then_inc(hot_ready[b], 1)
                for b in range(B):
                    dve.wait_ge(*banks.emptied("hot_t", b))
                    V.tensor_scalar(nothot_t[0:E2, b, :], hot_t[:, b, :], 1.0, -MASKED, ALU.subtract, ALU.mult)\
                     .then_inc(nothot_ready[b], 1)
                for b in range(B):
                    for c in range(0, C2, 2):
                        dve.wait_ge(*banks.full("h2", b, c))
                        V.tensor_scalar(wide[:, b, c, :], banks.bank("h2", b, c), col("bias1", c), 0.0, ALU.add, ALU.max)\
                         .then_inc(drained["dve"], 1)
                g = GAIN_OF[5]
                for b in range(B):
                    dve.wait_ge(*banks.emptied("out", 5, b))
                    link(V.scalar_tensor_tensor(flat(x[:, b, :, :]), flat(y[:, b, :, :]), gain[:, g:g + 1],
                                                flat(x[:, b, :, :]), ALU.mult, ALU.add))
                    normalise(6, b)

            def slot_attention():
                def release(ins):
                    ins.then_inc(drained["dve"], 1)

                for it in range(ITERS):
                    for b in range(B):
                        dve.wait_ge(*banks.full("ss", it, b))

                        def first(ins):
                            release(ins)
                            dve.wait_ge(*banks.emptied("ss", it, b))
                        rsqrt(nw[:, b, :, :], banks.bank("ss", it, b)[:, 0:T], 1.0, RMS_EPS, first)\
                            .then_inc(rstd_ready[b], 1)
                    for b in range(B):
                        dve.wait_ge(*banks.full("s", it, b))
                        dve.wait_ge(*banks.emptied("rstd_b", it, b))
                        V.tensor_tensor(sc[0:CTX, b, :], banks.bank("s", it, b)[0:CTX, :], rb[0:CTX, b, :], ALU.mult)\
                         .then_inc(drained["dve"], 1)
                        dve.wait_ge(*banks.emptied("s", it, b))
                        V.tensor_reduce(nmax[:, b, 0:1], sc[0:CTX, b, :], AX.X, ALU.max, negate=True)\
                         .then_inc(nmax_ready[b], 1)
                    for b in range(B):
                        dve.wait_ge(ex_ready[b], it + 1)
                        link(V.reciprocal(nmax[:, b, 2:3], nmax[:, b, 1:2]))
                        V.tensor_scalar(at[0:CTX, b, :], ex[0:CTX, b, :], nmax[:, b, 2:3], None, ALU.mult)\
                         .then_inc(at_ready[b], 1)
                    for b in range(B):
                        dve.wait_ge(*banks.full("asum", it, b))
                        V.tensor_scalar(route_s[:, b, 0, :], banks.bank("asum", it, b)[:, 0:T], RMS_EPS, None, ALU.add)\
                         .then_inc(drained["dve"], 1)
                        dve.wait_ge(*banks.emptied("asum", it, b))
                        V.reciprocal(route_s[:, b, 1, :], route_s[:, b, 0, :]).then_inc(ra_ready[b], 1)
                    for b in range(B):
                        dve.wait_ge(*banks.full("ra_b", it, b))
                        V.tensor_tensor(an[0:CTX, b, :], at[0:CTX, b, :], banks.bank("ra_b", it, b)[0:CTX, :], ALU.mult)\
                         .then_inc(drained["dve"], 1)
                    for b in range(B):
                        dve.wait_ge(*banks.emptied("hn", it, b))
                        link(V.scalar_tensor_tensor(tt[:, b, :], tr[:, b, :], 1.0, hnb[:, b, :], ALU.add, ALU.mult))
                        dve.wait_ge(*banks.full("n", it, b))
                        V.tensor_tensor(tt[:, b, :], tt[:, b, :], banks.bank("n", it, b), ALU.add)\
                         .then_inc(drained["dve"], 1)
                    for b in range(B):
                        dve.wait_ge(n_ready[b], it + 1)
                        link(V.tensor_tensor(dd[:, b, :], slots_t[:, b, :], nn[:, b, :], ALU.subtract))
                        link(V.scalar_tensor_tensor(dd[:, b, :], tz[:, b, :], 1.0, dd[:, b, :], ALU.add, ALU.mult))
                        V.scalar_tensor_tensor(slots_t[:, b, :], dd[:, b, :], 0.5, nn[:, b, :], ALU.mult, ALU.add)\
                         .then_inc(slots_ready[b], 1)
                for b in range(B):
                    add_out(6, b)
                    normalise(7, b)

            def quantised():
                for b in range(B):
                    dve.wait_ge(*banks.full("q_t", b))
                    V.tensor_scalar(lhs_q[:, b, :], banks.bank("q_t", b), -127.0, None, ALU.max)\
                     .then_inc(drained["dve"], 1)
                g = GAIN_OF[7]
                dve.wait_ge(*banks.emptied("rscale"))
                for b in range(B):
                    dve.wait_ge(*banks.full("out", 7, b))
                    for t in range(T):
                        last = V.scalar_tensor_tensor(o[:, b, t, :], banks.bank("out", 7, b)[:, t * P:(t + 1) * P],
                                                      route_s[:, b, 3, t:t + 1], rscale_b[:, :], ALU.mult, ALU.mult)
                    last.then_inc(drained["dve"], 1)
                    dve.wait_ge(*banks.emptied("out", 7, b))
                    V.scalar_tensor_tensor(flat(x[:, b, :, :]), flat(o[:, b, :, :]), gain[:, g:g + 1],
                                           flat(x[:, b, :, :]), ALU.mult, ALU.add).then_inc(x_final[b], 1)

            blocks = [lambda: attention(0, 0), ffn0, lambda: attention(2, 1), ffn1, lambda: attention(4, 2), ffn2,
                      slot_attention, quantised]
            for run in blocks[:stages]:
                run()
            if stages < 8:
                for b in range(B):
                    link(V.tensor_copy(y[:, b, :, :], x[:, b, :, :]))
                    V.tensor_copy(x[:, b, :, :], y[:, b, :, :]).then_inc(x_final[b], 1)



def _constants():
    part = np.arange(P)
    pair = np.arange(NC * P)
    head, key = pair // CTX, pair % CTX
    real = pair < HK
    out = {
        "ident": np.eye(P),
        "head_mask": part[:, None] // DH == np.arange(H)[None, :],
        "rev16": np.broadcast_to(E1 - np.arange(E1), (P, E1)),
        "rev32": np.broadcast_to(E2 - np.arange(E2), (P, E2)),
        "neg_ind": -1.0 * ((part[:, None] < 2 * H) & (part[:, None] % H == head[None, :HK])),
        "key_of": (part[:, None] == key[None, :]) & real[None, :],
        "sel1": (part[:, None] < 2 * E1) & (part[:, None] % E1 == np.arange(C1 * P)[None, :] // F1),
        "sel2": part[:, None] == np.arange(C2 * P)[None, :] // F2,
    }
    chunk_mask = np.zeros((P, NC, WIN))
    for c in range(NC):
        for j in range(WIN):
            chunk_mask[:, c, j] = (head[c * P:(c + 1) * P] == FIRST_HEAD[c] + j) & real[c * P:(c + 1) * P]
    out["chunk_mask"] = chunk_mask.reshape(P, NC * WIN)
    return [np.concatenate([np.asarray(out[name], np.float32).reshape(P, n) for name, n in pack], 1)
            for pack in (CONSTS, CONSTS_ONCE)]


def _side_by_side(m, n=P):
    k = -(-m.shape[0] // n)
    full = np.zeros((k * n,) + m.shape[1:], m.dtype)
    full[:m.shape[0]] = m
    return full.reshape(k, n, -1).transpose(1, 0, 2).reshape(n, -1)


def _layout(i):
    heads = lambda m: np.tile(m, (1, H))
    column = lambda v: np.reshape(v, (-1, P)).T
    packed = {
        "cols": [column(i["L0_xattn_bq"]), column(i["L1_xattn_bq"]), column(np.tile(i["L1_xattn_bk"], H)),
                 column(i["L2_xattn_bq"]), column(i["L2_xattn_bk"]), column(i["L0_ffn_b1"]),
                 column(i["L2_ffn_bias1"]), column(i["L3_xattn_gru_bi"]), column(i["L3_xattn_gru_bh"]),
                 column(i["L3_xattn_slot_norm_w"]), column(i["L3_xattn_input_norm_w"])],
        "rows": [v[None, :] for v in (
            np.concatenate([i["g_xattn"], i["g_ffn"]]), i["L0_xattn_bq"], np.tile(i["L1_xattn_bv"], H),
            i["L2_xattn_bv"], i["L0_xattn_bo"], i["L0_ffn_b2"], i["L1_xattn_bo"], i["L2_xattn_bo"],
            i["L2_ffn_router_b"])],
        "attn0": [i["L0_xattn_Wq"].T, i["L0_xattn_Wo"].T],
        "ffn0": [i["L0_ffn_w1"], _side_by_side(i["L0_ffn_w2"])],
        "attn1": [heads(i["L1_xattn_Wk"]), heads(i["L1_xattn_Wv"]), i["L1_xattn_Wq"], i["L1_xattn_Wo"]],
        "ffn1": [i["L1_ffn_gate_w"].T, i["L1_ffn_shared_gate_w"].T,
                 i["L1_ffn_w_gate_up"][:, :, :F1].transpose(1, 0, 2).reshape(D, E1 * F1),
                 i["L1_ffn_w_gate_up"][:, :, F1:].transpose(1, 0, 2).reshape(D, E1 * F1),
                 _side_by_side(i["L1_ffn_w_down"].reshape(E1 * F1, D)),
                 i["L1_ffn_shared_w_gate"].T, i["L1_ffn_shared_w_up"].T, _side_by_side(i["L1_ffn_shared_w_down"].T)],
        "attn2": [i["L2_xattn_wk"].T, i["L2_xattn_wv"].T, i["L2_xattn_wq"].T, i["L2_xattn_wo"].T],
        "ffn2": [i["L2_ffn_router_w"].T, i["L2_ffn_weights1"].transpose(1, 0, 2).reshape(D, E2 * F2),
                 _side_by_side(i["L2_ffn_weights2"].reshape(E2 * F2, D)), _side_by_side(i["L2_ffn_bias2"])],
        "attn3": [i["L3_xattn_Wk"].T, i["L3_xattn_Wv"].T, i["L3_xattn_Wq"], i["L3_xattn_gru_wi"].T,
                  i["L3_xattn_gru_wh"].T, i["L3_ffn_rhs"].T],
    }
    ctx_ = i["ctx_1024"]
    constants = _constants()
    out = {"x": i["x"], "mask": i["mask_Bx1xSxS2_if1"], "ctx_rows": ctx_,
           "ctx_t": ctx_.transpose(2, 0, 1).reshape(D, B * CTX), "consts": constants[0],
           "consts_once": constants[1]}
    out.update({k: np.concatenate(v, 1) for k, v in packed.items()})
    return {k: np.ascontiguousarray(v) for k, v in out.items()}


STAGES = 8


def kernel(**inputs):
    import concourse.bacc as bacc
    from concourse.bass_utils import run_bass_kernel_spmd

    nc = bacc.Bacc("TRN2", target_bir_lowering=False, num_devices=1)
    arrays = {f"in_{k}": v for k, v in _layout({k: np.asarray(v) for k, v in inputs.items()}).items()}
    a = {k[3:]: nc.dram_tensor(k, v.shape, mybir.dt.from_np(v.dtype), kind="ExternalInput").ap()
         for k, v in arrays.items()}
    out = nc.dram_tensor("out", (B, S, D), F32, kind="ExternalOutput").ap()
    program(nc, a, out, STAGES)
    return run_bass_kernel_spmd(nc, [arrays], core_ids=[0]).results[0]["out"]
```

```python
from contextlib import ExitStack

import numpy as np

import concourse.bass as bass
from concourse import mybir

ALU = mybir.AluOpType
ACT = mybir.ActivationFunctionType
AX = mybir.AxisListType
F32 = mybir.dt.float32
F32R = mybir.dt.float32r
BF16 = mybir.dt.bfloat16
I32 = mybir.dt.int32

P = 128
B = 2
S = 512
D = 128
T = S // P
CTX = 77
H = 16
DH = D // H
G3 = 3
GROUPS = -(-H // G3)
GR = P // 4
LANES = P // GR
PART_ROWS = [P, (GROUPS - LANES) * GR]
HEADS = [min(G3, H - G3 * g) for g in range(GROUPS)]
GK = G3 * CTX
NJ = -(-GK // P)
GKE = GK + GK % 2
SETS = [[(g, 0) for g in range(LANES)], [(g, 1) for g in range(LANES)], [(4, 0), (5, 0), (4, 1)]]
SLOT = {c: i for i, c in enumerate(c for group in SETS for c in group)}
ROWS = {(g, j): min(P, HEADS[g] * CTX - P * j) for g, j in SLOT}
VALUES = G3 * DH
BANKS = 8
E1, F1, SH = 16, 64, 352
E2, F2 = 32, 32
C1 = E1 * F1 // P
SHC = [(i, min(P, SH - i)) for i in range(0, SH, P)]
C2 = E2 * F2 // P
W0 = 512
C0 = W0 // P
ITERS = 3
MASKED = -(2.0 ** 100)
ROUND = 1.5 * 2.0 ** 23
MASK_PLACES = -(-B * T * CTX // S)
LN_EPS, RMS_EPS = 1e-5, 1e-6

COLS = [("bq0", 2), ("bk0", 2), ("bq1", 2), ("bk1", 2), ("bq2", 2), ("bk2", 2), ("b1", C0), ("bias1", C2),
        ("bi", 3), ("bh", 3), ("w_slot", 1), ("w_in", 1)]
ROWSPACK = [("g", 8), ("bv0", D), ("bv1", D), ("bv2", D), ("bo0", D), ("b2", D), ("bo1", D), ("bo2", D),
            ("router_b", E2)]
CONSTS = [("ident", P), ("head_mask", GROUPS * G3), ("chunk_mask", NJ * G3), ("rev16", E1), ("rev32", E2)]
ROUNDED = [("sel1", C1 * P)]
HALVES = [("key_of", NJ * P), ("ident16", P), ("sel2", C2 * P)]
PACKS = {
    "attn0": [("wq", GROUPS * GR), ("wv", D), ("wo", D)],
    "ffn0": [("w1", W0), ("w2", C0 * D)],
    "attn1": [("wk", GROUPS * GR), ("wv", D), ("wq", GROUPS * GR), ("wo", D)],
    "ffn1": [("gates", E1 + 1), ("w_g", C1 * P), ("w_u", C1 * P), ("w_down", C1 * D), ("s_g", SH), ("s_u", SH),
             ("s_down", len(SHC) * D)],
    "attn2": [("wk", GROUPS * GR), ("wv", D), ("wq", GROUPS * GR), ("wo", D)],
    "ffn2": [("router", E2), ("w1", C2 * P), ("w2", C2 * D), ("bias2", D)],
    "attn3": [("wk", D), ("wv", D), ("wq", D), ("wi", 3 * D), ("wh", 3 * D), ("rhs_t", D)],
}


def columns(pack):
    at, out = 0, {}
    for name, n in pack:
        out[name] = (at, at + n)
        at += n
    return out, at


HANDOVER = 0.15


def half_steps():
    out = []

    def step(phase, *args, on=False, **takes):
        out.append((phase, args, on, list(takes.items())))

    def norm(stage):
        step("norm", stage, dve=1.2, pool=1.2)
        step("norm_end", stage, dve=1.0)

    def attention(stage, layer):
        step("turn", stage, pe=0.43, act=0.5)
        step("query", layer, pe=1.7, act=0.7, dve=0.7)
        for u in range(T // 2):
            step("maxima", layer, u, on=u == 0, pe=1.2 if layer else 2.4, dve=3.3 + 1.2 * (u == 0))
        step("max_rows", layer, dve=0.4, pe=0.9, act=0, dve2=1.2)
        for i in range(len(SETS)):
            step("scores", layer, i, on=i < 2, pe=0.65 * len(SETS[i]) * (1 if layer else 1.33), act=0.6)
        for part in range(2):
            step("values", layer, part, on=part == 0, pe=1.9, act=0.5)
        for u in range(T // 2):
            step("values_back", layer, u, on=u == 0, pe=0.43, dve=0.8)
        step("out_turn", layer, pe=0.43, act=0.5)
        step("project", stage, layer, pe=0.43, dve=0.7)
        norm(stage + 1)

    attention(0, 0)
    step("turn", 1, pe=0.43, act=0.5)
    for m in range(C0):
        step("hidden0", m, on=m < C0 - 1, pe=0.86, act=0.5)
    step("down0", pe=3.4, act=0.5)
    step("back", 1, pe=0.43, dve=0.7)
    norm(2)
    attention(2, 1)
    step("turn", 3, pe=0.43, act=0.5)
    step("gates1", on=True, pe=0.8, dve=3.0)
    for i in range(len(SHC)):
        step("shared", i, on=True, pe=1.7, act=0.5, dve=0.6)
    step("weights_turn", dve=1.3, pe=0.43, act=0.5)
    for c in range(C1):
        step("experts", c, on=c < C1 - 1, pe=1.95, act=0.3, dve=1.2)
    step("down1", pe=9.5, act=0.5)
    step("back", 3, pe=0.86, dve=1.8)
    norm(4)
    attention(4, 2)
    step("turn", 5, pe=0.43, act=0.5)
    step("router", pe=0.8, dve=1.6)
    step("choice_turn", pe=0.43, act=0.5, dve=0.4)
    for c in range(C2):
        step("hidden2", c, on=c < C2 - 1, pe=1.07, act=0.5)
    step("down2", pe=7.7, act=0.5)
    step("back", 5, pe=0.43, dve=0.7)
    norm(6)
    step("turn", 6, pe=0.43, act=0.5)
    for it in range(ITERS):
        step("hidden_gate", it, "r", on=True, pe=0.86)
        step("square", it, act=0.5, pe=1.5, dve=0.1, pool=1.0)
        step("hidden_gate", it, "z", on=True, pe=0.86)
        step("slot_products", it, on=True, pe=0.86)
        step("slot_scores", it, pe=0.43, dve=1.3, act=0.8)
        step("hidden_gate", it, "hn", on=True, pe=0.86)
        step("slot_sums", it, dve=0.1, pe=1.5, act=0, dve2=0.3)
        step("slot_weights", it, pe=0.43, dve=0.6)
        step("gru", it, pe=2.6, act=0.6)
        step("gru_end", it, act=0.6, dve=1.3)
    step("slots_back", pe=0.43, dve=0.7)
    step("norm", 7, dve=1.2, pool=1.2)
    step("norm_end", 7, dve=3.6)
    step("turn", 7, pe=0.43, dve=0.5)
    step("quantised", pe=0.2, dve=1.6)
    return out


def schedule():
    order = [("norm", 0, (0,)), ("norm_end", 0, (0,)), ("keys_in", 0, (0,))]
    steps = [half_steps() for _ in range(B)]
    steps[1] = [("norm", (0,), False, [("dve", 1.2), ("pool", 1.2)]), ("norm_end", (0,), False, [("dve", 1.0)])] + steps[1]
    at, free = [0.0] * B, dict.fromkeys(("pe", "act", "dve", "pool"), 0.0)
    while any(steps):
        begins = [max(at[b], free[steps[b][0][3][0][0]]) if steps[b] else 1e9 for b in range(B)]
        b = begins.index(min(begins))
        phase, args, on, takes = steps[b].pop(0)
        order.append((phase, b, args))
        now = at[b]
        for i, (engine, us) in enumerate(takes):
            engine = engine.rstrip("2")
            now = max(now, free[engine]) + us
            free[engine] = now
            now += HANDOVER
            if i == 0 or not on:
                at[b] = now
        if b == 0:
            order += [(extra, 0, extra_args) for extra, *extra_args in PREPARATIONS.get((phase, *args), [])]
    return order


PREPARATIONS = {
    ("query", 0): [("masks",)],
    ("maxima", 0, 0): [("values_in", 0)],
    ("maxima", 0, 1): [("keys_in", 1)],
    ("max_rows", 0): [("place", 0), ("keys_in", 2)],
    ("scores", 0, 0): [("values_in", 1)],
    ("scores", 0, 1): [("values_in", 2), ("place", 1)],
    ("scores", 0, 2): [("place", 2)],
    ("values", 0, 1): [("slots_in", 0)],
    ("scores", 1, 0): [("slots_in", 1)],
    ("scores", 1, 1): [("slots_in", 2)],
    ("scores", 1, 2): [("slots_in", 3)],
    ("values", 1, 1): [("slots_in", 4)],
}


SCHEDULE = schedule()


def units_of(phase, b, args):
    if phase == "keys_in":
        return [(("k", *args), "act")]
    if phase == "values_in":
        return [(("v", *args), "dve")]
    if phase == "place":
        return [(("vrows", *args, j), "dve") for j in range(NJ)]
    if phase == "masks":
        return [(("mask_t", i), "act") for i in range(B)]
    if phase == "slots_in":
        return [[], [(("pn_t",), "act")], [(("kproj",), "act"), (("vproj",), "act")],
                [(("kq",), "dve"), (("vw", 0), "act"), (("vw", 1), "act")],
                [(("rq_t",), "dve"), (("rscale",), "act")]][args[0]]
    if phase == "turn":
        return [(("xn_t", args[0], b), "dve" if args[0] == 7 else "act")]
    if phase == "maxima":
        return [(("max", args[0], b, args[1], g), "dve") for g in range(GROUPS)]
    if phase in ("query", "max_rows"):
        name, reader = ("q", "act") if phase == "query" else ("max_t", "dve")
        return [((name, args[0], b, part), reader) for part in range(2)]
    if phase == "scores":
        return [(("p", args[0], b, *chunk), "act") for chunk in SETS[args[1]]]
    if phase == "hidden0":
        return [(("h0", b, args[0]), "act" if args[0] % 2 else "dve")]
    if phase == "hidden2":
        return [(("h2", b, args[0]), "act" if args[0] % 2 else "dve")]
    if phase == "shared":
        return [(("s_g", b, args[0]), "act"), (("s_u", b, args[0]), "dve")]
    if phase == "experts":
        return [(("e_g", b, args[0]), "act"), (("e_u", b, args[0]), "dve"), (("e_w", b, args[0]), "dve")]
    if phase == "down1":
        return [(("s_y", b), "act"), (("y", 3, b), "act")]
    if phase == "back":
        return ([(("s_out", b), "dve")] if args[0] == 3 else []) + [(("out", args[0], b), "dve")]
    if phase == "hidden_gate":
        return [((args[1], args[0], b), "act")]
    if phase == "slot_products":
        return [(("s", args[0], b), "act")]
    if phase == "slot_scores":
        return [(("rstd_b", args[0], b), "dve")]
    if phase == "gru":
        return [(("n", args[0], b), "dve")]
    one = {"values": ("pv", "act"), "values_back": ("o", "dve"),
           "out_turn": ("o_t", "act"), "gates1": ("gates1", "dve"), "weights_turn": ("comb_t", "act"),
           "router": ("router", "dve"), "choice_turn": ("hot_t", "act"), "square": ("ss", "dve"),
           "slot_sums": ("asum", "dve"), "slot_weights": ("ra_b", "dve")}
    if phase in one:
        name, reader = one[phase]
        return [((name, *args[:1], b, *args[1:]), reader)]
    return {"project": [(("out", *args[:1], b), "dve")], "down0": [(("y", 1, b), "act")],
            "down2": [(("y", 5, b), "act")], "slots_back": [(("out", 6, b), "dve")],
            "quantised": [(("out", 7, b), "dve")]}.get(phase, [])


def finished_by(phase, b, args):
    if phase == "hidden_gate" and args[1] != "hn":
        return []
    gates = [((name, args[0], b), "act") for name in ("r", "z")] if phase == "gru" else []
    return gates + units_of(phase, b, args)


class Banks:

    def __init__(self, psum, filled, drained):
        self.psum, self.filled, self.drained = psum, filled, drained
        self.bank_of, self.before = {}, {}
        last_in, turn, ring = {}, 0, BANKS
        for phase, b, args in SCHEDULE:
            if phase == "hidden_gate":
                ring = BANKS // 2
            for name, _ in units_of(phase, b, args):
                assert name not in self.bank_of
                if name[0] in ("r", "z"):
                    bank = BANKS // 2 + 2 * b + (name[0] == "z")
                else:
                    bank, turn = turn % ring, turn + 1
                self.bank_of[name], self.before[name] = bank, last_in.get(bank)
                last_in[bank] = name
        self.filled_at, self.drained_at = {}, {}
        counts = {"act": 0, "dve": 0}
        for phase, b, args in SCHEDULE:
            for name, reader in finished_by(phase, b, args):
                counts[reader] += 1
                self.filled_at[name] = len(self.filled_at) + 1
                self.drained_at[name] = self.drained[reader], counts[reader]
        assert self.filled_at.keys() == self.bank_of.keys()

    def bank(self, *name):
        return self.psum[:, self.bank_of[name], :]

    def full(self, *name):
        return self.filled, self.filled_at[name]

    def emptied(self, *name):
        return self.drained_at[name]

    def reused(self, *name):
        return self.before[name] is not None

    def free(self, *name):
        return self.drained_at[self.before[name]]


def program(nc, a, out):
    with ExitStack() as ctx:
        def sb(name, shape, dt=F32):
            return ctx.enter_context(nc.sbuf_tensor(name, shape, dt))

        def sem(name):
            return ctx.enter_context(nc.semaphore(name))

        x = sb("x", [P, B, T, D])
        cols_at, cols_n = columns(COLS)
        rows_at, rows_n = columns(ROWSPACK)
        const_at, const_n = columns(CONSTS)
        halves_at, halves_n = columns(HALVES)
        rounded_at, rounded_n = columns(ROUNDED)
        cols = sb("cols", [P, cols_n])
        rows = sb("rows", [P, rows_n])
        consts = sb("consts", [P, const_n])
        ctx_t = sb("ctx_t", [P, B * CTX])
        ctx_rows = sb("ctx_rows", [CTX, B, D])
        packs = {k: sb("w_" + k, [P, columns(v)[1]]) for k, v in PACKS.items() if k != "ffn2"}
        packs["ffn2"] = packs["ffn1"][:, 0:columns(PACKS["ffn2"])[1]]

        def w(pack, name):
            lo, hi = columns(PACKS[pack])[0][name]
            return packs[pack][:, lo:hi]

        def col(name, i=0):
            lo = cols_at[name][0] + i
            return cols[:, lo:lo + 1]

        def row(name):
            lo, hi = rows_at[name]
            return rows[:, lo:hi]

        def const(name):
            lo, hi = const_at[name]
            return consts[:, lo:hi]

        halves = sb("halves", [P, halves_n], BF16)

        def half(name):
            lo, hi = halves_at[name]
            return halves[:, lo:hi]

        ident = const("ident")

        ident16, sel2 = half("ident16"), half("sel2")
        key_of = half("key_of")[0:CTX, :]
        ones = sb("ones", [P, 2])
        sel1 = sb("sel1", [P, C1 * P], F32R)
        mask_b16 = sb("mask_b16", [P, B, T, CTX], BF16)
        mask_t = sb("mask_t", [CTX, B, S], BF16)
        gain = sb("gain", [P, 8])
        gbias = sb("gbias", [P, 4, D])
        keys_hi = sb("keys_hi", [P, B, GROUPS, GKE], F32R)
        keys_lo = sb("keys_lo", [P, B, GROUPS, GKE], F32R)
        k_hi = sb("k_hi", [P, 3, 2, B, CTX], F32R)
        k_lo = sb("k_lo", [P, 3, 2, B, CTX], F32R)
        v_cols = sb("v_cols", [P, NJ, 3 * B, GROUPS, GR])
        pn = sb("pn", [CTX, B, D])
        p_ss = sb("p_ss", [CTX, B])
        p_small = sb("p_small", [CTX, 4, B])
        pn_t = sb("pn_t", [P, B * CTX])
        kproj = sb("kproj", [P, B * CTX])
        vproj = sb("vproj", [P, B * CTX])
        kq = sb("kq", [P, B * CTX])
        vw = sb("vw", [CTX, B, 3 * D])
        half_bias = sb("half_bias", [P, 3])
        rscale = sb("rscale", [P, 4])
        rq = sb("rq", [P, D])
        rhs_q = sb("rhs_q", [P, D], BF16)
        rscale_b = sb("rscale_b", [P, D])

        stats = sb("stats", [P, B, T, 6])
        mv = sb("mv", [P, B, T, 2])
        nw = sb("nw", [P, B, 4, T])
        xn = sb("xn", [P, B, T, D])
        xn_t = sb("xn_t", [P, B, S])
        q = sb("q", [P, B, 2, S])
        q_hi = sb("q_hi", [P, B, 2, S], F32R)
        q_lo = sb("q_lo", [P, B, 2, S], F32R)
        q_t, q_u = q[:, :, 0, :], q[:, :, 1, :]
        minus_half = sb("minus_half", [P, T])
        mx_raw = sb("mx_raw", [P, B, T, GROUPS, G3])
        mx_hi = sb("mx_hi", [P, B, T, GROUPS, G3], F32R)
        mx = sb("mx", [P, B, T, GROUPS, GR])
        comb_t = sb("comb_t", [P, B, S], F32R)
        wide = sb("wide", [P, B, C1 + len(SHC), S])
        rsum = sb("rsum", [P, B, T, GROUPS, G3])
        o = sb("o", [P, B, T, GROUPS * VALUES])
        lg = sb("lg", [P, B, T, E2])
        route = sb("route", [P, B, 5, T, E2])
        route_s = sb("route_s", [P, B, 8, T])
        comb = sb("comb", [P, B, T, 2 * E1], F32R)
        nothot_t = sb("nothot_t", [P, B, S], BF16)
        o_t, slots_t, y_t, s_y_t = q_t, q_t, q_t, xn_t
        lhs_q = nothot_t
        hot_t = xn[0:E2, :, :, :].rearrange("p b t d -> p b (t d)")
        mask_b = o[:, :, :, 0:CTX]
        wide3 = wide[:, :, 0:11, :]
        sq, ss, sc, ex, zs, an, tr, hnb, tz, tt, dd = [wide3[:, :, i, :] for i in range(11)]
        nn = xn_t
        act_s = [q_t, q_u]
        mask_i = wide[:, 0, 0:MASK_PLACES, :].rearrange("p c s -> p (c s)")[:, 0:B * T * CTX].bitcast(I32)\
            .rearrange("p (b t k) -> p b t k", b=B, t=T)
        early = wide[:, 1, :, :].rearrange("p c s -> p (c s)")
        k_n = 3 * 2 * B * CTX
        k_t = early[:, 0:k_n].rearrange("p (l r b k) -> p l r b k", l=3, r=2, b=B)
        v_at, v_n = k_n, 3 * B * D
        v_rows = early[0:CTX, v_at:v_at + v_n].rearrange("p (l b d) -> p l b d", l=3, b=B)
        v_parts = early[0:CTX, v_at + v_n:v_at + v_n + 3 * v_n // 2].bitcast(BF16)\
            .rearrange("p (i l b d) -> p i l b d", i=3, l=3, b=B)
        rounded_in = early[:, v_at + v_n + 3 * v_n // 2:].bitcast(BF16)
        y = wide[:, :, 0, :].rearrange("p b (t d) -> p b t d", t=T)
        nmax = sb("nmax", [CTX, B, 4])

        psum = ctx.enter_context(nc.psum_tensor("psum", [P, BANKS, 512], F32))

        loaded = {k: sem("loaded_" + k) for k in
                  ["x", "cols", "rows", "consts", "rounded", "halves", "ctx_t", "ctx_rows", "mask"] + list(PACKS)}
        filled = sem("bank_filled")
        drained = {"act": sem("bank_drained_by_act"), "dve": sem("bank_drained_by_dve")}
        consts_made = sem("consts_made")
        zeros_made = sem("zeros_made")
        dve_step = sem("dve_step")
        pool_step = sem("pool_step")
        act_step = sem("act_step")
        gain_ready = sem("gain_ready")
        gbias_ready = sem("gbias_ready")
        sums_placed = sem("sums_placed")
        rounded_ready = sem("rounded_ready")
        v_parts_ready = sem("v_parts_ready")
        k_parts = sem("k_parts")
        mask_b_ready = sem("mask_b_ready")
        p_ss_ready = sem("p_ss_ready")
        pn_ready = sem("pn_ready")
        rq_ready = sem("rq_ready")

        def per_half(name):
            return [sem(f"{name}_{b}") for b in range(B)]

        var_ready = per_half("var_ready")
        xn_rstd_ready = per_half("xn_rstd_ready")
        xn_ready = per_half("xn_ready")
        q_parts = per_half("q_parts")
        q_lo_ready = per_half("q_lo_ready")
        max_ready = per_half("max_ready")
        keys_ready = per_half("keys_ready")
        bias_added = per_half("bias_added")
        gap_ready = per_half("gap_ready")
        second_ready = per_half("second_ready")
        comb_ready = per_half("comb_ready")
        hot_ready = per_half("hot_ready")
        nothot_ready = per_half("nothot_ready")
        sq_ready = per_half("sq_ready")
        rstd_ready = per_half("rstd_ready")
        nmax_ready = per_half("nmax_ready")
        ex_ready = per_half("ex_ready")
        at_ready = per_half("at_ready")
        ra_ready = per_half("ra_ready")
        n_ready = per_half("n_ready")
        slots_ready = per_half("slots_ready")
        x_final = per_half("x_final")
        stored = sem("stored")

        banks = Banks(psum, filled, drained)
        BIASED = {0: 0, 1: 1, 2: 2, 4: 3}
        GAIN_OF = [0, 4, 1, 5, 2, 6, 3, 7]

        block = ctx.enter_context(nc.Block())

        @block.sync
        def _(sp):
            for b in range(B):
                sp.dma_start(x[:, b, :, :], a["x"][b].rearrange("(t p) d -> p t d", p=P)).then_inc(loaded["x"], 16)
            sp.dma_start(ctx_t[:, :], a["ctx_t"]).then_inc(loaded["ctx_t"], 16)
            sp.dma_start(packs["attn0"][:, :], a["attn0"]).then_inc(loaded["attn0"], 16)
            sp.dma_start(cols[:, :], a["cols"]).then_inc(loaded["cols"], 16)
            sp.dma_start(rows[:, :], a["rows"].broadcast_to([P, rows_n])).then_inc(loaded["rows"], 16)
            sp.dma_start(consts[:, :], a["consts"]).then_inc(loaded["consts"], 16)
            sp.dma_start(halves[:, :], a["halves"].bitcast(BF16)).then_inc(loaded["halves"], 16)
            sp.dma_start(mask_i, a["mask"].rearrange("b o (t p) k -> p b (o t) k", p=P)).then_inc(loaded["mask"], 16)
            sp.dma_start(rounded_in[:, 0:rounded_n], a["rounded"].bitcast(BF16)).then_inc(loaded["rounded"], 16)
            sp.dma_start(packs["attn1"][:, :], a["attn1"]).then_inc(loaded["attn1"], 16)
            sp.dma_start(packs["attn2"][:, :], a["attn2"]).then_inc(loaded["attn2"], 16)
            sp.dma_start(packs["ffn0"][:, :], a["ffn0"]).then_inc(loaded["ffn0"], 16)
            sp.dma_start(ctx_rows[:, :, :], a["ctx_rows"].rearrange("b k d -> k b d")).then_inc(loaded["ctx_rows"], 16)
            sp.dma_start(packs["attn3"][:, :], a["attn3"]).then_inc(loaded["attn3"], 16)
            sp.dma_start(packs["ffn1"][:, :], a["ffn1"]).then_inc(loaded["ffn1"], 16)
            for b in range(B):
                sp.wait_ge(*banks.full("y", 3, b))
            sp.dma_start(packs["ffn2"][:, :], a["ffn2"]).then_inc(loaded["ffn2"], 16)
            for b in range(B):
                sp.wait_ge(x_final[b], 1)
                sp.dma_start(out[b].rearrange("(t p) d -> p t d", p=P), x[:, b, :, :]).then_inc(stored, 16)
            sp.wait_ge(stored, 16 * B)

        def spread_keys(engine, b, layer, k_part, keys):
            for part, r in enumerate(PART_ROWS):
                groups = slice(part * LANES, min(GROUPS, (part + 1) * LANES))
                n = groups.stop - groups.start
                engine.tensor_tensor(
                    keys[0:r, b, groups, 0:GK].rearrange("p g (h k) -> p g h k", h=G3),
                    k_part[0:r, layer, part, b, :].bitcast(F32).unsqueeze(1).unsqueeze(1).broadcast_to([r, n, G3, CTX]),
                    const("head_mask").rearrange("p (g h) -> p g h", h=G3)[0:r, groups, :].unsqueeze(3)
                    .broadcast_to([r, n, G3, CTX]), ALU.mult).then_inc(keys_ready[b], 1)

        @block.gpsimd
        def _(pool):
            G = nc.gpsimd
            steps = [0]

            def link(ins):
                steps[0] += 1
                ins.then_inc(pool_step, 1)
                pool.wait_ge(pool_step, steps[0])

            def norm(b, stage):
                pool.wait_ge(var_ready[b], stage + 1)
                link(G.tensor_scalar(nw[:, b, 0, :], mv[:, b, :, 1], LN_EPS, None, ALU.add))
                G.tensor_tensor(nw[:, b, 2, :], nw[:, b, 0, :], minus_half[:, :], ALU.pow)\
                 .then_inc(xn_rstd_ready[b], 1)

            def add_bias(b, stage):
                if stage in BIASED:
                    if stage == 0:
                        pool.wait_ge(gbias_ready, 1)
                    pool.wait_ge(xn_ready[b], stage + 1)
                    G.tensor_tensor(x[:, b, :, :], x[:, b, :, :],
                                    gbias[:, BIASED[stage]:BIASED[stage] + 1, :].broadcast_to([P, T, D]),
                                    ALU.add).then_inc(bias_added[b], 1)

            def keys_in(b, layer):
                if layer == 0:
                    pool.wait_ge(loaded["consts"], 16)
                    pool.wait_ge(k_parts, 1)
                    for i in range(B):
                        spread_keys(G, i, 0, k_lo, keys_lo)

            def query(b, layer):
                add_bias(b, 2 * layer)
                if b == 0 and layer == 0:
                    G.memset(v_cols[:, :, :, :, :], 0.0)
                    G.memset(comb_t[:, :, :].bitcast(F32), 0.0)
                    G.memset(nothot_t[:, :, :], 0.0).then_inc(zeros_made, 1)

            def hidden0(b, m):
                if m == 0:
                    add_bias(b, 1)

            def maxima(b, layer, u):
                if u == 0:
                    pool.wait_ge(q_parts[b], layer + 1)
                    for part, r in enumerate(PART_ROWS):
                        last = G.tensor_tensor(q_lo[0:r, b, part, :], q[0:r, b, part, :],
                                               q_hi[0:r, b, part, :].bitcast(F32), ALU.subtract)
                    last.then_inc(q_lo_ready[b], 1)

            def project(b, stage, layer):
                if layer < 2:
                    pool.wait_ge(k_parts, layer + 2)
                    pool.wait_ge(*banks.full("p", layer, b, *SETS[-1][-1]))
                    spread_keys(G, b, layer + 1, k_hi, keys_hi)
                    spread_keys(G, b, layer + 1, k_lo, keys_lo)

            def square(b, it):
                pool.wait_ge(*banks.emptied("ss", it, b))
                G.tensor_tensor(nw[:, b, 2, :], nw[:, b, 0, :], minus_half[:, :], ALU.pow)\
                 .then_inc(rstd_ready[b], 1)

            G.memset(ones[:, 0:1], 1.0)
            G.memset(ones[:, 1:2], 1.0 / D)
            G.memset(keys_hi[:, :, :, GK:GKE].bitcast(F32), 0.0)
            G.memset(mx_raw[:, :, :, :, :], 0.0)
            G.memset(mx[:, :, :, :, :], 0.0)
            G.memset(minus_half[:, :], -0.5).then_inc(consts_made, 1)
            pool.wait_ge(consts_made, 1)
            mine = {"norm": norm, "keys_in": keys_in, "query": query, "hidden0": hidden0, "maxima": maxima,
                    "project": project, "square": square}
            for phase, b, args in SCHEDULE:
                if phase in mine:
                    mine[phase](b, *args)

        @block.tensor
        def _(pe):
            def start_unit(*name):
                if banks.reused(*name):
                    pe.wait_ge(*banks.free(*name))
                return banks.bank(*name)

            def mm(out_, lhs, rhs, start=True, stop=True, **kw):
                return nc.tensor.matmul(out_, lhs, rhs, start=start, stop=stop, **kw)

            def keys_in(b, layer):
                pe.wait_ge(loaded[f"attn{layer}"], 16)
                if layer == 0:
                    pe.wait_ge(loaded["ctx_t"], 16)
                wk = w(f"attn{layer}", "wk" if layer else "wq")
                bk = start_unit("k", layer)
                for part, r in enumerate(PART_ROWS):
                    last = mm(bk[0:r, part * B * CTX:(part + 1) * B * CTX], wk[:, part * P:part * P + r], ctx_t[:, :])
                last.then_inc(filled, 1)

            def values_in(b, layer):
                bk = start_unit("v", layer)
                for i in range(B):
                    last = mm(bk[0:CTX, i * D:(i + 1) * D], ctx_t[:, i * CTX:(i + 1) * CTX], w(f"attn{layer}", "wv"))
                last.then_inc(filled, 1)

            def place(b, layer):
                if layer == 0:
                    pe.wait_ge(loaded["halves"], 16)
                pe.wait_ge(v_parts_ready, layer + 1)
                for j in range(NJ):
                    bk = start_unit("vrows", layer, j)
                    for part in range(3):
                        last = mm(bk[:, 0:B * D], key_of[:, j * P:(j + 1) * P],
                                  v_parts[:, part, layer, :, :].rearrange("p b e -> p (b e)"),
                                  start=part == 0, stop=part == 2)
                    last.then_inc(filled, 1)

            def masks(b):
                for i in range(B):
                    bk = start_unit("mask_t", i)
                    pe.wait_ge(mask_b_ready, i + 1)
                    for t in range(T):
                        last = nc.tensor.transpose(bk[0:CTX, t * P:(t + 1) * P], mask_b[:, i, t, :], ident)
                    last.then_inc(filled, 1)

            def slots_in(b, i):
                if i == 1:
                    bk = start_unit("pn_t")
                    pe.wait_ge(pn_ready, 1)
                    for i in range(B):
                        last = nc.tensor.transpose(bk[:, i * CTX:(i + 1) * CTX], pn[:, i, :], ident[0:CTX, 0:CTX])
                    last.then_inc(filled, 1)
                elif i == 2:
                    pe.wait_ge(loaded["attn3"], 16)
                    pe.wait_ge(*banks.emptied("pn_t"))
                    for name, weights in (("kproj", "wk"), ("vproj", "wv")):
                        bk = start_unit(name)
                        mm(bk[:, 0:B * CTX], w("attn3", weights), pn_t[:, :]).then_inc(filled, 1)
                elif i == 3:
                    bk = start_unit("kq")
                    pe.wait_ge(*banks.emptied("kproj"))
                    mm(bk[:, 0:B * CTX], w("attn3", "wq"), kproj[:, :]).then_inc(filled, 1)
                    for i in range(B):
                        bk = start_unit("vw", i)
                        pe.wait_ge(*banks.emptied("vproj"))
                        mm(bk[0:CTX, 0:3 * D], vproj[:, i * CTX:(i + 1) * CTX], w("attn3", "wi")).then_inc(filled, 1)
                elif i == 4:
                    bk = start_unit("rq_t")
                    pe.wait_ge(rq_ready, 1)
                    nc.tensor.transpose(bk[:, 0:D], rq[:, :], ident).then_inc(filled, 1)
                    bk = start_unit("rscale")
                    mm(bk[:, 0:D], rscale[:, 1:2].broadcast_to([P, P]), ident).then_inc(filled, 1)

            def turn(b, stage):
                bk = start_unit("xn_t", stage, b)
                pe.wait_ge(xn_ready[b], stage + 1)
                if stage == 0:
                    pe.wait_ge(loaded["consts"], 16)
                    pe.wait_ge(consts_made, 1)
                for t in range(T):
                    last = nc.tensor.transpose(bk[:, t * P:(t + 1) * P], (y if stage == 7 else xn)[:, b, t, :], ident)
                last.then_inc(filled, 1)

            def query(b, layer):
                for part, r in enumerate(PART_ROWS):
                    bk = start_unit("q", layer, b, part)
                    pe.wait_ge(*banks.emptied("xn_t", 2 * layer, b))
                    mm(bk[0:r, :], w(f"attn{layer}", "wq")[:, part * P:part * P + r], xn_t[:, b, :]).then_inc(filled, 1)

            def maxima(b, layer, u):
                if u == 0:
                    pe.wait_ge(keys_ready[b], 4 * (layer + 1))
                    pe.wait_ge(q_parts[b], layer + 1)
                for lanes in (range(LANES), range(LANES, GROUPS)):
                    bks = {g: start_unit("max", layer, b, u, g) for g in lanes}
                    for i in range(2):
                        t = 2 * u + i
                        for g in lanes:
                            part = g // LANES
                            r = PART_ROWS[part]
                            n = HEADS[g] * CTX
                            n += n % 2
                            last = mm(bks[g][:, i * GKE:i * GKE + n], q_hi[0:r, b, part, t * P:(t + 1) * P],
                                      keys_hi[0:r, b, g, 0:n], stop=layer > 0)
                            if i == 1 and layer > 0:
                                last.then_inc(filled, 1)
                        if layer == 0:
                            for g in lanes:
                                last = mm(bks[g][:, i * GKE:i * GKE + HEADS[g] * CTX].rearrange("p (h k) -> p h k", k=CTX),
                                          ident16[:, :],
                                          mask_b16[:, b, t, :].unsqueeze(1).broadcast_to([P, HEADS[g], CTX]), start=False)
                                if i == 1:
                                    last.then_inc(filled, 1)

            def max_rows(b, layer):
                for part, r in enumerate(PART_ROWS):
                    bk = start_unit("max_t", layer, b, part)
                    pe.wait_ge(max_ready[b], layer + 1)
                    for t in range(T):
                        last = nc.tensor.transpose(
                            bk[0:r, t * P:(t + 1) * P],
                            mx[:, b, t, :, :].rearrange("p g e -> p (g e)")[:, part * P:part * P + r], ident)
                    last.then_inc(filled, 1)

            def scores(b, layer, i):
                if i == 0:
                    pe.wait_ge(q_lo_ready[b], layer + 1)
                if i in (0, 2):
                    pe.wait_ge(*banks.emptied("max_t", layer, b, i // 2))
                if i == 0 and layer == 0:
                    pe.wait_ge(*banks.emptied("mask_t", b))
                    if b == 1:
                        pe.wait_ge(k_parts, 3)
                        pe.wait_ge(rounded_ready, 1)
                for g, j in SETS[i]:
                    bk = start_unit("p", layer, b, g, j)
                    part, r = g // LANES, ROWS[g, j]
                    k = PART_ROWS[part]
                    for n, (keys, queries) in enumerate(((keys_hi, q_lo), (keys_hi, q_hi), (keys_lo, q_hi))):
                        last = mm(bk[0:r, :], keys[0:k, b, g, j * P:j * P + r], queries[0:k, b, part, :], start=n == 0,
                                  stop=n == 2 and layer > 0)
                    if layer == 0:
                        last = mm(bk[0:r, :], key_of[:, j * P:j * P + r], mask_t[:, b, :], start=False)
                    last.then_inc(filled, 1)

            def values(b, layer, part):
                bk = start_unit("pv", layer, b, part)
                if part == 0:
                    pe.wait_ge(sums_placed, 1)
                    pe.wait_ge(*banks.emptied("vrows", layer, NJ - 1))
                    pe.wait_ge(*banks.emptied("p", layer, b, *SETS[1][-1]))
                else:
                    pe.wait_ge(*banks.emptied("p", layer, b, *SETS[2][-1]))
                for j in range(NJ):
                    for g in range(part * LANES, min(GROUPS, (part + 1) * LANES)):
                        if (g, j) in ROWS:
                            r = ROWS[g, j]
                            at_ = g % LANES * GR
                            last = mm(bk[at_:at_ + GR, :], v_cols[0:r, j, B * layer + b, g, :],
                                      wide[0:r, b, SLOT[g, j], :], start=j == 0, stop=(g, j + 1) not in ROWS)
                last.then_inc(filled, 1)

            def values_back(b, layer, u):
                bk = start_unit("o", layer, b, u)
                pe.wait_ge(*banks.emptied("pv", layer, b, 1))
                for i in range(2):
                    t = 2 * u + i
                    for part, r in enumerate(PART_ROWS):
                        at_ = i * GROUPS * GR + part * P
                        last = nc.tensor.transpose(bk[:, at_:at_ + r], q[0:r, b, part, t * P:(t + 1) * P],
                                                   ident[0:r, 0:r])
                last.then_inc(filled, 1)

            def out_turn(b, layer):
                bk = start_unit("o_t", layer, b)
                pe.wait_ge(*banks.emptied("o", layer, b, T // 2 - 1))
                for t in range(T):
                    last = nc.tensor.transpose(bk[:, t * P:(t + 1) * P], o[:, b, t, 0:D], ident)
                last.then_inc(filled, 1)

            def project(b, stage, layer):
                bk = start_unit("out", stage, b)
                pe.wait_ge(*banks.emptied("o_t", layer, b))
                for t in range(T):
                    last = mm(bk[:, t * P:(t + 1) * P], o_t[:, b, t * P:(t + 1) * P], w(f"attn{layer}", "wo"))
                last.then_inc(filled, 1)

            def sum_chunks(bk, b, weights, chunks, stop=True):
                for i, (at_, n) in enumerate(chunks):
                    last = mm(bk, weights[0:n, i * D:(i + 1) * D], wide[0:n, b, at_, :], start=i == 0,
                              stop=stop and i == len(chunks) - 1)
                return last

            def back(b, stage):
                pairs = [("s_out", ("s_y", b), s_y_t)] if stage == 3 else []
                for name, source, tile in pairs + [("out", ("y", stage, b), y_t)]:
                    bk = start_unit(name, *([stage] if name == "out" else []), b)
                    pe.wait_ge(*banks.emptied(*source))
                    for t in range(T):
                        last = nc.tensor.transpose(bk[:, t * P:(t + 1) * P], tile[:, b, t * P:(t + 1) * P], ident)
                    last.then_inc(filled, 1)

            def hidden0(b, m):
                bk = start_unit("h0", b, m)
                if m == 0:
                    pe.wait_ge(loaded["ffn0"], 16)
                    pe.wait_ge(*banks.emptied("xn_t", 1, b))
                mm(bk, w("ffn0", "w1")[:, m * P:(m + 1) * P], xn_t[:, b, :]).then_inc(filled, 1)

            def down0(b):
                bk = start_unit("y", 1, b)
                pe.wait_ge(*banks.emptied("h0", b, C0 - 1))
                pe.wait_ge(*banks.emptied("h0", b, C0 - 2))
                sum_chunks(bk, b, w("ffn0", "w2"), [(m, P) for m in range(C0)]).then_inc(filled, 1)

            def gates1(b):
                bk = start_unit("gates1", b)
                pe.wait_ge(loaded["ffn1"], 16)
                pe.wait_ge(*banks.emptied("xn_t", 3, b))
                for t in range(T):
                    last = mm(bk[:, t * (E1 + 1):(t + 1) * (E1 + 1)], xn_t[:, b, t * P:(t + 1) * P],
                              w("ffn1", "gates"))
                last.then_inc(filled, 1)

            def shared(b, i):
                lo, n = SHC[i]
                for name in ("s_g", "s_u"):
                    bk = start_unit(name, b, i)
                    mm(bk[0:n, :], w("ffn1", name)[:, lo:lo + n], xn_t[:, b, :]).then_inc(filled, 1)

            def weights_turn(b):
                bk = start_unit("comb_t", b)
                pe.wait_ge(comb_ready[b], 1)
                for t in range(T):
                    last = nc.tensor.transpose(bk[0:2 * E1, t * P:(t + 1) * P], comb[:, b, t, :].bitcast(F32), ident)
                last.then_inc(filled, 1)

            def experts(b, c):
                for name, weights in (("e_g", "w_g"), ("e_u", "w_u")):
                    bk = start_unit(name, b, c)
                    mm(bk, w("ffn1", weights)[:, c * P:(c + 1) * P], xn_t[:, b, :]).then_inc(filled, 1)
                bk = start_unit("e_w", b, c)
                if c == 0:
                    pe.wait_ge(rounded_ready, 1)
                    pe.wait_ge(zeros_made, 1)
                    pe.wait_ge(*banks.emptied("comb_t", b))
                mm(bk, sel1[:, c * P:(c + 1) * P], comb_t[:, b, :]).then_inc(filled, 1)

            def down1(b):
                bk = start_unit("s_y", b)
                pe.wait_ge(*banks.emptied("s_u", b, len(SHC) - 1))
                sum_chunks(bk, b, w("ffn1", "s_down"), [(C1 + i, n) for i, (_, n) in enumerate(SHC)])\
                    .then_inc(filled, 1)
                bk = start_unit("y", 3, b)
                pe.wait_ge(*banks.emptied("e_w", b, C1 - 1))
                sum_chunks(bk, b, w("ffn1", "w_down"), [(c, P) for c in range(C1)]).then_inc(filled, 1)

            def router(b):
                bk = start_unit("router", b)
                pe.wait_ge(loaded["ffn2"], 16)
                pe.wait_ge(*banks.emptied("xn_t", 5, b))
                for t in range(T):
                    last = mm(bk[:, t * E2:(t + 1) * E2], xn_t[:, b, t * P:(t + 1) * P], w("ffn2", "router"))
                last.then_inc(filled, 1)

            def choice_turn(b):
                bk = start_unit("hot_t", b)
                pe.wait_ge(hot_ready[b], 1)
                for t in range(T):
                    last = nc.tensor.transpose(bk[0:E2, t * P:(t + 1) * P], route[:, b, 3, t, :], ident)
                last.then_inc(filled, 1)

            def hidden2(b, c):
                bk = start_unit("h2", b, c)
                mm(bk, w("ffn2", "w1")[:, c * P:(c + 1) * P], xn_t[:, b, :], stop=False)
                if c == 0:
                    pe.wait_ge(nothot_ready[b], 1)
                mm(bk, sel2[:, c * P:(c + 1) * P], nothot_t[:, b, :], start=False).then_inc(filled, 1)

            def down2(b):
                bk = start_unit("y", 5, b)
                pe.wait_ge(*banks.emptied("h2", b, C2 - 1))
                pe.wait_ge(*banks.emptied("h2", b, C2 - 2))
                sum_chunks(bk, b, w("ffn2", "w2"), [(c, P) for c in range(C2)], stop=False)
                mm(bk, w("ffn2", "bias2")[0:E2, :], hot_t[:, b, :], start=False).then_inc(filled, 1)

            def square(b, it):
                bk = start_unit("ss", it, b)
                pe.wait_ge(sq_ready[b], it + 1)
                for t in range(T):
                    last = mm(bk[:, t:t + 1], sq[:, b, t * P:(t + 1) * P], ones[:, 1:2])
                last.then_inc(filled, 1)

            def hidden_gate(b, it, name):
                i = {"r": 0, "z": 1, "hn": 2}[name]
                bk = start_unit(name, it, b)
                if it == 0:
                    pe.wait_ge(*banks.emptied("xn_t", 6, b))
                else:
                    pe.wait_ge(slots_ready[b], it)
                last = mm(bk, w("attn3", "wh")[:, i * D:(i + 1) * D], slots_t[:, b, :], stop=name == "hn")
                if name == "hn":
                    last.then_inc(filled, 1)

            def slot_products(b, it):
                bk = start_unit("s", it, b)
                if it == 0:
                    pe.wait_ge(*banks.emptied("kq"))
                mm(bk[0:CTX, :], kq[:, b * CTX:(b + 1) * CTX], slots_t[:, b, :]).then_inc(filled, 1)

            def slot_scores(b, it):
                bk = start_unit("rstd_b", it, b)
                pe.wait_ge(rstd_ready[b], it + 1)
                for t in range(T):
                    last = mm(bk[0:CTX, t * P:(t + 1) * P], nw[:, b, 2, t:t + 1].broadcast_to([P, CTX]), ident)
                last.then_inc(filled, 1)

            def slot_sums(b, it):
                bk = start_unit("asum", it, b)
                pe.wait_ge(at_ready[b], it + 1)
                for t in range(T):
                    last = mm(bk[:, t:t + 1], ex[0:CTX, b, t * P:(t + 1) * P], nmax[:, b, 2:3])
                last.then_inc(filled, 1)

            def slot_weights(b, it):
                bk = start_unit("ra_b", it, b)
                pe.wait_ge(ra_ready[b], it + 1)
                for t in range(T):
                    last = mm(bk[0:CTX, t * P:(t + 1) * P], route_s[:, b, 1, t:t + 1].broadcast_to([P, CTX]), ident)
                last.then_inc(filled, 1)

            def gru(b, it):
                update = lambda i: (vw[:, b, i * D:(i + 1) * D], an[0:CTX, b, :])
                if it == 0:
                    pe.wait_ge(*banks.emptied("vw", B - 1))
                pe.wait_ge(*banks.emptied("ra_b", it, b))
                mm(banks.bank("r", it, b), *update(0), start=False).then_inc(filled, 1)
                mm(banks.bank("z", it, b), *update(1), start=False).then_inc(filled, 1)
                bk = start_unit("n", it, b)
                mm(bk, *update(2)).then_inc(filled, 1)

            def slots_back(b):
                bk = start_unit("out", 6, b)
                pe.wait_ge(slots_ready[b], ITERS)
                for t in range(T):
                    last = nc.tensor.transpose(bk[:, t * P:(t + 1) * P], slots_t[:, b, t * P:(t + 1) * P], ident)
                last.then_inc(filled, 1)

            def quantised(b):
                bk = start_unit("out", 7, b)
                pe.wait_ge(*banks.emptied("rq_t"))
                pe.wait_ge(*banks.emptied("xn_t", 7, b))
                for t in range(T):
                    last = mm(bk[:, t * P:(t + 1) * P], lhs_q[:, b, t * P:(t + 1) * P], rhs_q[:, :])
                last.then_inc(filled, 1)

            mine = {"keys_in": keys_in, "values_in": values_in, "place": place, "masks": masks, "slots_in": slots_in,
                    "turn": turn, "query": query, "maxima": maxima, "max_rows": max_rows, "scores": scores, "values": values,
                    "values_back": values_back, "out_turn": out_turn, "project": project, "hidden0": hidden0, "down0": down0, "back": back,
                    "gates1": gates1, "shared": shared, "weights_turn": weights_turn, "experts": experts,
                    "down1": down1, "router": router, "choice_turn": choice_turn, "hidden2": hidden2,
                    "down2": down2, "hidden_gate": hidden_gate, "slot_products": slot_products, "square": square,
                    "slot_scores": slot_scores, "slot_sums": slot_sums,
                    "slot_weights": slot_weights, "gru": gru, "slots_back": slots_back, "quantised": quantised}
            for phase, b, args in SCHEDULE:
                if phase in mine:
                    mine[phase](b, *args)

        @block.scalar
        def _(act):
            A = nc.scalar
            steps = [0]

            def link(ins):
                steps[0] += 1
                ins.then_inc(act_step, 1)
                act.wait_ge(act_step, steps[0])

            def empty(dst, fn, name, rows_=P, cols_=512, **kw):
                act.wait_ge(*banks.full(*name))
                A.activation(dst, banks.bank(*name)[0:rows_, 0:cols_], fn, **kw).then_inc(drained["act"], 1)

            def keys_out(layer):
                act.wait_ge(*banks.full("k", layer))
                for part, r in enumerate(PART_ROWS):
                    last = A.activation(k_t[0:r, layer, part, :, :].rearrange("p b k -> p (b k)"),
                                        banks.bank("k", layer)[0:r, part * B * CTX:(part + 1) * B * CTX],
                                        ACT.Identity, bias=col(f"bk{layer}", part)[0:r, :])
                last.then_inc(drained["act"], 1)

            def round_(name, dst):
                lo, hi = rounded_at[name]
                A.activation(dst[:, :], rounded_in[:, lo:hi], ACT.Copy).then_inc(rounded_ready, 1)

            def keys_in(b, layer):
                if layer == 0:
                    act.wait_ge(loaded["cols"], 16)
                keys_out(layer)
                if layer == 0:
                    act.wait_ge(loaded["rows"], 16)
                    A.activation(gain[:, :], row("g"), ACT.Tanh).then_inc(gain_ready, 1)

            def masks(b):
                for i in range(B):
                    empty(mask_t[:, i, :], ACT.Copy, ("mask_t", i), CTX)
                act.wait_ge(loaded["rounded"], 16)
                round_("sel1", sel1)

            def slots_in(b, i):
                if i == 0:
                    for i in range(2):
                        A.activation(half_bias[:, i:i + 1], col("bi", i), ACT.Identity, bias=col("bh", i))
                    link(A.activation(half_bias[:, 2:3], col("bh", 2), ACT.Identity, scale=0.5))
                    link(A.activation(half_bias[:, 0:2], half_bias[:, 0:2], ACT.Identity, scale=0.5))
                    act.wait_ge(loaded["ctx_rows"], 16)
                    for i in range(B):
                        last = A.activation(pn[:, i, :], ctx_rows[:, i, :], ACT.Square, accum_out=p_ss[:, i:i + 1])
                    last.then_inc(p_ss_ready, 1)
                elif i == 1:
                    empty(pn_t[:, :], ACT.Copy, ("pn_t",), cols_=B * CTX, scale=col("w_in"))
                elif i == 2:
                    empty(kproj[:, :], ACT.Copy, ("kproj",), cols_=B * CTX)
                    empty(vproj[:, :], ACT.Copy, ("vproj",), cols_=B * CTX)
                elif i == 3:
                    for i in range(B):
                        empty(vw[:, i, :], ACT.Copy, ("vw", i), CTX, 3 * D)
                else:
                    empty(rscale_b[:, :], ACT.Copy, ("rscale",), cols_=D)

            def turn(b, stage):
                if stage < 7:
                    empty((slots_t if stage == 6 else xn_t)[:, b, :], ACT.Copy, ("xn_t", stage, b))

            def query(b, layer):
                for part, r in enumerate(PART_ROWS):
                    empty(q[0:r, b, part, :], ACT.Identity, ("q", layer, b, part), r,
                          bias=col(f"bq{layer}", part)[0:r, :])

            def scores(b, layer, i):
                for g, j in SETS[i]:
                    r = ROWS[g, j]
                    empty(wide[0:r, b, SLOT[g, j], :], ACT.Exp, ("p", layer, b, g, j), r, scale=DH ** -0.5)

            def values(b, layer, part):
                r = PART_ROWS[part]
                empty(q[0:r, b, part, :], ACT.Copy, ("pv", layer, b, part), r)

            def out_turn(b, layer):
                empty(o_t[:, b, :], ACT.Copy, ("o_t", layer, b))

            def hidden0(b, m):
                if m % 2:
                    empty(wide[:, b, m, :], ACT.Relu, ("h0", b, m), bias=col("b1", m))

            def down0(b):
                empty(y_t[:, b, :], ACT.Copy, ("y", 1, b))

            def gates1(b):
                act.wait_ge(gap_ready[b], 1)
                A.activation(route_s[:, b, 4, :], route_s[:, b, 3, :], ACT.Exp)
                A.activation(route_s[:, b, 7, :], lg[:, b, :, E1], ACT.Tanh, scale=0.5).then_inc(second_ready[b], 1)

            users = [[] for _ in range(B)]

            def silu(b, r, source, user):
                if len(users[b]) >= 2:
                    act.wait_ge(*banks.emptied(*users[b][-2]))
                empty(act_s[len(users[b]) % 2][0:r, b, :], ACT.Silu, source, r)
                users[b].append(user)

            def shared(b, i):
                silu(b, SHC[i][1], ("s_g", b, i), ("s_u", b, i))

            def experts(b, c):
                silu(b, P, ("e_g", b, c), ("e_u", b, c))

            def weights_turn(b):
                empty(comb_t[0:2 * E1, b, :], ACT.Copy, ("comb_t", b), 2 * E1)

            def down1(b):
                empty(s_y_t[:, b, :], ACT.Copy, ("s_y", b))
                empty(y_t[:, b, :], ACT.Copy, ("y", 3, b))

            def choice_turn(b):
                empty(hot_t[:, b, :], ACT.Copy, ("hot_t", b), E2)

            def hidden2(b, c):
                if c % 2:
                    empty(wide[:, b, c, :], ACT.Relu, ("h2", b, c), bias=col("bias1", c))

            def down2(b):
                empty(y_t[:, b, :], ACT.Relu, ("y", 5, b))

            def square(b, it):
                if it == 0:
                    act.wait_ge(*banks.emptied("xn_t", 6, b))
                else:
                    act.wait_ge(slots_ready[b], it)
                A.activation(sq[:, b, :], slots_t[:, b, :], ACT.Square).then_inc(sq_ready[b], 1)

            def slot_products(b, it):
                empty(ss[0:CTX, b, :], ACT.Copy, ("s", it, b), CTX)

            def slot_scores(b, it):
                act.wait_ge(nmax_ready[b], it + 1)
                A.activation(ex[0:CTX, b, :], sc[0:CTX, b, :], ACT.Exp, bias=nmax[:, b, 0:1],
                             accum_out=nmax[:, b, 1:2]).then_inc(ex_ready[b], 1)

            def hidden_gate(b, it, name):
                if name == "hn":
                    empty(hnb[:, b, :], ACT.Identity, ("hn", it, b), bias=half_bias[:, 2:3], scale=0.5)

            def gru(b, it):
                empty(tr[:, b, :], ACT.Tanh, ("r", it, b), bias=half_bias[:, 0:1], scale=0.5)
                empty(tz[:, b, :], ACT.Tanh, ("z", it, b), bias=half_bias[:, 1:2], scale=0.5)

            def gru_end(b, it):
                act.wait_ge(*banks.emptied("n", it, b))
                A.activation(nn[:, b, :], tt[:, b, :], ACT.Tanh, bias=col("bi", 2)).then_inc(n_ready[b], 1)

            mine = {"keys_in": keys_in, "masks": masks, "slots_in": slots_in, "turn": turn,
                    "query": query, "scores": scores, "values": values, "out_turn": out_turn,
                    "hidden0": hidden0, "down0": down0, "gates1": gates1, "shared": shared,
                    "weights_turn": weights_turn, "experts": experts, "down1": down1, "choice_turn": choice_turn,
                    "hidden2": hidden2, "down2": down2, "square": square, "slot_scores": slot_scores, "gru": gru,
                    "hidden_gate": hidden_gate, "slot_products": slot_products, "gru_end": gru_end}
            for phase, b, args in SCHEDULE:
                if phase in mine:
                    mine[phase](b, *args)

        @block.vector
        def _(dve):
            V = nc.vector
            steps = [0]

            def link(ins):
                steps[0] += 1
                ins.then_inc(dve_step, 1)
                dve.wait_ge(dve_step, steps[0])

            def norm(b, stage):
                if stage == 0:
                    dve.wait_ge(loaded["x"], 16 * B)
                for t in range(T):
                    last = V.bn_stats(stats[:, b, t, :], x[:, b, t, :])
                link(last)
                for t in range(T):
                    last = V.bn_aggr(mv[:, b, t, :], stats[:, b, t, :])
                last.then_inc(var_ready[b], 1)

            def norm_end(b, stage):
                dve.wait_ge(xn_rstd_ready[b], stage + 1)
                for t in range(T):
                    last = V.tensor_scalar(xn[:, b, t, :], x[:, b, t, :], mv[:, b, t, 0:1], nw[:, b, 2, t:t + 1],
                                           ALU.subtract, ALU.mult)
                if stage < 7:
                    last.then_inc(xn_ready[b], 1)
                    return
                link(last)
                amax, scale, inverse = (route_s[:, b, i, :] for i in (2, 3, 4))
                link(V.tensor_reduce(amax, xn[:, b, :, :], AX.X, ALU.max, apply_absolute_value=True))
                link(V.tensor_scalar(scale, amax, 1e-12, 1.0 / 127.0, ALU.max, ALU.mult))
                link(V.reciprocal(inverse, scale))
                for t in range(T):
                    last = V.tensor_scalar(y[:, b, t, :], xn[:, b, t, :], inverse[:, t:t + 1], ROUND, ALU.mult, ALU.add)
                link(last)
                V.tensor_scalar(y[:, b, :, :], y[:, b, :, :], ROUND, 127.0, ALU.subtract, ALU.min)\
                 .then_inc(xn_ready[b], 1)

            def flat(tile):
                return tile.rearrange("p t d -> p (t d)")

            def add_out(b, stage):
                dve.wait_ge(*banks.full("out", stage, b))
                if stage in BIASED:
                    dve.wait_ge(bias_added[b], BIASED[stage] + 1)
                g = GAIN_OF[stage]
                V.scalar_tensor_tensor(flat(x[:, b, :, :]), banks.bank("out", stage, b), gain[:, g:g + 1],
                                       flat(x[:, b, :, :]), ALU.mult, ALU.add).then_inc(drained["dve"], 1)
                dve.wait_ge(*banks.emptied("out", stage, b))

            def split_keys(layer):
                dve.wait_ge(*banks.emptied("k", layer))
                for part, r in enumerate(PART_ROWS):
                    last = V.tensor_copy(k_hi[0:r, layer, part, :, :], k_t[0:r, layer, part, :, :])
                link(last)
                for part, r in enumerate(PART_ROWS):
                    last = V.tensor_tensor(k_lo[0:r, layer, part, :, :], k_t[0:r, layer, part, :, :],
                                           k_hi[0:r, layer, part, :, :].bitcast(F32), ALU.subtract)
                last.then_inc(k_parts, 1)

            def keys_in(b, layer):
                split_keys(layer)
                if layer == 0:
                    dve.wait_ge(loaded["consts"], 16)
                    for i in range(B):
                        spread_keys(V, i, 0, k_hi, keys_hi)

            def masks(b):
                dve.wait_ge(loaded["mask"], 16)
                for i in range(B):
                    V.tensor_scalar(mask_b16[:, i, :, :], mask_i[:, i, :, :], 0.0, MASKED, ALU.is_equal, ALU.mult)
                    V.tensor_scalar(mask_b[:, i, :, :], mask_i[:, i, :, :], 0.0, MASKED, ALU.is_equal, ALU.mult)\
                     .then_inc(mask_b_ready, 1)
                dve.wait_ge(loaded["rows"], 16)
                dve.wait_ge(gain_ready, 1)
                for i, (name, stage) in enumerate((("bo0", 0), ("b2", 1), ("bo1", 2), ("bo2", 4))):
                    g = GAIN_OF[stage]
                    last = V.tensor_scalar(gbias[:, i, :], row(name), gain[:, g:g + 1], None, ALU.mult)
                last.then_inc(gbias_ready, 1)

            def values_in(b, layer):
                dve.wait_ge(*banks.full("v", layer))
                rest = v_rows[:, layer, :, :]
                V.tensor_tensor(rest, banks.bank("v", layer)[0:CTX, 0:B * D].rearrange("p (b d) -> p b d", b=B),
                                row(f"bv{layer}")[0:CTX, :].unsqueeze(1).broadcast_to([CTX, B, D]), ALU.add)\
                 .then_inc(drained["dve"], 1)
                dve.wait_ge(*banks.emptied("v", layer))
                for part in range(3):
                    piece = v_parts[:, part, layer, :, :]
                    if part == 2:
                        V.tensor_copy(piece, rest).then_inc(v_parts_ready, 1)
                    else:
                        link(V.tensor_copy(piece, rest))
                        link(V.tensor_tensor(rest, rest, piece, ALU.subtract))

            def place(b, layer):
                masks_ = const("chunk_mask").rearrange("p (j h) -> p j h", j=NJ)
                if layer == 0:
                    dve.wait_ge(zeros_made, 1)
                    for j in range(NJ):
                        V.tensor_copy(v_cols[:, j, :, 0:GROUPS - 1, VALUES:VALUES + G3],
                                      masks_[:, j:j + 1, :].unsqueeze(1).broadcast_to([P, 3 * B, GROUPS - 1, G3]))
                    V.tensor_copy(v_cols[:, 0, :, GROUPS - 1, VALUES:VALUES + G3],
                                  masks_[:, 0:1, 0:1].broadcast_to([P, 3 * B, G3])).then_inc(sums_placed, 1)
                at_ = B * layer
                for j in range(NJ):
                    dve.wait_ge(*banks.full("vrows", layer, j))
                    bk = banks.bank("vrows", layer, j)[:, 0:B * D].rearrange("p (b h d) -> p b h d", b=B, h=H)
                    for h in range(G3):
                        last = V.tensor_scalar(
                            v_cols[:, j, at_:at_ + B, 0:len(range(h, H, G3)), h * DH:(h + 1) * DH], bk[:, :, h::G3, :],
                            masks_[:, j, h:h + 1], None, ALU.mult)
                    last.then_inc(drained["dve"], 1)

            def slots_in(b, i):
                if i == 0:
                    dve.wait_ge(p_ss_ready, 1)
                    link(V.tensor_scalar(p_small[:, 0, :], p_ss[:, :], 1.0 / D, RMS_EPS, ALU.mult, ALU.add))
                    v, hv, r, t = (p_small[:, i, :] for i in range(4))
                    V.tensor_scalar(r.bitcast(I32), v.bitcast(I32), -0.5, 1597463007.0, ALU.mult, ALU.add)
                    link(V.tensor_scalar(hv, v, -0.5, None, ALU.mult))
                    for i in range(3):
                        link(V.tensor_tensor(t, r, r, ALU.mult))
                        link(V.tensor_tensor(t, t, hv, ALU.mult))
                        link(V.scalar_tensor_tensor(r, t, 1.5, r, ALU.add, ALU.mult))
                    for i in range(B):
                        last = V.tensor_scalar(pn[:, i, :], ctx_rows[:, i, :], p_small[:, 2, i:i + 1], None, ALU.mult)
                    last.then_inc(pn_ready, 1)
                elif i == 2:
                    dve.wait_ge(loaded["attn3"], 16)
                    link(V.tensor_reduce(rscale[:, 0:1], w("attn3", "rhs_t"), AX.X, ALU.max, apply_absolute_value=True))
                    link(V.tensor_scalar(rscale[:, 1:2], rscale[:, 0:1], 1e-12, 1.0 / 127.0, ALU.max, ALU.mult))
                    link(V.reciprocal(rscale[:, 2:3], rscale[:, 1:2]))
                    link(V.tensor_scalar(rq[:, :], w("attn3", "rhs_t"), rscale[:, 2:3], ROUND, ALU.mult, ALU.add))
                    V.tensor_scalar(rq[:, :], rq[:, :], ROUND, 127.0, ALU.subtract, ALU.min).then_inc(rq_ready, 1)
                elif i == 3:
                    dve.wait_ge(*banks.full("kq"))
                    V.tensor_scalar(kq[:, :], banks.bank("kq")[:, 0:B * CTX], col("w_slot"), D ** -0.5, ALU.mult,
                                    ALU.mult).then_inc(drained["dve"], 1)
                elif i == 4:
                    dve.wait_ge(*banks.full("rq_t"))
                    V.tensor_scalar(rhs_q[:, :], banks.bank("rq_t")[:, 0:D], -127.0, None, ALU.max)\
                     .then_inc(drained["dve"], 1)

            def query(b, layer):
                for part, r in enumerate(PART_ROWS):
                    dve.wait_ge(*banks.emptied("q", layer, b, part))
                    last = V.tensor_copy(q_hi[0:r, b, part, :], q[0:r, b, part, :])
                last.then_inc(q_parts[b], 1)

            def maxima(b, layer, u):
                if b == 0 and layer == 0 and u == 0:
                    dve.wait_ge(consts_made, 1)
                for g in range(GROUPS):
                    dve.wait_ge(*banks.full("max", layer, b, u, g))
                    n = HEADS[g]
                    V.tensor_reduce(mx_raw[:, b, 2 * u:2 * u + 2, g, 0:n],
                                    banks.bank("max", layer, b, u, g)[:, 0:2 * GKE]
                                    .rearrange("p (t k) -> p t k", t=2)[:, :, 0:n * CTX]
                                    .rearrange("p t (h k) -> p t h k", k=CTX), AX.X, ALU.max)\
                     .then_inc(drained["dve"], 1)

            def max_rows(b, layer):
                dve.wait_ge(*banks.emptied("max", layer, b, T // 2 - 1, GROUPS - 1))
                link(V.tensor_copy(mx_hi[:, b, :, :, :], mx_raw[:, b, :, :, :]))
                V.tensor_copy(mx[:, b, :, :, VALUES:VALUES + G3], mx_hi[:, b, :, :, :].bitcast(F32))
                V.tensor_tensor(mx[:, b, :, :, VALUES + G3:VALUES + 2 * G3], mx_raw[:, b, :, :, :],
                                mx_hi[:, b, :, :, :].bitcast(F32), ALU.subtract).then_inc(max_ready[b], 1)
                dve.wait_ge(q_lo_ready[b], layer + 1)
                for part, r in enumerate(PART_ROWS):
                    dve.wait_ge(*banks.full("max_t", layer, b, part))
                    V.tensor_tensor(q_hi[0:r, b, part, :], q_hi[0:r, b, part, :].bitcast(F32),
                                    banks.bank("max_t", layer, b, part)[0:r, :], ALU.add).then_inc(drained["dve"], 1)

            def values_back(b, layer, u):
                dve.wait_ge(*banks.full("o", layer, b, u))
                both = banks.bank("o", layer, b, u)[:, 0:2 * GROUPS * GR].rearrange("p (t g e) -> p t g e", t=2, e=GR)
                link(V.reciprocal(rsum[:, b, 2 * u:2 * u + 2, :, :], both[:, :, :, VALUES:VALUES + G3]))
                for i in range(2):
                    t = 2 * u + i
                    last = V.tensor_tensor(o[:, b, t, :].rearrange("p (g h d) -> p g h d", g=GROUPS, h=G3),
                                           both[:, i, :, 0:VALUES].rearrange("p g (h d) -> p g h d", h=G3),
                                           rsum[:, b, t, :, :].unsqueeze(3).broadcast_to([P, GROUPS, G3, DH]), ALU.mult)
                last.then_inc(drained["dve"], 1)

            def project(b, stage, layer):
                add_out(b, stage)

            def hidden0(b, m):
                if m % 2 == 0:
                    dve.wait_ge(*banks.full("h0", b, m))
                    V.tensor_scalar(wide[:, b, m, :], banks.bank("h0", b, m), col("b1", m), 0.0, ALU.add, ALU.max)\
                     .then_inc(drained["dve"], 1)

            def largest(b, logits, n, top, ids, rev):
                link(V.tensor_reduce(top, logits, AX.X, ALU.max))
                eq, order = route[:, b, 0, :, 0:n], route[:, b, 1, :, 0:n]
                first = route_s[:, b, 1, :]
                link(V.tensor_tensor(eq, logits, top.unsqueeze(2).broadcast_to([P, T, n]), ALU.is_equal))
                link(V.tensor_tensor(order, eq, rev, ALU.mult))
                link(V.tensor_reduce(first, order, AX.X, ALU.max))
                return V.tensor_tensor(ids, rev, first.unsqueeze(2).broadcast_to([P, T, n]), ALU.is_equal)

            def gates1(b):
                rev = const("rev16").unsqueeze(1).broadcast_to([P, T, E1])
                dve.wait_ge(*banks.full("gates1", b))
                V.tensor_copy(lg[:, b, :, 0:E1 + 1],
                              banks.bank("gates1", b)[:, 0:T * (E1 + 1)].rearrange("p (t e) -> p t e", t=T))\
                 .then_inc(drained["dve"], 1)
                dve.wait_ge(*banks.emptied("gates1", b))
                logits = lg[:, b, :, 0:E1]
                top, second, gap = (route_s[:, b, i, :] for i in (0, 2, 3))
                one, two, rest = (route[:, b, i, :, 0:E1] for i in (2, 3, 4))
                link(largest(b, logits, E1, top, one, rev))
                link(V.scalar_tensor_tensor(rest, one, -3e38, logits, ALU.mult, ALU.add))
                link(largest(b, rest, E1, second, two, rev))
                V.tensor_tensor(gap, second, top, ALU.subtract).then_inc(gap_ready[b], 1)

            def weights_turn(b):
                e2, w1_, w2_, shared_ = (route_s[:, b, i, :] for i in (4, 5, 6, 7))
                one, two, rest = (route[:, b, i, :, 0:E1] for i in (2, 3, 4))
                dve.wait_ge(second_ready[b], 1)
                link(V.tensor_scalar(w2_, e2, 1.0, None, ALU.add))
                link(V.reciprocal(w1_, w2_))
                link(V.tensor_tensor(w2_, e2, w1_, ALU.mult))
                V.tensor_tensor(one, one, w1_.unsqueeze(2).broadcast_to([P, T, E1]), ALU.mult)
                link(V.tensor_tensor(two, two, w2_.unsqueeze(2).broadcast_to([P, T, E1]), ALU.mult))
                link(V.tensor_tensor(rest, one, two, ALU.add))
                link(V.tensor_copy(comb[:, b, :, 0:E1], rest))
                V.tensor_tensor(comb[:, b, :, E1:2 * E1], rest, comb[:, b, :, 0:E1].bitcast(F32), ALU.subtract)\
                 .then_inc(comb_ready[b], 1)
                link(V.tensor_scalar(shared_, shared_, 0.5, 0.5, ALU.mult, ALU.add))
                link(V.tensor_scalar(shared_, shared_, gain[:, GAIN_OF[3]:GAIN_OF[3] + 1], None, ALU.mult))

            count = [0] * B

            def shared(b, i):
                r = SHC[i][1]
                dve.wait_ge(*banks.emptied("s_g", b, i))
                dve.wait_ge(*banks.full("s_u", b, i))
                V.tensor_tensor(wide[0:r, b, C1 + i, :], act_s[count[b] % 2][0:r, b, :], banks.bank("s_u", b, i)[0:r, :],
                                ALU.mult).then_inc(drained["dve"], 1)
                count[b] += 1

            def experts(b, c):
                slot = count[b] % 2
                dve.wait_ge(*banks.emptied("e_g", b, c))
                dve.wait_ge(*banks.full("e_u", b, c))
                V.tensor_tensor(wide[:, b, c, :], act_s[slot][:, b, :], banks.bank("e_u", b, c), ALU.mult)\
                 .then_inc(drained["dve"], 1)
                dve.wait_ge(*banks.emptied("e_u", b, c))
                dve.wait_ge(*banks.full("e_w", b, c))
                V.tensor_tensor(wide[:, b, c, :], wide[:, b, c, :], banks.bank("e_w", b, c), ALU.mult)\
                 .then_inc(drained["dve"], 1)
                count[b] += 1

            def back(b, stage):
                if stage == 3:
                    dve.wait_ge(*banks.full("s_out", b))
                    for t in range(T):
                        last = V.scalar_tensor_tensor(x[:, b, t, :], banks.bank("s_out", b)[:, t * P:(t + 1) * P],
                                                      route_s[:, b, 7, t:t + 1], x[:, b, t, :], ALU.mult, ALU.add)
                    last.then_inc(drained["dve"], 1)
                    dve.wait_ge(*banks.emptied("s_out", b))
                add_out(b, stage)

            def router(b):
                rev = const("rev32").unsqueeze(1).broadcast_to([P, T, E2])
                dve.wait_ge(*banks.full("router", b))
                V.tensor_tensor(lg[:, b, :, :], banks.bank("router", b)[:, 0:T * E2].rearrange("p (t e) -> p t e", t=T),
                                row("router_b").unsqueeze(1).broadcast_to([P, T, E2]), ALU.add)\
                 .then_inc(drained["dve"], 1)
                dve.wait_ge(*banks.emptied("router", b))
                largest(b, lg[:, b, :, :], E2, route_s[:, b, 0, :], route[:, b, 3, :, :], rev)\
                    .then_inc(hot_ready[b], 1)

            def choice_turn(b):
                dve.wait_ge(*banks.emptied("hot_t", b))
                V.tensor_scalar(nothot_t[0:E2, b, :], hot_t[:, b, :], 1.0, -MASKED, ALU.subtract, ALU.mult)\
                 .then_inc(nothot_ready[b], 1)

            def hidden2(b, c):
                if c % 2 == 0:
                    dve.wait_ge(*banks.full("h2", b, c))
                    V.tensor_scalar(wide[:, b, c, :], banks.bank("h2", b, c), col("bias1", c), 0.0, ALU.add, ALU.max)\
                     .then_inc(drained["dve"], 1)

            def square(b, it):
                dve.wait_ge(*banks.full("ss", it, b))
                V.tensor_scalar(nw[:, b, 0, :], banks.bank("ss", it, b)[:, 0:T], RMS_EPS, None, ALU.add)\
                 .then_inc(drained["dve"], 1)

            def slot_scores(b, it):
                dve.wait_ge(*banks.full("rstd_b", it, b))
                dve.wait_ge(*banks.emptied("s", it, b))
                V.tensor_tensor(sc[0:CTX, b, :], ss[0:CTX, b, :], banks.bank("rstd_b", it, b)[0:CTX, :], ALU.mult)\
                 .then_inc(drained["dve"], 1)
                dve.wait_ge(*banks.emptied("rstd_b", it, b))
                V.tensor_reduce(nmax[:, b, 0:1], sc[0:CTX, b, :], AX.X, ALU.max, negate=True)\
                 .then_inc(nmax_ready[b], 1)

            def slot_sums(b, it):
                dve.wait_ge(ex_ready[b], it + 1)
                V.reciprocal(nmax[:, b, 2:3], nmax[:, b, 1:2]).then_inc(at_ready[b], 1)
                dve.wait_ge(*banks.full("asum", it, b))
                V.tensor_scalar(route_s[:, b, 0, :], banks.bank("asum", it, b)[:, 0:T], RMS_EPS, None, ALU.add)\
                 .then_inc(drained["dve"], 1)
                dve.wait_ge(*banks.emptied("asum", it, b))
                V.reciprocal(route_s[:, b, 1, :], route_s[:, b, 0, :]).then_inc(ra_ready[b], 1)

            def slot_weights(b, it):
                dve.wait_ge(*banks.full("ra_b", it, b))
                V.scalar_tensor_tensor(an[0:CTX, b, :], ex[0:CTX, b, :], nmax[:, b, 2:3],
                                       banks.bank("ra_b", it, b)[0:CTX, :], ALU.mult, ALU.mult)\
                 .then_inc(drained["dve"], 1)

            def gru(b, it):
                dve.wait_ge(*banks.emptied("r", it, b))
                link(V.scalar_tensor_tensor(tt[:, b, :], tr[:, b, :], 1.0, hnb[:, b, :], ALU.add, ALU.mult))
                dve.wait_ge(*banks.full("n", it, b))
                V.tensor_tensor(tt[:, b, :], tt[:, b, :], banks.bank("n", it, b), ALU.add)\
                 .then_inc(drained["dve"], 1)

            def gru_end(b, it):
                dve.wait_ge(*banks.emptied("z", it, b))
                link(V.tensor_scalar(zs[:, b, :], tz[:, b, :], 0.5, 0.5, ALU.mult, ALU.add))
                V.tensor_tensor(zs[:, b, :], zs[:, b, :], slots_t[:, b, :], ALU.mult)
                dve.wait_ge(n_ready[b], it + 1)
                link(V.scalar_tensor_tensor(dd[:, b, :], tz[:, b, :], 1.0, nn[:, b, :], ALU.subtract, ALU.mult))
                V.scalar_tensor_tensor(slots_t[:, b, :], dd[:, b, :], -0.5, zs[:, b, :], ALU.mult, ALU.add)\
                 .then_inc(slots_ready[b], 1)

            def slots_back(b):
                add_out(b, 6)

            def turn(b, stage):
                if stage == 7:
                    dve.wait_ge(*banks.full("xn_t", 7, b))
                    V.tensor_scalar(lhs_q[:, b, :], banks.bank("xn_t", 7, b), -127.0, None, ALU.max)\
                     .then_inc(drained["dve"], 1)

            def quantised(b):
                g = GAIN_OF[7]
                dve.wait_ge(*banks.emptied("rscale"))
                dve.wait_ge(*banks.full("out", 7, b))
                for t in range(T):
                    last = V.scalar_tensor_tensor(xn[:, b, t, :], banks.bank("out", 7, b)[:, t * P:(t + 1) * P],
                                                  route_s[:, b, 3, t:t + 1], rscale_b[:, :], ALU.mult, ALU.mult)
                last.then_inc(drained["dve"], 1)
                dve.wait_ge(*banks.emptied("out", 7, b))
                V.scalar_tensor_tensor(flat(x[:, b, :, :]), flat(xn[:, b, :, :]), gain[:, g:g + 1],
                                       flat(x[:, b, :, :]), ALU.mult, ALU.add).then_inc(x_final[b], 1)

            mine = {"norm": norm, "norm_end": norm_end, "keys_in": keys_in, "masks": masks, "values_in": values_in,
                    "place": place, "slots_in": slots_in, "query": query, "maxima": maxima, "max_rows": max_rows, "values_back": values_back, "project": project,
                    "hidden0": hidden0, "back": back, "gates1": gates1, "weights_turn": weights_turn,
                    "shared": shared, "experts": experts, "router": router, "choice_turn": choice_turn,
                    "hidden2": hidden2, "square": square, "slot_scores": slot_scores, "slot_sums": slot_sums,
                    "slot_weights": slot_weights, "gru": gru, "gru_end": gru_end, "slots_back": slots_back,
                    "turn": turn, "quantised": quantised}
            for phase, b, args in SCHEDULE:
                if phase in mine:
                    mine[phase](b, *args)



def _constants():
    part = np.arange(P)
    row_ = part % GR
    pair = np.arange(NJ * P)
    head, key = pair // CTX, pair % CTX
    real = pair < GK
    out = {
        "ident": np.eye(P),
        "head_mask": np.stack([(part // GR == g % LANES)
                               & ((row_ < VALUES) & (row_ // DH == h) | (row_ == VALUES + h) | (row_ == VALUES + G3 + h))
                               for g in range(GROUPS) for h in range(G3)], 1),
        "chunk_mask": np.stack([(head == h) & real for h in range(G3)], 1).reshape(NJ, P, G3).transpose(1, 0, 2),
        "rev16": np.broadcast_to(E1 - np.arange(E1), (P, E1)),
        "rev32": np.broadcast_to(E2 - np.arange(E2), (P, E2)),
        "key_of": (part[:, None] == key[None, :]) & real[None, :],
        "sel1": (part[:, None] < 2 * E1) & (part[:, None] % E1 == np.arange(C1 * P)[None, :] // F1),
        "sel2": part[:, None] == np.arange(C2 * P)[None, :] // F2,
    }
    out["ident16"] = out["ident"]

    def pack(names):
        return np.concatenate([np.asarray(out[name], np.float32).reshape(P, n) for name, n in names], 1)

    def bits(m):
        return np.where(m == 0, 0, 0x3F80).astype(np.uint16)

    return {"consts": pack(CONSTS), "rounded": bits(pack(ROUNDED)), "halves": bits(pack(HALVES))}



def _side_by_side(m, n=P):
    k = -(-m.shape[0] // n)
    full = np.zeros((k * n,) + m.shape[1:], m.dtype)
    full[:m.shape[0]] = m
    return full.reshape(k, n, -1).transpose(1, 0, 2).reshape(n, -1)


def _layout(i):
    heads = lambda m: np.tile(m, (1, H))
    column = lambda v: np.reshape(v, (-1, P)).T
    filled = lambda m, n: np.concatenate([m, np.zeros(m.shape[:-1] + (n - m.shape[-1],), m.dtype)], -1)

    def grouped(m, rest=0.0):
        m = filled(m, GROUPS * VALUES).reshape(m.shape[:-1] + (GROUPS, VALUES))
        m = np.concatenate([m, np.full(m.shape[:-1] + (2 * G3,), rest, m.dtype)], -1)
        return filled(m, GR).reshape(m.shape[:-2] + (GROUPS * GR,))

    def group_columns(v, rest=0.0):
        return filled(grouped(v, rest), 2 * P).reshape(2, P).T

    packed = {
        "cols": [group_columns(i["L0_xattn_bq"]), group_columns(i["L0_xattn_bq"], -1.0),
                 group_columns(i["L1_xattn_bq"]), group_columns(np.tile(i["L1_xattn_bk"], H), -1.0),
                 group_columns(i["L2_xattn_bq"]), group_columns(i["L2_xattn_bk"], -1.0), column(i["L0_ffn_b1"]),
                 column(i["L2_ffn_bias1"]), column(i["L3_xattn_gru_bi"]), column(i["L3_xattn_gru_bh"]),
                 column(i["L3_xattn_slot_norm_w"]), column(i["L3_xattn_input_norm_w"])],
        "rows": [v[None, :] for v in (
            np.concatenate([i["g_xattn"], i["g_ffn"]]), i["L0_xattn_bq"], np.tile(i["L1_xattn_bv"], H),
            i["L2_xattn_bv"], i["L0_xattn_bo"], i["L0_ffn_b2"], i["L1_xattn_bo"], i["L2_xattn_bo"],
            i["L2_ffn_router_b"])],
        "attn0": [grouped(i["L0_xattn_Wq"].T), i["L0_xattn_Wq"].T, i["L0_xattn_Wo"].T],
        "ffn0": [i["L0_ffn_w1"], _side_by_side(i["L0_ffn_w2"])],
        "attn1": [grouped(heads(i["L1_xattn_Wk"])), heads(i["L1_xattn_Wv"]), grouped(i["L1_xattn_Wq"]), i["L1_xattn_Wo"]],
        "ffn1": [i["L1_ffn_gate_w"].T, i["L1_ffn_shared_gate_w"].T,
                 i["L1_ffn_w_gate_up"][:, :, :F1].transpose(1, 0, 2).reshape(D, E1 * F1),
                 i["L1_ffn_w_gate_up"][:, :, F1:].transpose(1, 0, 2).reshape(D, E1 * F1),
                 _side_by_side(i["L1_ffn_w_down"].reshape(E1 * F1, D)),
                 i["L1_ffn_shared_w_gate"].T, i["L1_ffn_shared_w_up"].T, _side_by_side(i["L1_ffn_shared_w_down"].T)],
        "attn2": [grouped(i["L2_xattn_wk"].T), i["L2_xattn_wv"].T, grouped(i["L2_xattn_wq"].T), i["L2_xattn_wo"].T],
        "ffn2": [i["L2_ffn_router_w"].T, i["L2_ffn_weights1"].transpose(1, 0, 2).reshape(D, E2 * F2),
                 _side_by_side(i["L2_ffn_weights2"].reshape(E2 * F2, D)), _side_by_side(i["L2_ffn_bias2"])],
        "attn3": [i["L3_xattn_Wk"].T, i["L3_xattn_Wv"].T, i["L3_xattn_Wq"], i["L3_xattn_gru_wi"].T,
                  i["L3_xattn_gru_wh"].T, i["L3_ffn_rhs"].T],
    }
    ctx_ = i["ctx_1024"]
    out = {"x": i["x"], "mask": i["mask_Bx1xSxS2_if1"], "ctx_rows": ctx_,
           "ctx_t": ctx_.transpose(2, 0, 1).reshape(D, B * CTX), **_constants()}
    out.update({k: np.concatenate(v, 1) for k, v in packed.items()})
    return {k: np.ascontiguousarray(v) for k, v in out.items()}


def kernel(**inputs):
    import concourse.bacc as bacc
    from concourse.bass_utils import run_bass_kernel_spmd

    nc = bacc.Bacc("TRN2", target_bir_lowering=False, num_devices=1)
    arrays = {f"in_{k}": v for k, v in _layout({k: np.asarray(v) for k, v in inputs.items()}).items()}
    a = {k[3:]: nc.dram_tensor(k, v.shape, mybir.dt.from_np(v.dtype), kind="ExternalInput").ap()
         for k, v in arrays.items()}
    out = nc.dram_tensor("out", (B, S, D), F32, kind="ExternalOutput").ap()
    program(nc, a, out)
    return run_bass_kernel_spmd(nc, [arrays], core_ids=[0]).results[0]["out"]
```

```python
from contextlib import ExitStack

import numpy as np

import concourse.bass as bass
from concourse import mybir

ALU = mybir.AluOpType
ACT = mybir.ActivationFunctionType
AX = mybir.AxisListType
F32 = mybir.dt.float32
F32R = mybir.dt.float32r
BF16 = mybir.dt.bfloat16
I32 = mybir.dt.int32

P = 128
B = 2
S = 512
D = 128
T = S // P
CTX = 77
H = 16
DH = D // H
G3 = 3
GROUPS = -(-H // G3)
GR = P // 4
LANES = P // GR
PART_ROWS = [P, (GROUPS - LANES) * GR]
HEADS = [min(G3, H - G3 * g) for g in range(GROUPS)]
GK = G3 * CTX
NJ = -(-GK // P)
GKE = GK + GK % 2
SETS = [[(g, 0) for g in range(LANES)], [(g, 1) for g in range(LANES)], [(4, 0), (5, 0), (4, 1)]]
SLOT = {c: i for i, c in enumerate(c for group in SETS for c in group)}
ROWS = {(g, j): min(P, HEADS[g] * CTX - P * j) for g, j in SLOT}
VALUES = G3 * DH
BANKS = 8
E1, F1, SH = 16, 64, 352
E2, F2 = 32, 32
C1 = E1 * F1 // P
SHC = [(i, min(P, SH - i)) for i in range(0, SH, P)]
C2 = E2 * F2 // P
W0 = 512
C0 = W0 // P
ITERS = 3
MASKED = -(2.0 ** 100)
ROUND = 1.5 * 2.0 ** 23
MASK_PLACES = -(-B * T * CTX // S)
LN_EPS, RMS_EPS = 1e-5, 1e-6

COLS = [("bq0", 2), ("bk0", 2), ("bq1", 2), ("bk1", 2), ("bq2", 2), ("bk2", 2), ("b1", C0), ("bias1", C2),
        ("bi", 3), ("bh", 3), ("w_slot", 1), ("w_in", 1)]
ROWSPACK = [("g", 8), ("bv0", D), ("bv1", D), ("bv2", D), ("bo0", D), ("b2", D), ("bo1", D), ("bo2", D),
            ("router_b", E2)]
CONSTS = [("ident", P), ("head_mask", GROUPS * G3), ("chunk_mask", NJ * G3), ("rev16", E1), ("rev32", E2)]
ROUNDED = [("sel1", C1 * P)]
HALVES = [("key_of", NJ * P), ("ident16", P), ("sel2", C2 * P)]
PACKS = {
    "attn0": [("wq", GROUPS * GR), ("wv", D), ("wo", D)],
    "ffn0": [("w1", W0), ("w2", C0 * D)],
    "attn1": [("wk", GROUPS * GR), ("wv", D), ("wq", GROUPS * GR), ("wo", D)],
    "ffn1": [("gates", E1 + 1), ("w_g", C1 * P), ("w_u", C1 * P), ("w_down", C1 * D), ("s_g", SH), ("s_u", SH),
             ("s_down", len(SHC) * D)],
    "attn2": [("wk", GROUPS * GR), ("wv", D), ("wq", GROUPS * GR), ("wo", D)],
    "ffn2": [("router", E2), ("w1", C2 * P), ("w2", C2 * D), ("bias2", D)],
    "attn3": [("wk", D), ("wv", D), ("wq", D), ("wi", 3 * D), ("wh", 3 * D), ("rhs_t", D)],
}


def columns(pack):
    at, out = 0, {}
    for name, n in pack:
        out[name] = (at, at + n)
        at += n
    return out, at


HANDOVER = 0.15
LAG = 0
PREFER_STREAM = 0.0, 0.037, 0.293
PREFER_ENGINE = {"pe": 0.0, "act": -1.097, "dve": -0.1, "pool": -1.237}
PER_STEP_LEFT = -0.001
OPEN = 3
FILLERS = {"slot_weights": 2, "gru": 3, "slots_back": 4, "quantised": 3}
EARLY = 2
PREPARATION = 2


class Step:

    def __init__(self, stream, phase, args, on, side, after, takes):
        self.stream, self.phase, self.args = stream, phase, args
        self.on, self.side, self.after, self.takes = on, side, after, list(takes.items())
        self.ends = []


def stream_steps(b):
    out = []

    def step(phase, *args, on=False, side=False, after=(), **takes):
        out.append(Step(b, phase, args, on, side, after, takes))

    if b == PREPARATION:
        step("keys_in", 0, pe=1.2, act=0.7, dve=4.0, pool=5.2)
        step("mask_parts", dve=1.8)
        step("masks", pe=0.9, act=2.0)
        step("values_in", 0, on=True, pe=0.5, dve=1.8)
        step("keys_in", 1, on=True, pe=0.6, act=0.6, dve=0.8)
        step("keys_in", 2, pe=0.6, act=0.6, dve=0.8, after=[(0, "bias", 0)])
        step("place", 0, pe=1.3, dve=1.7)
        for layer in (1, 2):
            step("values_in", layer, pe=0.5, dve=1.8)
            step("place", layer, pe=1.3, dve=1.3)
        step("slots_in", 0, act=1.5, dve=1.8)
        step("slots_in", 1, pe=0.3, act=0.5)
        step("slots_in", 2, pe=0.5, act=0.6, dve=0.9)
        step("slots_in", 3, pe=2.5, act=0.8, dve=0.3)
        step("slots_in", 4, pe=0.4, act=0.2, dve=0.2)
        return out

    def norm(stage):
        step("norm", stage, dve=1.2, pool=1.2)
        step("norm_end", stage, dve=1.05 if stage < 7 else 3.6)

    def attention(stage, layer):
        step("bias", stage, side=True, pool=1.2)
        step("turn", stage, pe=0.43, act=0.5)
        step("query", layer, pe=1.75, act=2.2, after=[(PREPARATION, "keys_in", 0)])
        step("q_low", layer, side=True, pool=2.4)
        for u in range(T // 2):
            step("maxima", layer, u, on=u == 0, pe=1.3 if layer else 2.4, dve=3.0,
                 after=[(b, "keys_next", layer)] if layer else [(PREPARATION, "mask_parts")])
        step("max_parts", layer, dve=0.4)
        for part in range(2):
            step("max_rows", layer, part, on=True, pe=0.45, dve=0.6, after=[(b, "q_low", layer), (PREPARATION, "masks")])
        for i in range(len(SETS)):
            step("scores", layer, i, on=True, pe=0.65 * len(SETS[i]) * (1 if layer else 1.33), act=0.5 * len(SETS[i]),
                 after=[(b, "max_rows", layer, i // 2)] + ([(PREPARATION, "place", 2)] if b else []))
        if layer < 2:
            step("keys_next", layer + 1, side=True, pool=5.2,
                 after=[(PREPARATION, "keys_in", layer + 1), (b, "scores", layer, 2)])
        for part in range(2):
            step("values", layer, part, on=part == 0, pe=1.8, act=0.5,
                 after=[(PREPARATION, "place", layer), (b, "scores", layer, part + 1)])
        for u in range(T // 2):
            step("values_back", layer, u, on=u == 0, pe=0.43, dve=0.8)
        step("out_turn", layer, pe=0.43, act=0.5)
        step("project", stage, layer, pe=0.86, dve=0.7, after=[(b, "bias", stage)])
        norm(stage + 1)

    norm(0)
    attention(0, 0)
    step("bias", 1, side=True, pool=1.2)
    step("turn", 1, pe=0.43, act=0.5)
    for m in range(C0):
        step("hidden0", m, on=True, pe=0.86, **{"act" if m % 2 else "dve": 0.6})
    step("down0", pe=3.4, act=0.5)
    step("back", 1, pe=0.43, dve=0.7, after=[(b, "bias", 1)])
    norm(2)
    attention(2, 1)
    step("turn", 3, pe=0.43, act=0.5)
    step("gates1", on=True, pe=0.5, dve=2.1, act=0.85)
    for i in range(len(SHC)):
        step("shared", i, on=True, pe=1.7, act=0.9, dve=0.6)
    for c in range(C1):
        step("experts", c, on=True, pe=1.7, act=0.5, dve=0.6)
        if c == EARLY - 1:
            step("weights_turn", dve=1.4, pe=0.43, act=0.5, after=[(b, "gates1")])
        if c >= EARLY:
            step("weigh", c - EARLY, on=True, pe=0.22, dve=0.6)
    for c in range(C1 - EARLY, C1):
        step("weigh", c, on=True, pe=0.22, dve=0.6)
    step("down1", pe=9.4, act=1.0)
    step("back", 3, pe=0.86, dve=1.8)
    norm(4)
    attention(4, 2)
    step("turn", 5, pe=0.43, act=0.5)
    step("router", on=True, pe=0.5, dve=1.5, after=[(1, "down1")])
    for c in range(C2 + OPEN):
        if c < C2:
            step("hidden2", c, on=True, pe=0.86)
        if c == OPEN - 1:
            step("choice_turn", pe=0.43, act=0.5, dve=0.4, after=[(b, "router")])
        if c >= OPEN:
            step("choose", c - OPEN, on=True, pe=0.22, **{"act" if (c - OPEN) % 2 else "dve": 0.6})
    step("down2", pe=7.7, act=0.5)
    step("back", 5, pe=0.43, dve=0.7)
    norm(6)
    step("turn", 6, pe=0.43, act=0.5)
    for it in range(ITERS):
        step("hidden_gate", it, "r", on=True, pe=0.86)
        step("square", it, act=0.5, pe=0.85, dve=0.1, pool=1.0)
        step("hidden_gate", it, "z", on=True, pe=0.86)
        step("slot_products", it, on=True, pe=0.86, act=0.5)
        step("slot_scores", it, pe=0.86, dve=1.3, act=0.8)
        step("hidden_gate", it, "hn", on=True, pe=0.86, act=0.6)
        step("slot_inverse", it, dve=0.1)
        step("slot_sums", it, pe=0.75, dve=0.3)
        step("slot_weights", it, pe=0.86, dve=0.6)
        step("gru", it, on=True, pe=1.7, act=0.6, dve=1.25)
        step("gru_z", it, on=True, pe=0.86, act=0.6, dve=1.0)
        step("gru_end", it, act=0.6, dve=1.3, after=[(b, "gru", it), (b, "gru_z", it)])
    step("slots_back", pe=0.43, dve=0.7)
    norm(7)
    step("turn", 7, pe=0.86, dve=0.6)
    step("quantised", pe=0.2, dve=1.6)
    return out


def schedule():
    streams = [stream_steps(b) for b in range(B + 1)]
    steps = {(st.stream, st.phase, *st.args): st for stream in streams for st in stream}
    orders = {"pe": [], "act": [], "dve": [], "pool": []}
    free = dict.fromkeys(orders, 0.0)
    banks = BankTurn()
    drained = {}
    done_at = [0.0, LAG, 0.0]

    def begin(st, earlier):
        engine = st.takes[len(st.ends)][0]
        if any(engine in [e for e, _ in other.takes[len(other.ends):]] for other in earlier):
            return None
        if st.ends:
            at = st.ends[-1]
        else:
            at = done_at[st.stream]
            for other in earlier:
                if not other.side:
                    if not (other.on and other.ends):
                        return None
                    at = max(at, other.ends[0])
            for key in st.after:
                other = steps[key]
                if len(other.ends) < len(other.takes):
                    return None
                at = max(at, other.ends[-1])
        if engine == "pe":
            at = max(at, banks.deal(st.phase, units_of(st.phase, st.stream, st.args), st.stream, drained)[1])
            if at == float("inf"):
                return None
        return max(at + HANDOVER, free[engine])

    while any(streams):
        best = None
        for stream in streams:
            earlier = []
            for st in stream:
                if len(st.ends) < len(st.takes):
                    at = begin(st, earlier)
                    if at is not None:
                        rank = at + PREFER_STREAM[st.stream] + PREFER_ENGINE[st.takes[len(st.ends)][0]] - PER_STEP_LEFT * len(stream)
                        if best is None or rank < best[0] - 1e-6:
                            best = rank, at, st
                    if not st.ends and not st.side:
                        break
                    earlier.append(st)
        _, at, st = best
        engine, us = st.takes[len(st.ends)]
        if engine == "pe":
            banks.take(st.phase, units_of(st.phase, st.stream, st.args), st.stream, drained)
        free[engine] = at + us
        st.ends.append(at + us)
        for name, reader in finished_by(st.phase, st.stream, st.args):
            if reader == engine:
                drained[name] = at + us
        orders[engine].append((st.phase, st.stream, st.args))
        if len(st.ends) == len(st.takes):
            streams[st.stream].remove(st)
            if not st.side:
                done_at[st.stream] = max(done_at[st.stream], st.ends[0 if st.on else -1])
    return orders, banks.dealt, max(free.values())


class BankTurn:

    def __init__(self):
        self.last_in, self.ring, self.dealt = {}, BANKS, {}

    def deal(self, phase, units, b, drained):
        ring = BANKS // 2 if phase == "hidden_gate" else self.ring

        def since(bank):
            if bank is None:
                return float("inf")
            return drained.get(self.last_in[bank], float("inf")) if bank in self.last_in else 0.0

        free, dealt = sorted(range(ring), key=since) + [None], []
        for name, _ in units:
            if name[0] in ("r", "z"):
                dealt.append((name, BANKS // 2 + 2 * b + (name[0] == "z")))
            else:
                dealt.append((name, free.pop(0) if free else None))
        return dealt, max([since(bank) for _, bank in dealt], default=0.0)

    def take(self, phase, units, b, drained):
        dealt, _ = self.deal(phase, units, b, drained)
        if phase == "hidden_gate":
            self.ring = BANKS // 2
        for name, bank in dealt:
            self.dealt[name] = bank, self.last_in.get(bank)
            self.last_in[bank] = name


def units_of(phase, b, args):
    if phase == "keys_in":
        return [(("k", *args), "act")]
    if phase == "values_in":
        return [(("v", *args), "dve")]
    if phase == "place":
        return [(("vrows", *args, j), "dve") for j in range(NJ)]
    if phase == "masks":
        return [(("mask_t", i), "act") for i in range(B)]
    if phase == "slots_in":
        return [[], [(("pn_t",), "act")], [(("kproj",), "act"), (("vproj",), "act")],
                [(("kq",), "dve"), (("vw", 0), "act"), (("vw", 1), "act")],
                [(("rq_t",), "dve"), (("rscale",), "act")]][args[0]]
    if phase == "turn":
        return [(("xn_t", args[0], b), "dve" if args[0] == 7 else "act")]
    if phase == "maxima":
        return [(("max", args[0], b, args[1], g), "dve") for g in range(GROUPS)]
    if phase == "query":
        return [(("q", args[0], b, part), "act") for part in range(2)]
    if phase == "max_rows":
        return [(("max_t", args[0], b, args[1]), "dve")]
    if phase == "scores":
        return [(("p", args[0], b, *chunk), "act") for chunk in SETS[args[1]]]
    if phase == "hidden0":
        return [(("h0", b, args[0]), "act" if args[0] % 2 else "dve")]
    if phase == "hidden2":
        return [(("h2", b, args[0]), "act" if args[0] % 2 else "dve")]
    if phase == "shared":
        return [(("s_g", b, args[0]), "act"), (("s_u", b, args[0]), "dve")]
    if phase == "experts":
        return [(("e_g", b, args[0]), "act"), (("e_u", b, args[0]), "dve")]
    if phase == "weigh":
        return [(("e_w", b, args[0]), "dve")]
    if phase == "down1":
        return [(("s_y", b), "act"), (("y", 3, b), "act")]
    if phase == "back":
        return ([(("s_out", b), "dve")] if args[0] == 3 else []) + [(("out", args[0], b), "dve")]
    if phase == "hidden_gate":
        return [((args[1], args[0], b), "act")]
    if phase == "slot_products":
        return [(("s", args[0], b), "act")]
    if phase == "slot_scores":
        return [(("rstd_b", args[0], b), "dve")]
    if phase == "gru":
        return [(("n", args[0], b), "dve")]
    one = {"values": ("pv", "act"), "values_back": ("o", "dve"),
           "out_turn": ("o_t", "act"), "gates1": ("gates1", "dve"), "weights_turn": ("comb_t", "act"),
           "router": ("router", "dve"), "choice_turn": ("hot_t", "act"), "square": ("ss", "dve"),
           "slot_sums": ("asum", "dve"), "slot_weights": ("ra_b", "dve")}
    if phase in one:
        name, reader = one[phase]
        return [((name, *args[:1], b, *args[1:]), reader)]
    return {"project": [(("out", *args[:1], b), "dve")], "down0": [(("y", 1, b), "act")],
            "down2": [(("y", 5, b), "act")], "slots_back": [(("out", 6, b), "dve")],
            "quantised": [(("out", 7, b), "dve")]}.get(phase, [])


def finished_by(phase, b, args):
    if phase == "hidden2" or phase == "hidden_gate" and args[1] != "hn":
        return []
    if phase == "choose":
        return units_of("hidden2", b, args)
    if phase == "gru_z":
        return [(("z", args[0], b), "act")]
    return ([(("r", args[0], b), "act")] if phase == "gru" else []) + units_of(phase, b, args)


ORDERS, DEALT, _ = schedule()


class Banks:

    def __init__(self, psum, filled, drained):
        self.psum, self.filled, self.drained = psum, filled, drained
        self.bank_of, self.before, self.filled_at, self.drained_at = {}, {}, {}, {}
        for phase, b, args in ORDERS["pe"]:
            for name, _ in units_of(phase, b, args):
                self.bank_of[name], self.before[name] = DEALT[name]
            for name, _ in finished_by(phase, b, args):
                self.filled_at[name] = len(self.filled_at) + 1
        for engine in ("act", "dve"):
            count = 0
            for phase, b, args in ORDERS[engine]:
                for name, reader in finished_by(phase, b, args):
                    if reader == engine:
                        count += 1
                        self.drained_at[name] = self.drained[reader], count
        assert self.filled_at.keys() == self.bank_of.keys() == self.drained_at.keys()

    def bank(self, *name):
        return self.psum[:, self.bank_of[name], :]

    def full(self, *name):
        return self.filled, self.filled_at[name]

    def emptied(self, *name):
        return self.drained_at[name]

    def reused(self, *name):
        return self.before[name] is not None

    def free(self, *name):
        return self.drained_at[self.before[name]]


def program(nc, a, out):
    with ExitStack() as ctx:
        def sb(name, shape, dt=F32):
            return ctx.enter_context(nc.sbuf_tensor(name, shape, dt))

        def sem(name):
            return ctx.enter_context(nc.semaphore(name))

        x = sb("x", [P, B, T, D])
        cols_at, cols_n = columns(COLS)
        rows_at, rows_n = columns(ROWSPACK)
        const_at, const_n = columns(CONSTS)
        halves_at, halves_n = columns(HALVES)
        rounded_at, rounded_n = columns(ROUNDED)
        cols = sb("cols", [P, cols_n])
        rows = sb("rows", [P, rows_n])
        consts = sb("consts", [P, const_n])
        ctx_t = sb("ctx_t", [P, B * CTX])
        ctx_rows = sb("ctx_rows", [CTX, B, D])
        packs = {k: sb("w_" + k, [P, columns(v)[1]]) for k, v in PACKS.items() if k != "ffn2"}
        packs["ffn2"] = packs["ffn1"][:, 0:columns(PACKS["ffn2"])[1]]

        def w(pack, name):
            lo, hi = columns(PACKS[pack])[0][name]
            return packs[pack][:, lo:hi]

        def col(name, i=0):
            lo = cols_at[name][0] + i
            return cols[:, lo:lo + 1]

        def row(name):
            lo, hi = rows_at[name]
            return rows[:, lo:hi]

        def const(name):
            lo, hi = const_at[name]
            return consts[:, lo:hi]

        halves = sb("halves", [P, halves_n], BF16)

        def half(name):
            lo, hi = halves_at[name]
            return halves[:, lo:hi]

        ident = const("ident")

        ident16, sel2 = half("ident16"), half("sel2")
        key_of = half("key_of")[0:CTX, :]
        ones = sb("ones", [P, 2])
        sel1 = sb("sel1", [P, C1 * P], F32R)
        mask_b16 = sb("mask_b16", [P, B, T, CTX], BF16)
        mask_t = sb("mask_t", [CTX, B, S], BF16)
        gain = sb("gain", [P, 8])
        gbias = sb("gbias", [P, 4, D])
        keys_hi = sb("keys_hi", [P, B, GROUPS, GKE], F32R)
        keys_lo = sb("keys_lo", [P, B, GROUPS, GKE], F32R)
        k_hi = sb("k_hi", [P, 3, 2, B, CTX], F32R)
        k_lo = sb("k_lo", [P, 3, 2, B, CTX], F32R)
        v_cols = sb("v_cols", [P, NJ, 3 * B, GROUPS, GR])
        pn = sb("pn", [CTX, B, D])
        p_ss = sb("p_ss", [CTX, B])
        p_small = sb("p_small", [CTX, 4, B])
        pn_t = sb("pn_t", [P, B * CTX])
        kproj = sb("kproj", [P, B * CTX])
        vproj = sb("vproj", [P, B * CTX])
        kq = sb("kq", [P, B * CTX])
        vw = sb("vw", [CTX, B, 3 * D])
        half_bias = sb("half_bias", [P, 3])
        rscale = sb("rscale", [P, 4])
        rq = sb("rq", [P, D])
        rhs_q = sb("rhs_q", [P, D], BF16)
        rscale_b = sb("rscale_b", [P, D])

        stats = sb("stats", [P, B, T, 6])
        mv = sb("mv", [P, B, T, 2])
        nw = sb("nw", [P, B, 3, T])
        xn = sb("xn", [P, B, T, D])
        xn_t = sb("xn_t", [P, B, S])
        q = sb("q", [P, B, 2, S])
        q_hi = sb("q_hi", [P, B, 2, S], F32R)
        q_lo = sb("q_lo", [P, B, 2, S], F32R)
        q_t, q_u = q[:, :, 0, :], q[:, :, 1, :]
        minus_half = sb("minus_half", [P, T])
        mx_raw = sb("mx_raw", [P, B, T, GROUPS, G3])
        mx_hi = sb("mx_hi", [P, B, T, GROUPS, G3], F32R)
        mx = sb("mx", [P, B, T, GROUPS, GR])
        comb_t = sb("comb_t", [P, B, S], F32R)
        wide = sb("wide", [P, B, C1 + len(SHC), S])
        rsum = sb("rsum", [P, B, T, GROUPS, G3])
        o = sb("o", [P, B, T, GROUPS * VALUES])
        lg = sb("lg", [P, B, T, E2])
        route = sb("route", [P, B, 5, T, E2])
        route_s = sb("route_s", [P, B, 8, T])
        comb = sb("comb", [P, B, T, 2 * E1], F32R)
        nothot_t = sb("nothot_t", [P, B, S], BF16)
        o_t, slots_t, y_t, s_y_t = q_t, q_t, q_t, xn_t
        lhs_q = nothot_t
        hot_t = xn[0:E2, :, :, :].rearrange("p b t d -> p b (t d)")
        mask_b = o[:, :, :, 0:CTX]
        wide3 = wide[:, :, 0:11, :]
        sq, ss, sc, ex, zs, an, tr, hnb, tz, tt, dd = [wide3[:, :, i, :] for i in range(11)]
        nn = xn_t
        act_s = [q_t, q_u]
        mask_i = wide[:, 0, 0:MASK_PLACES, :].rearrange("p c s -> p (c s)")[:, 0:B * T * CTX].bitcast(I32)\
            .rearrange("p (b t k) -> p b t k", b=B, t=T)
        early = wide[:, 1, :, :].rearrange("p c s -> p (c s)")
        k_n = 3 * 2 * B * CTX
        k_t = early[:, 0:k_n].rearrange("p (l r b k) -> p l r b k", l=3, r=2, b=B)
        v_at, v_n = k_n, 3 * B * D
        v_rows = early[0:CTX, v_at:v_at + v_n].rearrange("p (l b d) -> p l b d", l=3, b=B)
        v_parts = early[0:CTX, v_at + v_n:v_at + v_n + 3 * v_n // 2].bitcast(BF16)\
            .rearrange("p (i l b d) -> p i l b d", i=3, l=3, b=B)
        rounded_in = early[:, v_at + v_n + 3 * v_n // 2:].bitcast(BF16)
        y = wide[:, :, 0, :].rearrange("p b (t d) -> p b t d", t=T)
        nmax = sb("nmax", [CTX, B, 4])

        psum = ctx.enter_context(nc.psum_tensor("psum", [P, BANKS, 512], F32))

        loaded = {k: sem("loaded_" + k) for k in
                  ["x", "cols", "rows", "consts", "rounded", "halves", "ctx_t", "ctx_rows", "mask"] + list(PACKS)}
        filled = sem("bank_filled")
        drained = {"act": sem("bank_drained_by_act"), "dve": sem("bank_drained_by_dve")}
        consts_made = sem("consts_made")
        zeros_made = sem("zeros_made")
        dve_step = sem("dve_step")
        pool_step = sem("pool_step")
        act_step = sem("act_step")
        gain_ready = sem("gain_ready")
        gbias_ready = sem("gbias_ready")
        sums_placed = sem("sums_placed")
        rounded_ready = sem("rounded_ready")
        v_parts_ready = sem("v_parts_ready")
        k_parts = sem("k_parts")
        mask_b_ready = sem("mask_b_ready")
        p_ss_ready = sem("p_ss_ready")
        pn_ready = sem("pn_ready")
        rq_ready = sem("rq_ready")

        def per_half(name):
            return [sem(f"{name}_{b}") for b in range(B)]

        var_ready = per_half("var_ready")
        xn_rstd_ready = per_half("xn_rstd_ready")
        xn_ready = per_half("xn_ready")
        q_parts = per_half("q_parts")
        q_lo_ready = per_half("q_lo_ready")
        max_ready = per_half("max_ready")
        keys_ready = per_half("keys_ready")
        bias_added = per_half("bias_added")
        gap_ready = per_half("gap_ready")
        second_ready = per_half("second_ready")
        comb_ready = per_half("comb_ready")
        hot_ready = per_half("hot_ready")
        nothot_ready = per_half("nothot_ready")
        sq_ready = per_half("sq_ready")
        rstd_ready = per_half("rstd_ready")
        nmax_ready = per_half("nmax_ready")
        ex_ready = per_half("ex_ready")
        slot_inverse_ready = per_half("slot_inverse_ready")
        ra_ready = per_half("ra_ready")
        n_ready = per_half("n_ready")
        slots_ready = per_half("slots_ready")
        x_final = per_half("x_final")
        stored = sem("stored")

        banks = Banks(psum, filled, drained)
        BIASED = {0: 0, 1: 1, 2: 2, 4: 3}
        GAIN_OF = [0, 4, 1, 5, 2, 6, 3, 7]

        block = ctx.enter_context(nc.Block())

        @block.sync
        def _(sp):
            for b in range(B):
                sp.dma_start(x[:, b, :, :], a["x"][b].rearrange("(t p) d -> p t d", p=P)).then_inc(loaded["x"], 16)
            sp.dma_start(ctx_t[:, :], a["ctx_t"]).then_inc(loaded["ctx_t"], 16)
            sp.dma_start(packs["attn0"][:, :], a["attn0"]).then_inc(loaded["attn0"], 16)
            sp.dma_start(cols[:, :], a["cols"]).then_inc(loaded["cols"], 16)
            sp.dma_start(rows[:, :], a["rows"].broadcast_to([P, rows_n])).then_inc(loaded["rows"], 16)
            sp.dma_start(consts[:, :], a["consts"]).then_inc(loaded["consts"], 16)
            sp.dma_start(halves[:, :], a["halves"].bitcast(BF16)).then_inc(loaded["halves"], 16)
            sp.dma_start(mask_i, a["mask"].rearrange("b o (t p) k -> p b (o t) k", p=P)).then_inc(loaded["mask"], 16)
            sp.dma_start(rounded_in[:, 0:rounded_n], a["rounded"].bitcast(BF16)).then_inc(loaded["rounded"], 16)
            sp.dma_start(packs["attn1"][:, :], a["attn1"]).then_inc(loaded["attn1"], 16)
            sp.dma_start(packs["attn2"][:, :], a["attn2"]).then_inc(loaded["attn2"], 16)
            sp.dma_start(packs["ffn0"][:, :], a["ffn0"]).then_inc(loaded["ffn0"], 16)
            sp.dma_start(ctx_rows[:, :, :], a["ctx_rows"].rearrange("b k d -> k b d")).then_inc(loaded["ctx_rows"], 16)
            sp.dma_start(packs["attn3"][:, :], a["attn3"]).then_inc(loaded["attn3"], 16)
            sp.dma_start(packs["ffn1"][:, :], a["ffn1"]).then_inc(loaded["ffn1"], 16)
            for b in range(B):
                sp.wait_ge(*banks.full("y", 3, b))
            sp.dma_start(packs["ffn2"][:, :], a["ffn2"]).then_inc(loaded["ffn2"], 16)
            for b in range(B):
                sp.wait_ge(x_final[b], 1)
                sp.dma_start(out[b].rearrange("(t p) d -> p t d", p=P), x[:, b, :, :]).then_inc(stored, 16)
            sp.wait_ge(stored, 16 * B)

        def spread_keys(engine, b, layer, k_part, keys):
            for part, r in enumerate(PART_ROWS):
                groups = slice(part * LANES, min(GROUPS, (part + 1) * LANES))
                n = groups.stop - groups.start
                engine.tensor_tensor(
                    keys[0:r, b, groups, 0:GK].rearrange("p g (h k) -> p g h k", h=G3),
                    k_part[0:r, layer, part, b, :].bitcast(F32).unsqueeze(1).unsqueeze(1).broadcast_to([r, n, G3, CTX]),
                    const("head_mask").rearrange("p (g h) -> p g h", h=G3)[0:r, groups, :].unsqueeze(3)
                    .broadcast_to([r, n, G3, CTX]), ALU.mult).then_inc(keys_ready[b], 1)

        @block.gpsimd
        def _(pool):
            G = nc.gpsimd
            steps = [0]

            def link(ins):
                steps[0] += 1
                ins.then_inc(pool_step, 1)
                pool.wait_ge(pool_step, steps[0])

            def norm(b, stage):
                pool.wait_ge(var_ready[b], stage + 1)
                link(G.tensor_scalar(nw[:, b, 0, :], mv[:, b, :, 1], LN_EPS, None, ALU.add))
                G.tensor_tensor(nw[:, b, 2, :], nw[:, b, 0, :], minus_half[:, :], ALU.pow)\
                 .then_inc(xn_rstd_ready[b], 1)

            def bias(b, stage):
                if stage == 0:
                    pool.wait_ge(gbias_ready, 1)
                pool.wait_ge(xn_ready[b], T * (stage + 1))
                G.tensor_tensor(x[:, b, :, :], x[:, b, :, :],
                                gbias[:, BIASED[stage]:BIASED[stage] + 1, :].broadcast_to([P, T, D]),
                                ALU.add).then_inc(bias_added[b], 1)

            def keys_in(b, layer):
                pool.wait_ge(loaded["consts"], 16)
                pool.wait_ge(k_parts, 1)
                for i in range(B):
                    spread_keys(G, i, 0, k_lo, keys_lo)
                G.memset(v_cols[:, :, :, :, :], 0.0)
                G.memset(comb_t[:, :, :].bitcast(F32), 0.0)
                G.memset(nothot_t[:, :, :], 0.0).then_inc(zeros_made, 1)

            def q_low(b, layer):
                pool.wait_ge(*banks.emptied("q", layer, b, 1))
                for part, r in enumerate(PART_ROWS):
                    last = G.tensor_tensor(q_lo[0:r, b, part, :], q[0:r, b, part, :],
                                           q_hi[0:r, b, part, :].bitcast(F32), ALU.subtract)
                last.then_inc(q_lo_ready[b], 1)

            def keys_next(b, layer):
                pool.wait_ge(k_parts, layer + 1)
                pool.wait_ge(*banks.full("p", layer - 1, b, *SETS[-1][-1]))
                spread_keys(G, b, layer, k_hi, keys_hi)
                spread_keys(G, b, layer, k_lo, keys_lo)

            def square(b, it):
                pool.wait_ge(*banks.emptied("ss", it, b))
                G.tensor_tensor(nw[:, b, 2, :], nw[:, b, 0, :], minus_half[:, :], ALU.pow)\
                 .then_inc(rstd_ready[b], 1)

            G.memset(ones[:, 0:1], 1.0)
            G.memset(ones[:, 1:2], 1.0 / D)
            G.memset(keys_hi[:, :, :, GK:GKE].bitcast(F32), 0.0)
            G.memset(mx_raw[:, :, :, :, :], 0.0)
            G.memset(mx[:, :, :, :, :], 0.0)
            G.memset(minus_half[:, :], -0.5).then_inc(consts_made, 1)
            pool.wait_ge(consts_made, 1)
            mine = {"norm": norm, "bias": bias, "keys_in": keys_in, "q_low": q_low, "keys_next": keys_next,
                    "square": square}
            for phase, b, args in ORDERS["pool"]:
                mine[phase](b, *args)

        @block.tensor
        def _(pe):
            def start_unit(*name):
                if banks.reused(*name):
                    pe.wait_ge(*banks.free(*name))
                return banks.bank(*name)

            def mm(out_, lhs, rhs, start=True, stop=True, **kw):
                return nc.tensor.matmul(out_, lhs, rhs, start=start, stop=stop, **kw)

            def keep_warm(bk, phase):
                for _ in range(FILLERS.get(phase, 0)):
                    mm(bk, ident16, halves[:, 0:S])

            def keys_in(b, layer):
                pe.wait_ge(loaded[f"attn{layer}"], 16)
                if layer == 0:
                    pe.wait_ge(loaded["ctx_t"], 16)
                wk = w(f"attn{layer}", "wk" if layer else "wq")
                bk = start_unit("k", layer)
                for part, r in enumerate(PART_ROWS):
                    last = mm(bk[0:r, part * B * CTX:(part + 1) * B * CTX], wk[:, part * P:part * P + r], ctx_t[:, :])
                last.then_inc(filled, 1)

            def values_in(b, layer):
                bk = start_unit("v", layer)
                for i in range(B):
                    last = mm(bk[0:CTX, i * D:(i + 1) * D], ctx_t[:, i * CTX:(i + 1) * CTX], w(f"attn{layer}", "wv"))
                last.then_inc(filled, 1)

            def place(b, layer):
                if layer == 0:
                    pe.wait_ge(loaded["halves"], 16)
                pe.wait_ge(v_parts_ready, layer + 1)
                for j in range(NJ):
                    bk = start_unit("vrows", layer, j)
                    for part in range(3):
                        last = mm(bk[:, 0:B * D], key_of[:, j * P:(j + 1) * P],
                                  v_parts[:, part, layer, :, :].rearrange("p b e -> p (b e)"),
                                  start=part == 0, stop=part == 2)
                    last.then_inc(filled, 1)

            def masks(b):
                for i in range(B):
                    bk = start_unit("mask_t", i)
                    pe.wait_ge(mask_b_ready, i + 1)
                    for t in range(T):
                        last = nc.tensor.transpose(bk[0:CTX, t * P:(t + 1) * P], mask_b[:, i, t, :], ident)
                    last.then_inc(filled, 1)

            def slots_in(b, i):
                if i == 1:
                    bk = start_unit("pn_t")
                    pe.wait_ge(pn_ready, 1)
                    for i in range(B):
                        last = nc.tensor.transpose(bk[:, i * CTX:(i + 1) * CTX], pn[:, i, :], ident[0:CTX, 0:CTX])
                    last.then_inc(filled, 1)
                elif i == 2:
                    pe.wait_ge(loaded["attn3"], 16)
                    pe.wait_ge(*banks.emptied("pn_t"))
                    for name, weights in (("kproj", "wk"), ("vproj", "wv")):
                        bk = start_unit(name)
                        mm(bk[:, 0:B * CTX], w("attn3", weights), pn_t[:, :]).then_inc(filled, 1)
                elif i == 3:
                    bk = start_unit("kq")
                    pe.wait_ge(*banks.emptied("kproj"))
                    mm(bk[:, 0:B * CTX], w("attn3", "wq"), kproj[:, :]).then_inc(filled, 1)
                    for i in range(B):
                        bk = start_unit("vw", i)
                        pe.wait_ge(*banks.emptied("vproj"))
                        mm(bk[0:CTX, 0:3 * D], vproj[:, i * CTX:(i + 1) * CTX], w("attn3", "wi")).then_inc(filled, 1)
                elif i == 4:
                    bk = start_unit("rq_t")
                    pe.wait_ge(rq_ready, 1)
                    nc.tensor.transpose(bk[:, 0:D], rq[:, :], ident).then_inc(filled, 1)
                    bk = start_unit("rscale")
                    mm(bk[:, 0:D], rscale[:, 1:2].broadcast_to([P, P]), ident).then_inc(filled, 1)

            def turn(b, stage):
                bk = start_unit("xn_t", stage, b)
                if stage == 0:
                    pe.wait_ge(loaded["consts"], 16)
                    pe.wait_ge(consts_made, 1)
                for t in range(T):
                    pe.wait_ge(xn_ready[b], T * stage + t + 1)
                    last = nc.tensor.transpose(bk[:, t * P:(t + 1) * P], (y if stage == 7 else xn)[:, b, t, :], ident)
                last.then_inc(filled, 1)

            def query(b, layer):
                for part, r in enumerate(PART_ROWS):
                    bk = start_unit("q", layer, b, part)
                    pe.wait_ge(*banks.emptied("xn_t", 2 * layer, b))
                    mm(bk[0:r, :], w(f"attn{layer}", "wq")[:, part * P:part * P + r], xn_t[:, b, :]).then_inc(filled, 1)

            def maxima(b, layer, u):
                if u == 0:
                    pe.wait_ge(keys_ready[b], 4 * (layer + 1))
                for lanes in (range(LANES), range(LANES, GROUPS)):
                    bks = {g: start_unit("max", layer, b, u, g) for g in lanes}
                    if layer == 0:
                        pe.wait_ge(mask_b_ready, b + 1)
                    if u == 0:
                        pe.wait_ge(q_parts[b], 2 * layer + (1 if lanes[0] == 0 else 2))
                    for i in range(2):
                        t = 2 * u + i
                        for g in lanes:
                            part = g // LANES
                            r = PART_ROWS[part]
                            n = HEADS[g] * CTX
                            n += n % 2
                            last = mm(bks[g][:, i * GKE:i * GKE + n], q_hi[0:r, b, part, t * P:(t + 1) * P],
                                      keys_hi[0:r, b, g, 0:n], stop=layer > 0)
                            if i == 1 and layer > 0:
                                last.then_inc(filled, 1)
                        if layer == 0:
                            for g in lanes:
                                last = mm(bks[g][:, i * GKE:i * GKE + HEADS[g] * CTX].rearrange("p (h k) -> p h k", k=CTX),
                                          ident16[:, :],
                                          mask_b16[:, b, t, :].unsqueeze(1).broadcast_to([P, HEADS[g], CTX]), start=False)
                                if i == 1:
                                    last.then_inc(filled, 1)

            def max_rows(b, layer, part):
                r = PART_ROWS[part]
                bk = start_unit("max_t", layer, b, part)
                pe.wait_ge(max_ready[b], layer + 1)
                for t in range(T):
                    last = nc.tensor.transpose(
                        bk[0:r, t * P:(t + 1) * P],
                        mx[:, b, t, :, :].rearrange("p g e -> p (g e)")[:, part * P:part * P + r], ident)
                last.then_inc(filled, 1)

            def scores(b, layer, i):
                if i == 0:
                    pe.wait_ge(q_lo_ready[b], layer + 1)
                if i in (0, 2):
                    pe.wait_ge(*banks.emptied("max_t", layer, b, i // 2))
                if i == 0 and layer == 0:
                    pe.wait_ge(*banks.emptied("mask_t", b))
                    if b == 1:
                        pe.wait_ge(k_parts, 3)
                        pe.wait_ge(rounded_ready, 1)
                for g, j in SETS[i]:
                    bk = start_unit("p", layer, b, g, j)
                    part, r = g // LANES, ROWS[g, j]
                    k = PART_ROWS[part]
                    for n, (keys, queries) in enumerate(((keys_hi, q_lo), (keys_hi, q_hi), (keys_lo, q_hi))):
                        last = mm(bk[0:r, :], keys[0:k, b, g, j * P:j * P + r], queries[0:k, b, part, :], start=n == 0,
                                  stop=n == 2 and layer > 0)
                    if layer == 0:
                        last = mm(bk[0:r, :], key_of[:, j * P:j * P + r], mask_t[:, b, :], start=False)
                    last.then_inc(filled, 1)

            def values(b, layer, part):
                bk = start_unit("pv", layer, b, part)
                if part == 0:
                    pe.wait_ge(sums_placed, 1)
                    pe.wait_ge(*banks.emptied("vrows", layer, NJ - 1))
                    pe.wait_ge(*banks.emptied("p", layer, b, *SETS[1][-1]))
                else:
                    pe.wait_ge(*banks.emptied("p", layer, b, *SETS[2][-1]))
                for j in range(NJ):
                    for g in range(part * LANES, min(GROUPS, (part + 1) * LANES)):
                        if (g, j) in ROWS:
                            r = ROWS[g, j]
                            at_ = g % LANES * GR
                            last = mm(bk[at_:at_ + GR, :], v_cols[0:r, j, B * layer + b, g, :],
                                      wide[0:r, b, SLOT[g, j], :], start=j == 0, stop=(g, j + 1) not in ROWS)
                last.then_inc(filled, 1)

            def values_back(b, layer, u):
                bk = start_unit("o", layer, b, u)
                pe.wait_ge(*banks.emptied("pv", layer, b, 1))
                for i in range(2):
                    t = 2 * u + i
                    for part, r in enumerate(PART_ROWS):
                        at_ = i * GROUPS * GR + part * P
                        last = nc.tensor.transpose(bk[:, at_:at_ + r], q[0:r, b, part, t * P:(t + 1) * P],
                                                   ident[0:r, 0:r])
                last.then_inc(filled, 1)

            def out_turn(b, layer):
                bk = start_unit("o_t", layer, b)
                pe.wait_ge(*banks.emptied("o", layer, b, T // 2 - 1))
                for t in range(T):
                    last = nc.tensor.transpose(bk[:, t * P:(t + 1) * P], o[:, b, t, 0:D], ident)
                last.then_inc(filled, 1)

            def project(b, stage, layer):
                bk = start_unit("out", stage, b)
                pe.wait_ge(*banks.emptied("o_t", layer, b))
                for t in range(T):
                    last = mm(bk[:, t * P:(t + 1) * P], o_t[:, b, t * P:(t + 1) * P], w(f"attn{layer}", "wo"))
                last.then_inc(filled, 1)

            def sum_chunks(bk, b, weights, chunks, source, stop=True):
                for i, (at_, n) in enumerate(chunks):
                    pe.wait_ge(*banks.emptied(source, b, i))
                    last = mm(bk, weights[0:n, i * D:(i + 1) * D], wide[0:n, b, at_, :], start=i == 0,
                              stop=stop and i == len(chunks) - 1)
                return last

            def back(b, stage):
                pairs = [("s_out", ("s_y", b), s_y_t)] if stage == 3 else []
                for name, source, tile in pairs + [("out", ("y", stage, b), y_t)]:
                    bk = start_unit(name, *([stage] if name == "out" else []), b)
                    pe.wait_ge(*banks.emptied(*source))
                    for t in range(T):
                        last = nc.tensor.transpose(bk[:, t * P:(t + 1) * P], tile[:, b, t * P:(t + 1) * P], ident)
                    last.then_inc(filled, 1)

            def hidden0(b, m):
                bk = start_unit("h0", b, m)
                if m == 0:
                    pe.wait_ge(loaded["ffn0"], 16)
                    pe.wait_ge(*banks.emptied("xn_t", 1, b))
                mm(bk, w("ffn0", "w1")[:, m * P:(m + 1) * P], xn_t[:, b, :]).then_inc(filled, 1)

            def down0(b):
                bk = start_unit("y", 1, b)
                sum_chunks(bk, b, w("ffn0", "w2"), [(m, P) for m in range(C0)], "h0").then_inc(filled, 1)

            def gates1(b):
                bk = start_unit("gates1", b)
                pe.wait_ge(loaded["ffn1"], 16)
                pe.wait_ge(*banks.emptied("xn_t", 3, b))
                for t in range(T):
                    last = mm(bk[:, t * (E1 + 1):(t + 1) * (E1 + 1)], xn_t[:, b, t * P:(t + 1) * P],
                              w("ffn1", "gates"))
                last.then_inc(filled, 1)

            def shared(b, i):
                lo, n = SHC[i]
                for name in ("s_g", "s_u"):
                    bk = start_unit(name, b, i)
                    mm(bk[0:n, :], w("ffn1", name)[:, lo:lo + n], xn_t[:, b, :]).then_inc(filled, 1)

            def weights_turn(b):
                bk = start_unit("comb_t", b)
                pe.wait_ge(comb_ready[b], 1)
                for t in range(T):
                    last = nc.tensor.transpose(bk[0:2 * E1, t * P:(t + 1) * P], comb[:, b, t, :].bitcast(F32), ident)
                last.then_inc(filled, 1)

            def experts(b, c):
                for name, weights in (("e_g", "w_g"), ("e_u", "w_u")):
                    bk = start_unit(name, b, c)
                    mm(bk, w("ffn1", weights)[:, c * P:(c + 1) * P], xn_t[:, b, :]).then_inc(filled, 1)

            def weigh(b, c):
                bk = start_unit("e_w", b, c)
                if c == 0:
                    pe.wait_ge(rounded_ready, 1)
                    pe.wait_ge(zeros_made, 1)
                    pe.wait_ge(*banks.emptied("comb_t", b))
                mm(bk, sel1[:, c * P:(c + 1) * P], comb_t[:, b, :]).then_inc(filled, 1)

            def down1(b):
                bk = start_unit("s_y", b)
                sum_chunks(bk, b, w("ffn1", "s_down"), [(C1 + i, n) for i, (_, n) in enumerate(SHC)], "s_u")\
                    .then_inc(filled, 1)
                bk = start_unit("y", 3, b)
                sum_chunks(bk, b, w("ffn1", "w_down"), [(c, P) for c in range(C1)], "e_w").then_inc(filled, 1)

            def router(b):
                bk = start_unit("router", b)
                pe.wait_ge(loaded["ffn2"], 16)
                pe.wait_ge(*banks.emptied("xn_t", 5, b))
                for t in range(T):
                    last = mm(bk[:, t * E2:(t + 1) * E2], xn_t[:, b, t * P:(t + 1) * P], w("ffn2", "router"))
                last.then_inc(filled, 1)

            def choice_turn(b):
                bk = start_unit("hot_t", b)
                pe.wait_ge(hot_ready[b], 1)
                for t in range(T):
                    last = nc.tensor.transpose(bk[0:E2, t * P:(t + 1) * P], route[:, b, 3, t, :], ident)
                last.then_inc(filled, 1)

            def hidden2(b, c):
                bk = start_unit("h2", b, c)
                if c == 0:
                    pe.wait_ge(loaded["ffn2"], 16)
                    pe.wait_ge(*banks.emptied("xn_t", 5, b))
                mm(bk, w("ffn2", "w1")[:, c * P:(c + 1) * P], xn_t[:, b, :], stop=False)

            def choose(b, c):
                if c == 0:
                    pe.wait_ge(nothot_ready[b], 1)
                mm(banks.bank("h2", b, c), sel2[:, c * P:(c + 1) * P], nothot_t[:, b, :], start=False).then_inc(filled, 1)

            def down2(b):
                bk = start_unit("y", 5, b)
                sum_chunks(bk, b, w("ffn2", "w2"), [(c, P) for c in range(C2)], "h2", stop=False)
                mm(bk, w("ffn2", "bias2")[0:E2, :], hot_t[:, b, :], start=False).then_inc(filled, 1)

            def square(b, it):
                bk = start_unit("ss", it, b)
                pe.wait_ge(sq_ready[b], it + 1)
                for t in range(T):
                    last = mm(bk[:, t:t + 1], sq[:, b, t * P:(t + 1) * P], ones[:, 1:2])
                last.then_inc(filled, 1)

            def hidden_gate(b, it, name):
                i = {"r": 0, "z": 1, "hn": 2}[name]
                bk = start_unit(name, it, b)
                if it == 0:
                    pe.wait_ge(*banks.emptied("xn_t", 6, b))
                else:
                    pe.wait_ge(slots_ready[b], it)
                last = mm(bk, w("attn3", "wh")[:, i * D:(i + 1) * D], slots_t[:, b, :], stop=name == "hn")
                if name == "hn":
                    last.then_inc(filled, 1)

            def slot_products(b, it):
                bk = start_unit("s", it, b)
                if it == 0:
                    pe.wait_ge(*banks.emptied("kq"))
                mm(bk[0:CTX, :], kq[:, b * CTX:(b + 1) * CTX], slots_t[:, b, :]).then_inc(filled, 1)

            def slot_scores(b, it):
                bk = start_unit("rstd_b", it, b)
                pe.wait_ge(rstd_ready[b], it + 1)
                for t in range(T):
                    last = mm(bk[0:CTX, t * P:(t + 1) * P], nw[:, b, 2, t:t + 1].broadcast_to([P, CTX]), ident)
                last.then_inc(filled, 1)

            def slot_sums(b, it):
                bk = start_unit("asum", it, b)
                pe.wait_ge(slot_inverse_ready[b], it + 1)
                for t in range(T):
                    last = mm(bk[:, t:t + 1], ex[0:CTX, b, t * P:(t + 1) * P], nmax[:, b, 2:3])
                last.then_inc(filled, 1)

            def slot_weights(b, it):
                bk = start_unit("ra_b", it, b)
                keep_warm(bk, "slot_weights")
                pe.wait_ge(ra_ready[b], it + 1)
                for t in range(T):
                    last = mm(bk[0:CTX, t * P:(t + 1) * P], route_s[:, b, 1, t:t + 1].broadcast_to([P, CTX]), ident)
                last.then_inc(filled, 1)

            def gru(b, it):
                update = lambda i: (vw[:, b, i * D:(i + 1) * D], an[0:CTX, b, :])
                if it == 0:
                    pe.wait_ge(*banks.emptied("vw", B - 1))
                bk = start_unit("n", it, b)
                keep_warm(bk, "gru")
                pe.wait_ge(*banks.emptied("ra_b", it, b))
                mm(banks.bank("r", it, b), *update(0), start=False).then_inc(filled, 1)
                mm(bk, *update(2)).then_inc(filled, 1)

            def gru_z(b, it):
                mm(banks.bank("z", it, b), vw[:, b, D:2 * D], an[0:CTX, b, :], start=False).then_inc(filled, 1)

            def slots_back(b):
                bk = start_unit("out", 6, b)
                keep_warm(bk, "slots_back")
                pe.wait_ge(slots_ready[b], ITERS)
                for t in range(T):
                    last = nc.tensor.transpose(bk[:, t * P:(t + 1) * P], slots_t[:, b, t * P:(t + 1) * P], ident)
                last.then_inc(filled, 1)

            def quantised(b):
                bk = start_unit("out", 7, b)
                keep_warm(bk, "quantised")
                pe.wait_ge(*banks.emptied("rq_t"))
                pe.wait_ge(*banks.emptied("xn_t", 7, b))
                for t in range(T):
                    last = mm(bk[:, t * P:(t + 1) * P], lhs_q[:, b, t * P:(t + 1) * P], rhs_q[:, :])
                last.then_inc(filled, 1)

            mine = {"keys_in": keys_in, "values_in": values_in, "place": place, "masks": masks, "slots_in": slots_in,
                    "turn": turn, "query": query, "maxima": maxima, "max_rows": max_rows, "scores": scores, "values": values,
                    "values_back": values_back, "out_turn": out_turn, "project": project, "hidden0": hidden0, "down0": down0, "back": back,
                    "gates1": gates1, "shared": shared, "weights_turn": weights_turn, "experts": experts, "weigh": weigh,
                    "down1": down1, "router": router, "choice_turn": choice_turn, "hidden2": hidden2, "choose": choose,
                    "down2": down2, "hidden_gate": hidden_gate, "slot_products": slot_products, "square": square,
                    "slot_scores": slot_scores, "slot_sums": slot_sums,
                    "slot_weights": slot_weights, "gru": gru, "gru_z": gru_z, "slots_back": slots_back, "quantised": quantised}
            for phase, b, args in ORDERS["pe"]:
                mine[phase](b, *args)

        @block.scalar
        def _(act):
            A = nc.scalar
            steps = [0]

            def link(ins):
                steps[0] += 1
                ins.then_inc(act_step, 1)
                act.wait_ge(act_step, steps[0])

            def empty(dst, fn, name, rows_=P, cols_=512, **kw):
                act.wait_ge(*banks.full(*name))
                A.activation(dst, banks.bank(*name)[0:rows_, 0:cols_], fn, **kw).then_inc(drained["act"], 1)

            def keys_out(layer):
                act.wait_ge(*banks.full("k", layer))
                for part, r in enumerate(PART_ROWS):
                    last = A.activation(k_t[0:r, layer, part, :, :].rearrange("p b k -> p (b k)"),
                                        banks.bank("k", layer)[0:r, part * B * CTX:(part + 1) * B * CTX],
                                        ACT.Identity, bias=col(f"bk{layer}", part)[0:r, :])
                last.then_inc(drained["act"], 1)

            def round_(name, dst):
                lo, hi = rounded_at[name]
                A.activation(dst[:, :], rounded_in[:, lo:hi], ACT.Copy).then_inc(rounded_ready, 1)

            def keys_in(b, layer):
                if layer == 0:
                    act.wait_ge(loaded["cols"], 16)
                keys_out(layer)
                if layer == 0:
                    act.wait_ge(loaded["rows"], 16)
                    A.activation(gain[:, :], row("g"), ACT.Tanh).then_inc(gain_ready, 1)

            def masks(b):
                for i in range(B):
                    empty(mask_t[:, i, :], ACT.Copy, ("mask_t", i), CTX)
                act.wait_ge(loaded["rounded"], 16)
                round_("sel1", sel1)

            def slots_in(b, i):
                if i == 0:
                    for i in range(2):
                        A.activation(half_bias[:, i:i + 1], col("bi", i), ACT.Identity, bias=col("bh", i))
                    link(A.activation(half_bias[:, 2:3], col("bh", 2), ACT.Identity, scale=0.5))
                    link(A.activation(half_bias[:, 0:2], half_bias[:, 0:2], ACT.Identity, scale=0.5))
                    act.wait_ge(loaded["ctx_rows"], 16)
                    for i in range(B):
                        last = A.activation(pn[:, i, :], ctx_rows[:, i, :], ACT.Square, accum_out=p_ss[:, i:i + 1])
                    last.then_inc(p_ss_ready, 1)
                elif i == 1:
                    empty(pn_t[:, :], ACT.Copy, ("pn_t",), cols_=B * CTX, scale=col("w_in"))
                elif i == 2:
                    empty(kproj[:, :], ACT.Copy, ("kproj",), cols_=B * CTX)
                    empty(vproj[:, :], ACT.Copy, ("vproj",), cols_=B * CTX)
                elif i == 3:
                    for i in range(B):
                        empty(vw[:, i, :], ACT.Copy, ("vw", i), CTX, 3 * D)
                else:
                    empty(rscale_b[:, :], ACT.Copy, ("rscale",), cols_=D)

            def turn(b, stage):
                if stage < 7:
                    empty((slots_t if stage == 6 else xn_t)[:, b, :], ACT.Copy, ("xn_t", stage, b))

            def query(b, layer):
                for part, r in enumerate(PART_ROWS):
                    act.wait_ge(*banks.full("q", layer, b, part))
                    A.activation(q_hi[0:r, b, part, :], banks.bank("q", layer, b, part)[0:r, :], ACT.Identity,
                                 bias=col(f"bq{layer}", part)[0:r, :]).then_inc(q_parts[b], 1)
                for part, r in enumerate(PART_ROWS):
                    empty(q[0:r, b, part, :], ACT.Identity, ("q", layer, b, part), r,
                          bias=col(f"bq{layer}", part)[0:r, :])

            def scores(b, layer, i):
                for g, j in SETS[i]:
                    r = ROWS[g, j]
                    empty(wide[0:r, b, SLOT[g, j], :], ACT.Exp, ("p", layer, b, g, j), r, scale=DH ** -0.5)

            def values(b, layer, part):
                r = PART_ROWS[part]
                empty(q[0:r, b, part, :], ACT.Copy, ("pv", layer, b, part), r)

            def out_turn(b, layer):
                empty(o_t[:, b, :], ACT.Copy, ("o_t", layer, b))

            def hidden0(b, m):
                if m % 2:
                    empty(wide[:, b, m, :], ACT.Relu, ("h0", b, m), bias=col("b1", m))

            def down0(b):
                empty(y_t[:, b, :], ACT.Copy, ("y", 1, b))

            def gates1(b):
                act.wait_ge(gap_ready[b], 1)
                A.activation(route_s[:, b, 4, :], route_s[:, b, 3, :], ACT.Exp)
                A.activation(route_s[:, b, 7, :], lg[:, b, :, E1], ACT.Tanh, scale=0.5).then_inc(second_ready[b], 1)

            users = [[] for _ in range(B)]

            def silu(b, r, source, user):
                if len(users[b]) >= 2:
                    act.wait_ge(*banks.emptied(*users[b][-2]))
                empty(act_s[len(users[b]) % 2][0:r, b, :], ACT.Silu, source, r)
                users[b].append(user)

            def shared(b, i):
                silu(b, SHC[i][1], ("s_g", b, i), ("s_u", b, i))

            def experts(b, c):
                silu(b, P, ("e_g", b, c), ("e_u", b, c))

            def weights_turn(b):
                empty(comb_t[0:2 * E1, b, :], ACT.Copy, ("comb_t", b), 2 * E1)

            def down1(b):
                empty(s_y_t[:, b, :], ACT.Copy, ("s_y", b))
                empty(y_t[:, b, :], ACT.Copy, ("y", 3, b))

            def choice_turn(b):
                empty(hot_t[:, b, :], ACT.Copy, ("hot_t", b), E2)

            def choose(b, c):
                if c % 2:
                    empty(wide[:, b, c, :], ACT.Relu, ("h2", b, c), bias=col("bias1", c))

            def down2(b):
                empty(y_t[:, b, :], ACT.Relu, ("y", 5, b))

            def square(b, it):
                if it == 0:
                    act.wait_ge(*banks.emptied("xn_t", 6, b))
                else:
                    act.wait_ge(slots_ready[b], it)
                A.activation(sq[:, b, :], slots_t[:, b, :], ACT.Square).then_inc(sq_ready[b], 1)

            def slot_products(b, it):
                empty(ss[0:CTX, b, :], ACT.Copy, ("s", it, b), CTX)

            def slot_scores(b, it):
                act.wait_ge(nmax_ready[b], it + 1)
                A.activation(ex[0:CTX, b, :], sc[0:CTX, b, :], ACT.Exp, bias=nmax[:, b, 0:1],
                             accum_out=nmax[:, b, 1:2]).then_inc(ex_ready[b], 1)

            def hidden_gate(b, it, name):
                if name == "hn":
                    empty(hnb[:, b, :], ACT.Identity, ("hn", it, b), bias=half_bias[:, 2:3], scale=0.5)

            def gru(b, it):
                empty(tr[:, b, :], ACT.Tanh, ("r", it, b), bias=half_bias[:, 0:1], scale=0.5)

            def gru_z(b, it):
                empty(tz[:, b, :], ACT.Tanh, ("z", it, b), bias=half_bias[:, 1:2], scale=0.5)

            def gru_end(b, it):
                act.wait_ge(*banks.emptied("n", it, b))
                A.activation(nn[:, b, :], tt[:, b, :], ACT.Tanh, bias=col("bi", 2)).then_inc(n_ready[b], 1)

            mine = {"keys_in": keys_in, "masks": masks, "slots_in": slots_in, "turn": turn,
                    "query": query, "scores": scores, "values": values, "out_turn": out_turn,
                    "hidden0": hidden0, "down0": down0, "gates1": gates1, "shared": shared,
                    "weights_turn": weights_turn, "experts": experts, "down1": down1, "choice_turn": choice_turn,
                    "choose": choose, "down2": down2, "square": square, "slot_scores": slot_scores, "gru": gru, "gru_z": gru_z,
                    "hidden_gate": hidden_gate, "slot_products": slot_products, "gru_end": gru_end}
            for phase, b, args in ORDERS["act"]:
                mine[phase](b, *args)

        @block.vector
        def _(dve):
            V = nc.vector
            steps = [0]

            def link(ins):
                steps[0] += 1
                ins.then_inc(dve_step, 1)
                dve.wait_ge(dve_step, steps[0])

            def norm(b, stage):
                if stage == 0:
                    dve.wait_ge(loaded["x"], 16 * B)
                for t in range(T):
                    last = V.bn_stats(stats[:, b, t, :], x[:, b, t, :])
                link(last)
                for t in range(T):
                    last = V.bn_aggr(mv[:, b, t, :], stats[:, b, t, :])
                last.then_inc(var_ready[b], 1)

            def norm_end(b, stage):
                dve.wait_ge(xn_rstd_ready[b], stage + 1)
                for t in range(T):
                    last = V.tensor_scalar(xn[:, b, t, :], x[:, b, t, :], mv[:, b, t, 0:1], nw[:, b, 2, t:t + 1],
                                           ALU.subtract, ALU.mult)
                    if stage < 7:
                        last.then_inc(xn_ready[b], 1)
                if stage < 7:
                    return
                link(last)
                amax, scale, inverse = (route_s[:, b, i, :] for i in (2, 3, 4))
                link(V.tensor_reduce(amax, xn[:, b, :, :], AX.X, ALU.max, apply_absolute_value=True))
                link(V.tensor_scalar(scale, amax, 1e-12, 1.0 / 127.0, ALU.max, ALU.mult))
                link(V.reciprocal(inverse, scale))
                for t in range(T):
                    last = V.tensor_scalar(y[:, b, t, :], xn[:, b, t, :], inverse[:, t:t + 1], ROUND, ALU.mult, ALU.add)
                link(last)
                V.tensor_scalar(y[:, b, :, :], y[:, b, :, :], ROUND, 127.0, ALU.subtract, ALU.min)\
                 .then_inc(xn_ready[b], T)

            def flat(tile):
                return tile.rearrange("p t d -> p (t d)")

            def add_out(b, stage):
                dve.wait_ge(*banks.full("out", stage, b))
                if stage in BIASED:
                    dve.wait_ge(bias_added[b], BIASED[stage] + 1)
                g = GAIN_OF[stage]
                V.scalar_tensor_tensor(flat(x[:, b, :, :]), banks.bank("out", stage, b), gain[:, g:g + 1],
                                       flat(x[:, b, :, :]), ALU.mult, ALU.add).then_inc(drained["dve"], 1)
                dve.wait_ge(*banks.emptied("out", stage, b))

            def split_keys(layer):
                dve.wait_ge(*banks.emptied("k", layer))
                for part, r in enumerate(PART_ROWS):
                    last = V.tensor_copy(k_hi[0:r, layer, part, :, :], k_t[0:r, layer, part, :, :])
                link(last)
                for part, r in enumerate(PART_ROWS):
                    last = V.tensor_tensor(k_lo[0:r, layer, part, :, :], k_t[0:r, layer, part, :, :],
                                           k_hi[0:r, layer, part, :, :].bitcast(F32), ALU.subtract)
                last.then_inc(k_parts, 1)

            def keys_in(b, layer):
                split_keys(layer)
                if layer == 0:
                    dve.wait_ge(loaded["consts"], 16)
                    for i in range(B):
                        spread_keys(V, i, 0, k_hi, keys_hi)

            def mask_parts(b):
                dve.wait_ge(loaded["mask"], 16)
                for i in range(B):
                    V.tensor_scalar(mask_b16[:, i, :, :], mask_i[:, i, :, :], 0.0, MASKED, ALU.is_equal, ALU.mult)
                    V.tensor_scalar(mask_b[:, i, :, :], mask_i[:, i, :, :], 0.0, MASKED, ALU.is_equal, ALU.mult)\
                     .then_inc(mask_b_ready, 1)
                dve.wait_ge(loaded["rows"], 16)
                dve.wait_ge(gain_ready, 1)
                for i, (name, stage) in enumerate((("bo0", 0), ("b2", 1), ("bo1", 2), ("bo2", 4))):
                    g = GAIN_OF[stage]
                    last = V.tensor_scalar(gbias[:, i, :], row(name), gain[:, g:g + 1], None, ALU.mult)
                last.then_inc(gbias_ready, 1)

            def values_in(b, layer):
                dve.wait_ge(*banks.full("v", layer))
                rest = v_rows[:, layer, :, :]
                V.tensor_tensor(rest, banks.bank("v", layer)[0:CTX, 0:B * D].rearrange("p (b d) -> p b d", b=B),
                                row(f"bv{layer}")[0:CTX, :].unsqueeze(1).broadcast_to([CTX, B, D]), ALU.add)\
                 .then_inc(drained["dve"], 1)
                dve.wait_ge(*banks.emptied("v", layer))
                for part in range(3):
                    piece = v_parts[:, part, layer, :, :]
                    if part == 2:
                        V.tensor_copy(piece, rest).then_inc(v_parts_ready, 1)
                    else:
                        link(V.tensor_copy(piece, rest))
                        link(V.tensor_tensor(rest, rest, piece, ALU.subtract))

            def place(b, layer):
                masks_ = const("chunk_mask").rearrange("p (j h) -> p j h", j=NJ)
                if layer == 0:
                    dve.wait_ge(zeros_made, 1)
                    for j in range(NJ):
                        V.tensor_copy(v_cols[:, j, :, 0:GROUPS - 1, VALUES:VALUES + G3],
                                      masks_[:, j:j + 1, :].unsqueeze(1).broadcast_to([P, 3 * B, GROUPS - 1, G3]))
                    V.tensor_copy(v_cols[:, 0, :, GROUPS - 1, VALUES:VALUES + G3],
                                  masks_[:, 0:1, 0:1].broadcast_to([P, 3 * B, G3])).then_inc(sums_placed, 1)
                at_ = B * layer
                for j in range(NJ):
                    dve.wait_ge(*banks.full("vrows", layer, j))
                    bk = banks.bank("vrows", layer, j)[:, 0:B * D].rearrange("p (b h d) -> p b h d", b=B, h=H)
                    for h in range(G3):
                        last = V.tensor_scalar(
                            v_cols[:, j, at_:at_ + B, 0:len(range(h, H, G3)), h * DH:(h + 1) * DH], bk[:, :, h::G3, :],
                            masks_[:, j, h:h + 1], None, ALU.mult)
                    last.then_inc(drained["dve"], 1)

            def slots_in(b, i):
                if i == 0:
                    dve.wait_ge(p_ss_ready, 1)
                    link(V.tensor_scalar(p_small[:, 0, :], p_ss[:, :], 1.0 / D, RMS_EPS, ALU.mult, ALU.add))
                    v, hv, r, t = (p_small[:, i, :] for i in range(4))
                    V.tensor_scalar(r.bitcast(I32), v.bitcast(I32), -0.5, 1597463007.0, ALU.mult, ALU.add)
                    link(V.tensor_scalar(hv, v, -0.5, None, ALU.mult))
                    for i in range(3):
                        link(V.tensor_tensor(t, r, r, ALU.mult))
                        link(V.tensor_tensor(t, t, hv, ALU.mult))
                        link(V.scalar_tensor_tensor(r, t, 1.5, r, ALU.add, ALU.mult))
                    for i in range(B):
                        last = V.tensor_scalar(pn[:, i, :], ctx_rows[:, i, :], p_small[:, 2, i:i + 1], None, ALU.mult)
                    last.then_inc(pn_ready, 1)
                elif i == 2:
                    dve.wait_ge(loaded["attn3"], 16)
                    link(V.tensor_reduce(rscale[:, 0:1], w("attn3", "rhs_t"), AX.X, ALU.max, apply_absolute_value=True))
                    link(V.tensor_scalar(rscale[:, 1:2], rscale[:, 0:1], 1e-12, 1.0 / 127.0, ALU.max, ALU.mult))
                    link(V.reciprocal(rscale[:, 2:3], rscale[:, 1:2]))
                    link(V.tensor_scalar(rq[:, :], w("attn3", "rhs_t"), rscale[:, 2:3], ROUND, ALU.mult, ALU.add))
                    V.tensor_scalar(rq[:, :], rq[:, :], ROUND, 127.0, ALU.subtract, ALU.min).then_inc(rq_ready, 1)
                elif i == 3:
                    dve.wait_ge(*banks.full("kq"))
                    V.tensor_scalar(kq[:, :], banks.bank("kq")[:, 0:B * CTX], col("w_slot"), D ** -0.5, ALU.mult,
                                    ALU.mult).then_inc(drained["dve"], 1)
                elif i == 4:
                    dve.wait_ge(*banks.full("rq_t"))
                    V.tensor_scalar(rhs_q[:, :], banks.bank("rq_t")[:, 0:D], -127.0, None, ALU.max)\
                     .then_inc(drained["dve"], 1)

            def maxima(b, layer, u):
                if b == 0 and layer == 0 and u == 0:
                    dve.wait_ge(consts_made, 1)
                for g in range(GROUPS):
                    dve.wait_ge(*banks.full("max", layer, b, u, g))
                    n = HEADS[g]
                    V.tensor_reduce(mx_raw[:, b, 2 * u:2 * u + 2, g, 0:n],
                                    banks.bank("max", layer, b, u, g)[:, 0:2 * GKE]
                                    .rearrange("p (t k) -> p t k", t=2)[:, :, 0:n * CTX]
                                    .rearrange("p t (h k) -> p t h k", k=CTX), AX.X, ALU.max)\
                     .then_inc(drained["dve"], 1)

            def max_parts(b, layer):
                dve.wait_ge(*banks.emptied("max", layer, b, T // 2 - 1, GROUPS - 1))
                link(V.tensor_copy(mx_hi[:, b, :, :, :], mx_raw[:, b, :, :, :]))
                V.tensor_copy(mx[:, b, :, :, VALUES:VALUES + G3], mx_hi[:, b, :, :, :].bitcast(F32))
                V.tensor_tensor(mx[:, b, :, :, VALUES + G3:VALUES + 2 * G3], mx_raw[:, b, :, :, :],
                                mx_hi[:, b, :, :, :].bitcast(F32), ALU.subtract).then_inc(max_ready[b], 1)

            def max_rows(b, layer, part):
                r = PART_ROWS[part]
                dve.wait_ge(q_lo_ready[b], layer + 1)
                dve.wait_ge(*banks.full("max_t", layer, b, part))
                V.tensor_tensor(q_hi[0:r, b, part, :], q_hi[0:r, b, part, :].bitcast(F32),
                                banks.bank("max_t", layer, b, part)[0:r, :], ALU.add).then_inc(drained["dve"], 1)

            def values_back(b, layer, u):
                dve.wait_ge(*banks.full("o", layer, b, u))
                both = banks.bank("o", layer, b, u)[:, 0:2 * GROUPS * GR].rearrange("p (t g e) -> p t g e", t=2, e=GR)
                link(V.reciprocal(rsum[:, b, 2 * u:2 * u + 2, :, :], both[:, :, :, VALUES:VALUES + G3]))
                for i in range(2):
                    t = 2 * u + i
                    last = V.tensor_tensor(o[:, b, t, :].rearrange("p (g h d) -> p g h d", g=GROUPS, h=G3),
                                           both[:, i, :, 0:VALUES].rearrange("p g (h d) -> p g h d", h=G3),
                                           rsum[:, b, t, :, :].unsqueeze(3).broadcast_to([P, GROUPS, G3, DH]), ALU.mult)
                last.then_inc(drained["dve"], 1)

            def project(b, stage, layer):
                add_out(b, stage)

            def hidden0(b, m):
                if m % 2 == 0:
                    dve.wait_ge(*banks.full("h0", b, m))
                    V.tensor_scalar(wide[:, b, m, :], banks.bank("h0", b, m), col("b1", m), 0.0, ALU.add, ALU.max)\
                     .then_inc(drained["dve"], 1)

            def largest(b, logits, n, top, ids, rev):
                link(V.tensor_reduce(top, logits, AX.X, ALU.max))
                eq, order = route[:, b, 0, :, 0:n], route[:, b, 1, :, 0:n]
                first = route_s[:, b, 1, :]
                link(V.tensor_tensor(eq, logits, top.unsqueeze(2).broadcast_to([P, T, n]), ALU.is_equal))
                link(V.tensor_tensor(order, eq, rev, ALU.mult))
                link(V.tensor_reduce(first, order, AX.X, ALU.max))
                return V.tensor_tensor(ids, rev, first.unsqueeze(2).broadcast_to([P, T, n]), ALU.is_equal)

            def gates1(b):
                rev = const("rev16").unsqueeze(1).broadcast_to([P, T, E1])
                dve.wait_ge(*banks.full("gates1", b))
                V.tensor_copy(lg[:, b, :, 0:E1 + 1],
                              banks.bank("gates1", b)[:, 0:T * (E1 + 1)].rearrange("p (t e) -> p t e", t=T))\
                 .then_inc(drained["dve"], 1)
                dve.wait_ge(*banks.emptied("gates1", b))
                logits = lg[:, b, :, 0:E1]
                top, second, gap = (route_s[:, b, i, :] for i in (0, 2, 3))
                one, two, rest = (route[:, b, i, :, 0:E1] for i in (2, 3, 4))
                link(largest(b, logits, E1, top, one, rev))
                link(V.scalar_tensor_tensor(rest, one, -3e38, logits, ALU.mult, ALU.add))
                link(largest(b, rest, E1, second, two, rev))
                V.tensor_tensor(gap, second, top, ALU.subtract).then_inc(gap_ready[b], 1)

            def weights_turn(b):
                e2, w1_, w2_, shared_ = (route_s[:, b, i, :] for i in (4, 5, 6, 7))
                one, two, rest = (route[:, b, i, :, 0:E1] for i in (2, 3, 4))
                dve.wait_ge(second_ready[b], 1)
                link(V.tensor_scalar(w2_, e2, 1.0, None, ALU.add))
                link(V.reciprocal(w1_, w2_))
                link(V.tensor_tensor(w2_, e2, w1_, ALU.mult))
                V.tensor_tensor(one, one, w1_.unsqueeze(2).broadcast_to([P, T, E1]), ALU.mult)
                link(V.tensor_tensor(two, two, w2_.unsqueeze(2).broadcast_to([P, T, E1]), ALU.mult))
                link(V.tensor_tensor(rest, one, two, ALU.add))
                link(V.tensor_copy(comb[:, b, :, 0:E1], rest))
                V.tensor_tensor(comb[:, b, :, E1:2 * E1], rest, comb[:, b, :, 0:E1].bitcast(F32), ALU.subtract)\
                 .then_inc(comb_ready[b], 1)
                link(V.tensor_scalar(shared_, shared_, 0.5, 0.5, ALU.mult, ALU.add))
                link(V.tensor_scalar(shared_, shared_, gain[:, GAIN_OF[3]:GAIN_OF[3] + 1], None, ALU.mult))

            count = [0] * B

            def shared(b, i):
                r = SHC[i][1]
                dve.wait_ge(*banks.emptied("s_g", b, i))
                dve.wait_ge(*banks.full("s_u", b, i))
                V.tensor_tensor(wide[0:r, b, C1 + i, :], act_s[count[b] % 2][0:r, b, :], banks.bank("s_u", b, i)[0:r, :],
                                ALU.mult).then_inc(drained["dve"], 1)
                count[b] += 1

            def experts(b, c):
                slot = count[b] % 2
                dve.wait_ge(*banks.emptied("e_g", b, c))
                dve.wait_ge(*banks.full("e_u", b, c))
                V.tensor_tensor(wide[:, b, c, :], act_s[slot][:, b, :], banks.bank("e_u", b, c), ALU.mult)\
                 .then_inc(drained["dve"], 1)
                count[b] += 1

            def weigh(b, c):
                dve.wait_ge(*banks.emptied("e_u", b, c))
                dve.wait_ge(*banks.full("e_w", b, c))
                V.tensor_tensor(wide[:, b, c, :], wide[:, b, c, :], banks.bank("e_w", b, c), ALU.mult)\
                 .then_inc(drained["dve"], 1)

            def back(b, stage):
                if stage == 3:
                    dve.wait_ge(*banks.full("s_out", b))
                    for t in range(T):
                        last = V.scalar_tensor_tensor(x[:, b, t, :], banks.bank("s_out", b)[:, t * P:(t + 1) * P],
                                                      route_s[:, b, 7, t:t + 1], x[:, b, t, :], ALU.mult, ALU.add)
                    last.then_inc(drained["dve"], 1)
                    dve.wait_ge(*banks.emptied("s_out", b))
                add_out(b, stage)

            def router(b):
                rev = const("rev32").unsqueeze(1).broadcast_to([P, T, E2])
                dve.wait_ge(*banks.full("router", b))
                V.tensor_tensor(lg[:, b, :, :], banks.bank("router", b)[:, 0:T * E2].rearrange("p (t e) -> p t e", t=T),
                                row("router_b").unsqueeze(1).broadcast_to([P, T, E2]), ALU.add)\
                 .then_inc(drained["dve"], 1)
                dve.wait_ge(*banks.emptied("router", b))
                largest(b, lg[:, b, :, :], E2, route_s[:, b, 0, :], route[:, b, 3, :, :], rev)\
                    .then_inc(hot_ready[b], 1)

            def choice_turn(b):
                dve.wait_ge(*banks.emptied("hot_t", b))
                V.tensor_scalar(nothot_t[0:E2, b, :], hot_t[:, b, :], 1.0, -MASKED, ALU.subtract, ALU.mult)\
                 .then_inc(nothot_ready[b], 1)

            def choose(b, c):
                if c % 2 == 0:
                    dve.wait_ge(*banks.full("h2", b, c))
                    V.tensor_scalar(wide[:, b, c, :], banks.bank("h2", b, c), col("bias1", c), 0.0, ALU.add, ALU.max)\
                     .then_inc(drained["dve"], 1)

            def square(b, it):
                dve.wait_ge(*banks.full("ss", it, b))
                V.tensor_scalar(nw[:, b, 0, :], banks.bank("ss", it, b)[:, 0:T], RMS_EPS, None, ALU.add)\
                 .then_inc(drained["dve"], 1)

            def slot_scores(b, it):
                dve.wait_ge(*banks.full("rstd_b", it, b))
                dve.wait_ge(*banks.emptied("s", it, b))
                V.tensor_tensor(sc[0:CTX, b, :], ss[0:CTX, b, :], banks.bank("rstd_b", it, b)[0:CTX, :], ALU.mult)\
                 .then_inc(drained["dve"], 1)
                dve.wait_ge(*banks.emptied("rstd_b", it, b))
                V.tensor_reduce(nmax[:, b, 0:1], sc[0:CTX, b, :], AX.X, ALU.max, negate=True)\
                 .then_inc(nmax_ready[b], 1)

            def slot_inverse(b, it):
                dve.wait_ge(ex_ready[b], it + 1)
                V.reciprocal(nmax[:, b, 2:3], nmax[:, b, 1:2]).then_inc(slot_inverse_ready[b], 1)

            def slot_sums(b, it):
                dve.wait_ge(*banks.full("asum", it, b))
                V.tensor_scalar(route_s[:, b, 0, :], banks.bank("asum", it, b)[:, 0:T], RMS_EPS, None, ALU.add)\
                 .then_inc(drained["dve"], 1)
                dve.wait_ge(*banks.emptied("asum", it, b))
                V.reciprocal(route_s[:, b, 1, :], route_s[:, b, 0, :]).then_inc(ra_ready[b], 1)

            def slot_weights(b, it):
                dve.wait_ge(*banks.full("ra_b", it, b))
                V.scalar_tensor_tensor(an[0:CTX, b, :], ex[0:CTX, b, :], nmax[:, b, 2:3],
                                       banks.bank("ra_b", it, b)[0:CTX, :], ALU.mult, ALU.mult)\
                 .then_inc(drained["dve"], 1)

            def gru(b, it):
                dve.wait_ge(*banks.emptied("r", it, b))
                link(V.scalar_tensor_tensor(tt[:, b, :], tr[:, b, :], 1.0, hnb[:, b, :], ALU.add, ALU.mult))
                dve.wait_ge(*banks.full("n", it, b))
                V.tensor_tensor(tt[:, b, :], tt[:, b, :], banks.bank("n", it, b), ALU.add)\
                 .then_inc(drained["dve"], 1)

            def gru_z(b, it):
                dve.wait_ge(*banks.emptied("z", it, b))
                link(V.tensor_scalar(zs[:, b, :], tz[:, b, :], 0.5, 0.5, ALU.mult, ALU.add))
                link(V.tensor_tensor(zs[:, b, :], zs[:, b, :], slots_t[:, b, :], ALU.mult))

            def gru_end(b, it):
                dve.wait_ge(n_ready[b], it + 1)
                link(V.scalar_tensor_tensor(dd[:, b, :], tz[:, b, :], 1.0, nn[:, b, :], ALU.subtract, ALU.mult))
                V.scalar_tensor_tensor(slots_t[:, b, :], dd[:, b, :], -0.5, zs[:, b, :], ALU.mult, ALU.add)\
                 .then_inc(slots_ready[b], 1)

            def slots_back(b):
                add_out(b, 6)

            def turn(b, stage):
                if stage == 7:
                    dve.wait_ge(*banks.full("xn_t", 7, b))
                    V.tensor_scalar(lhs_q[:, b, :], banks.bank("xn_t", 7, b), -127.0, None, ALU.max)\
                     .then_inc(drained["dve"], 1)

            def quantised(b):
                g = GAIN_OF[7]
                dve.wait_ge(*banks.emptied("rscale"))
                dve.wait_ge(*banks.full("out", 7, b))
                for t in range(T):
                    last = V.scalar_tensor_tensor(xn[:, b, t, :], banks.bank("out", 7, b)[:, t * P:(t + 1) * P],
                                                  route_s[:, b, 3, t:t + 1], rscale_b[:, :], ALU.mult, ALU.mult)
                last.then_inc(drained["dve"], 1)
                dve.wait_ge(*banks.emptied("out", 7, b))
                V.scalar_tensor_tensor(flat(x[:, b, :, :]), flat(xn[:, b, :, :]), gain[:, g:g + 1],
                                       flat(x[:, b, :, :]), ALU.mult, ALU.add).then_inc(x_final[b], 1)

            mine = {"norm": norm, "norm_end": norm_end, "keys_in": keys_in, "mask_parts": mask_parts, "values_in": values_in,
                    "place": place, "slots_in": slots_in, "maxima": maxima, "max_parts": max_parts, "max_rows": max_rows, "values_back": values_back, "project": project,
                    "hidden0": hidden0, "back": back, "gates1": gates1, "weights_turn": weights_turn,
                    "shared": shared, "experts": experts, "weigh": weigh, "router": router, "choice_turn": choice_turn,
                    "choose": choose, "square": square, "slot_scores": slot_scores, "slot_inverse": slot_inverse, "slot_sums": slot_sums,
                    "slot_weights": slot_weights, "gru": gru, "gru_z": gru_z, "gru_end": gru_end, "slots_back": slots_back,
                    "turn": turn, "quantised": quantised}
            for phase, b, args in ORDERS["dve"]:
                mine[phase](b, *args)



def _constants():
    part = np.arange(P)
    row_ = part % GR
    pair = np.arange(NJ * P)
    head, key = pair // CTX, pair % CTX
    real = pair < GK
    out = {
        "ident": np.eye(P),
        "head_mask": np.stack([(part // GR == g % LANES)
                               & ((row_ < VALUES) & (row_ // DH == h) | (row_ == VALUES + h) | (row_ == VALUES + G3 + h))
                               for g in range(GROUPS) for h in range(G3)], 1),
        "chunk_mask": np.stack([(head == h) & real for h in range(G3)], 1).reshape(NJ, P, G3).transpose(1, 0, 2),
        "rev16": np.broadcast_to(E1 - np.arange(E1), (P, E1)),
        "rev32": np.broadcast_to(E2 - np.arange(E2), (P, E2)),
        "key_of": (part[:, None] == key[None, :]) & real[None, :],
        "sel1": (part[:, None] < 2 * E1) & (part[:, None] % E1 == np.arange(C1 * P)[None, :] // F1),
        "sel2": part[:, None] == np.arange(C2 * P)[None, :] // F2,
    }
    out["ident16"] = out["ident"]

    def pack(names):
        return np.concatenate([np.asarray(out[name], np.float32).reshape(P, n) for name, n in names], 1)

    def bits(m):
        return np.where(m == 0, 0, 0x3F80).astype(np.uint16)

    return {"consts": pack(CONSTS), "rounded": bits(pack(ROUNDED)), "halves": bits(pack(HALVES))}



def _side_by_side(m, n=P):
    k = -(-m.shape[0] // n)
    full = np.zeros((k * n,) + m.shape[1:], m.dtype)
    full[:m.shape[0]] = m
    return full.reshape(k, n, -1).transpose(1, 0, 2).reshape(n, -1)


def _layout(i):
    heads = lambda m: np.tile(m, (1, H))
    column = lambda v: np.reshape(v, (-1, P)).T
    filled = lambda m, n: np.concatenate([m, np.zeros(m.shape[:-1] + (n - m.shape[-1],), m.dtype)], -1)

    def grouped(m, rest=0.0):
        m = filled(m, GROUPS * VALUES).reshape(m.shape[:-1] + (GROUPS, VALUES))
        m = np.concatenate([m, np.full(m.shape[:-1] + (2 * G3,), rest, m.dtype)], -1)
        return filled(m, GR).reshape(m.shape[:-2] + (GROUPS * GR,))

    def group_columns(v, rest=0.0):
        return filled(grouped(v, rest), 2 * P).reshape(2, P).T

    packed = {
        "cols": [group_columns(i["L0_xattn_bq"]), group_columns(i["L0_xattn_bq"], -1.0),
                 group_columns(i["L1_xattn_bq"]), group_columns(np.tile(i["L1_xattn_bk"], H), -1.0),
                 group_columns(i["L2_xattn_bq"]), group_columns(i["L2_xattn_bk"], -1.0), column(i["L0_ffn_b1"]),
                 column(i["L2_ffn_bias1"]), column(i["L3_xattn_gru_bi"]), column(i["L3_xattn_gru_bh"]),
                 column(i["L3_xattn_slot_norm_w"]), column(i["L3_xattn_input_norm_w"])],
        "rows": [v[None, :] for v in (
            np.concatenate([i["g_xattn"], i["g_ffn"]]), i["L0_xattn_bq"], np.tile(i["L1_xattn_bv"], H),
            i["L2_xattn_bv"], i["L0_xattn_bo"], i["L0_ffn_b2"], i["L1_xattn_bo"], i["L2_xattn_bo"],
            i["L2_ffn_router_b"])],
        "attn0": [grouped(i["L0_xattn_Wq"].T), i["L0_xattn_Wq"].T, i["L0_xattn_Wo"].T],
        "ffn0": [i["L0_ffn_w1"], _side_by_side(i["L0_ffn_w2"])],
        "attn1": [grouped(heads(i["L1_xattn_Wk"])), heads(i["L1_xattn_Wv"]), grouped(i["L1_xattn_Wq"]), i["L1_xattn_Wo"]],
        "ffn1": [i["L1_ffn_gate_w"].T, i["L1_ffn_shared_gate_w"].T,
                 i["L1_ffn_w_gate_up"][:, :, :F1].transpose(1, 0, 2).reshape(D, E1 * F1),
                 i["L1_ffn_w_gate_up"][:, :, F1:].transpose(1, 0, 2).reshape(D, E1 * F1),
                 _side_by_side(i["L1_ffn_w_down"].reshape(E1 * F1, D)),
                 i["L1_ffn_shared_w_gate"].T, i["L1_ffn_shared_w_up"].T, _side_by_side(i["L1_ffn_shared_w_down"].T)],
        "attn2": [grouped(i["L2_xattn_wk"].T), i["L2_xattn_wv"].T, grouped(i["L2_xattn_wq"].T), i["L2_xattn_wo"].T],
        "ffn2": [i["L2_ffn_router_w"].T, i["L2_ffn_weights1"].transpose(1, 0, 2).reshape(D, E2 * F2),
                 _side_by_side(i["L2_ffn_weights2"].reshape(E2 * F2, D)), _side_by_side(i["L2_ffn_bias2"])],
        "attn3": [i["L3_xattn_Wk"].T, i["L3_xattn_Wv"].T, i["L3_xattn_Wq"], i["L3_xattn_gru_wi"].T,
                  i["L3_xattn_gru_wh"].T, i["L3_ffn_rhs"].T],
    }
    ctx_ = i["ctx_1024"]
    out = {"x": i["x"], "mask": i["mask_Bx1xSxS2_if1"], "ctx_rows": ctx_,
           "ctx_t": ctx_.transpose(2, 0, 1).reshape(D, B * CTX), **_constants()}
    out.update({k: np.concatenate(v, 1) for k, v in packed.items()})
    return {k: np.ascontiguousarray(v) for k, v in out.items()}


def kernel(**inputs):
    import concourse.bacc as bacc
    from concourse.bass_utils import run_bass_kernel_spmd

    nc = bacc.Bacc("TRN2", target_bir_lowering=False, num_devices=1)
    arrays = {f"in_{k}": v for k, v in _layout({k: np.asarray(v) for k, v in inputs.items()}).items()}
    a = {k[3:]: nc.dram_tensor(k, v.shape, mybir.dt.from_np(v.dtype), kind="ExternalInput").ap()
         for k, v in arrays.items()}
    out = nc.dram_tensor("out", (B, S, D), F32, kind="ExternalOutput").ap()
    program(nc, a, out)
    return run_bass_kernel_spmd(nc, [arrays], core_ids=[0]).results[0]["out"]
```
